# Optimizing a Trainium2 kernel written in Bass

```python
import numpy as np
import jax
import jax.numpy as jnp

def _softmax(x, axis=-1):
    return jax.nn.softmax(x, axis=axis)

def _gelu(x):
    return jax.nn.gelu(x, approximate=True)

def _silu(x):
    return jax.nn.silu(x)

def _sigmoid(x):
    return jax.nn.sigmoid(x)

def _layernorm(x, axis=-1, eps=1e-05):
    m = jnp.mean(x, axis=axis, keepdims=True)
    v = jnp.var(x, axis=axis, keepdims=True)
    return (x - m) / jnp.sqrt(v + eps)

def _scatter_add(tgt, idx, src, axis=0):
    return tgt.at[idx].add(src)

def _segment_sum(src, seg, n):
    return jax.ops.segment_sum(src, seg, n)
kernel_name = 'mk_hybrid_d1_jaxref_r8_6cbede'

def setup_inputs(seed: int=0):
    np.random.seed(seed)
    _w = jnp.asarray

    def _L0_attn_a_setup():
        import jax, jax.numpy as jnp
        import numpy as np
        C = 64
        key = jax.random.key(seed)
        k1, k2, k3, k4, k5 = jax.random.split(key, 5)
        B, T, D, H = (4, 512, 128, 8)
        out = jax.random.normal(k1, (B, T, D), jnp.float32)
        W_write = jax.random.normal(k2, (D, D), jnp.float32) * 0.02
        W_read = jax.random.normal(k3, (D, D), jnp.float32) * 0.02
        W_beta = jax.random.normal(k4, (H, D), jnp.float32) * 0.02
        decay = 4.6 + jax.random.normal(k5, (H,), jnp.float32) * 0.1
        return {'out': out, 'W_write': W_write, 'W_read': W_read, 'W_beta': W_beta, 'decay': decay}
    _L0_attn_a_in = _L0_attn_a_setup()

    def _L0_attn_b_setup():
        import jax, jax.numpy as jnp
        import numpy as np
        TWO_PI = 6.283185307179586
        key = jax.random.key(seed)
        k1, k2, k3, k4, k5, k6 = jax.random.split(key, 6)
        B, T, D = (2, 1024, 128)
        x = jax.random.normal(k1, (B, T, D), dtype=jnp.float32)
        s = 1.0 / np.sqrt(D)
        Wk = jax.random.uniform(k2, (D, D), jnp.float32, -s, s)
        Wv = jax.random.uniform(k3, (D, D), jnp.float32, -s, s)
        Wo = jax.random.uniform(k4, (D, D), jnp.float32, -s, s)
        freqs = jax.random.uniform(k5, (D,), jnp.float32, 0.0, TWO_PI)
        return {'x': x, 'Wk': Wk, 'Wv': Wv, 'Wo': Wo, 'freqs': freqs}
    _L0_attn_b_in = _L0_attn_b_setup()

    def _L0_ffn_setup():
        import jax, jax.numpy as jnp
        import numpy as np
        ALPHA = 1.702
        LIMIT = 9.0
        TOP_K = 2

        def swiglu(x):
            g, v = (x[..., 0::2], x[..., 1::2])
            g = jnp.clip(g, None, LIMIT)
            v = jnp.clip(v, -LIMIT, LIMIT)
            return g * jax.nn.sigmoid(ALPHA * g) * (v + 1)
        key = jax.random.key(seed)
        ks = jax.random.split(key, 6)
        B, L, D = (2, 256, 128)
        E, F = (8, 256)
        s_gate = 1.0 / np.sqrt(D)
        s1 = 1.0 / np.sqrt(D)
        s2 = 1.0 / np.sqrt(F)
        return {'x': jax.random.normal(ks[0], (B, L, D), dtype=jnp.float32), 'gate_w': jax.random.normal(ks[1], (D, E), dtype=jnp.float32) * s_gate, 'dense_1_w': jax.random.normal(ks[2], (E, 2 * F, D), dtype=jnp.float32) * s1, 'dense_1_b': jnp.zeros((E, 2 * F), dtype=jnp.float32), 'dense_2_w': jax.random.normal(ks[3], (E, D, F), dtype=jnp.float32) * s2, 'dense_2_b': jnp.zeros((E, D), dtype=jnp.float32)}
    _L0_ffn_in = _L0_ffn_setup()
    _d = {'L0_attn_a_out': _L0_attn_a_in['out'], 'L0_attn_a_W_write': _L0_attn_a_in['W_write'], 'L0_attn_a_W_read': _L0_attn_a_in['W_read'], 'L0_attn_a_W_beta': _L0_attn_a_in['W_beta'], 'L0_attn_a_decay': _L0_attn_a_in['decay'], 'L0_attn_b_Wk': _L0_attn_b_in['Wk'], 'L0_attn_b_Wv': _L0_attn_b_in['Wv'], 'L0_attn_b_Wo': _L0_attn_b_in['Wo'], 'L0_attn_b_freqs': _L0_attn_b_in['freqs'], 'L0_ffn_gate_w': _L0_ffn_in['gate_w'], 'L0_ffn_dense_1_w': _L0_ffn_in['dense_1_w'], 'L0_ffn_dense_1_b': _L0_ffn_in['dense_1_b'], 'L0_ffn_dense_2_w': _L0_ffn_in['dense_2_w'], 'L0_ffn_dense_2_b': _L0_ffn_in['dense_2_b']}
    _x0 = _d['L0_attn_a_out']
    _d['L0_attn_a_out'] = jax.random.normal(jax.random.fold_in(jax.random.key(seed), 1), (2, 2048, 128), dtype=_x0.dtype)
    del _x0
    return _d

def reference(L0_attn_a_out, L0_attn_a_W_write, L0_attn_a_W_read, L0_attn_a_W_beta, L0_attn_a_decay, L0_attn_b_Wk, L0_attn_b_Wv, L0_attn_b_Wo, L0_attn_b_freqs, L0_ffn_gate_w, L0_ffn_dense_1_w, L0_ffn_dense_1_b, L0_ffn_dense_2_w, L0_ffn_dense_2_b):

    def _L0_attn_a_ref(out, W_write, W_read, W_beta, decay):
        import jax, jax.numpy as jnp
        import numpy as np
        C = 64
        B, T, D = out.shape
        H = decay.shape[0]
        d = D // H
        assert T % C == 0
        N = T // C
        x = out.astype(jnp.float32)
        xh = x.reshape(B, T, H, d)
        rk = xh / jnp.maximum(jnp.linalg.norm(xh, axis=-1, keepdims=True), 1e-12)
        rk = rk.transpose(0, 2, 1, 3)
        wk = jnp.pad(rk[:, :, :-1], ((0, 0), (0, 0), (1, 0), (0, 0)))
        v = (x @ W_write.T).reshape(B, T, H, d).transpose(0, 2, 1, 3)
        beta = jax.nn.sigmoid(x @ W_beta.T).transpose(0, 2, 1)[..., None]
        v = v * beta
        wk_beta = wk * beta
        log_gamma = jnp.log(jax.nn.sigmoid(decay))
        pos = jnp.arange(C, dtype=jnp.float32)
        cum_decay = (pos + 1.0) * log_gamma[:, None]
        tril = jnp.tril(jnp.ones((C, C), jnp.float32))
        L_mask = jnp.exp((cum_decay[:, :, None] - cum_decay[:, None, :]) * tril) * tril
        decay_exp = jnp.exp(cum_decay)[:, :, None]
        chunk_total = jnp.exp(cum_decay[:, -1])[:, None, None]
        dw = jnp.exp(cum_decay[:, -1:] - cum_decay)[:, :, None]
        rk_c = rk.reshape(B, H, N, C, d)
        wk_c = wk.reshape(B, H, N, C, d)
        v_c = v.reshape(B, H, N, C, d)
        wkb_c = wk_beta.reshape(B, H, N, C, d)
        strict_lower = jnp.tril(jnp.ones((C, C), bool), -1)
        A = -(wkb_c @ jnp.swapaxes(wk_c, -1, -2)) * L_mask[None, :, None]
        A = jnp.where(strict_lower, A, 0.0)

        def ut_body(i, A):
            row = A[..., i, :]
            new_row = row + jnp.einsum('bhnj,bhnjk->bhnk', row, A)
            return A.at[..., i, :].set(new_row)
        A = jax.lax.fori_loop(1, C, ut_body, A)
        A = A + jnp.eye(C, dtype=A.dtype)
        v_c = A @ v_c
        wk_cum = A @ (wkb_c * decay_exp[None, :, None])
        causal = jnp.tril(jnp.ones((C, C), bool))
        xs = (jnp.moveaxis(rk_c, 2, 0), jnp.moveaxis(wk_c, 2, 0), jnp.moveaxis(v_c, 2, 0), jnp.moveaxis(wk_cum, 2, 0))
        S0 = jnp.zeros((B, H, d, d), jnp.float32)

        def chunk_step(S, xs_i):
            rk_i, wk_i, v_i, wkc_i = xs_i
            attn = rk_i @ jnp.swapaxes(wk_i, -1, -2) * L_mask[None]
            attn = jnp.where(causal, attn, 0.0)
            v_new = v_i - wkc_i @ S
            o_i = rk_i * decay_exp[None] @ S + attn @ v_new
            S_new = chunk_total[None] * S + jnp.swapaxes(wk_i * dw[None], -1, -2) @ v_new
            return (S_new, o_i)
        _, o = jax.lax.scan(chunk_step, S0, xs)
        o = jnp.moveaxis(o, 0, 2).reshape(B, H, T, d).transpose(0, 2, 1, 3).reshape(B, T, D)
        return out + (o @ W_read.T).astype(out.dtype)

    def _L0_attn_b_ref(x, Wk, Wv, Wo, freqs):
        import jax, jax.numpy as jnp
        import numpy as np
        TWO_PI = 6.283185307179586
        B, T, C = x.shape
        k_real = x @ Wk.T
        v_real = x @ Wv.T
        v = v_real.astype(jnp.complex64)
        t = jnp.arange(T, dtype=jnp.float32)
        rotors = jnp.exp(1j * (t[:, None] * freqs[None, :])).astype(jnp.complex64)
        memory_trace = jnp.cumsum(v * rotors[None, :, :], axis=1)
        retrieved = jnp.real(memory_trace * jnp.conj(rotors)[None, :, :])
        return retrieved @ Wo.T

    def _L0_ffn_ref(x, gate_w, dense_1_w, dense_1_b, dense_2_w, dense_2_b):
        import jax, jax.numpy as jnp
        import numpy as np
        ALPHA = 1.702
        LIMIT = 9.0
        TOP_K = 2

        def swiglu(x):
            g, v = (x[..., 0::2], x[..., 1::2])
            g = jnp.clip(g, None, LIMIT)
            v = jnp.clip(v, -LIMIT, LIMIT)
            return g * jax.nn.sigmoid(ALPHA * g) * (v + 1)
        B, L, D = x.shape
        xf = x.reshape(B * L, D)
        gate = xf @ gate_w
        weights, sel = jax.lax.top_k(gate, k=TOP_K)
        weights = jax.nn.softmax(weights, axis=-1)
        h = jnp.einsum('ecd,td->tec', dense_1_w, xf) + dense_1_b[None]
        h = swiglu(h)
        y = jnp.einsum('edf,tef->ted', dense_2_w, h) + dense_2_b[None]
        y_sel = jnp.take_along_axis(y, sel[:, :, None], axis=1)
        out = jnp.einsum('tkd,tk->td', y_sel, weights)
        return out.reshape(B, L, D)
    x = L0_attn_a_out
    x = x + _L0_attn_a_ref(_layernorm(x, axis=-1), L0_attn_a_W_write, L0_attn_a_W_read, L0_attn_a_W_beta, L0_attn_a_decay)
    x = x + _L0_ffn_ref(_layernorm(x, axis=-1), L0_ffn_gate_w, L0_ffn_dense_1_w, L0_ffn_dense_1_b, L0_ffn_dense_2_w, L0_ffn_dense_2_b)
    x = x + _L0_attn_b_ref(_layernorm(x, axis=-1), L0_attn_b_Wk, L0_attn_b_Wv, L0_attn_b_Wo, L0_attn_b_freqs)
    x = x + _L0_ffn_ref(_layernorm(x, axis=-1), L0_ffn_gate_w, L0_ffn_dense_1_w, L0_ffn_dense_1_b, L0_ffn_dense_2_w, L0_ffn_dense_2_b)
    return x

_drawn_inputs = setup_inputs


def setup_inputs(seed=0):
    import zlib

    import numpy as np

    out = dict(_drawn_inputs(seed))
    spreads = {'L0_ffn_dense_1_b': (0.0, 0.1), 'L0_ffn_dense_2_b': (0.0, 0.1)}
    factors = {'L0_attn_a_W_beta': 6.925, 'L0_attn_a_decay': 8.0}
    for name, (base, spread) in spreads.items():
        noise = np.random.default_rng([zlib.crc32(name.encode()), seed]).standard_normal(out[name].shape)
        drawn = base * np.exp(spread * noise) if base else spread * noise
        out[name] = jnp.asarray(drawn.astype(out[name].dtype))
    for name, factor in factors.items():
        out[name] = (out[name] * factor).astype(out[name].dtype)
    return out
```

```python
import math
from contextlib import ExitStack

import concourse.bass as bass
from concourse import mybir

F32 = mybir.dt.float32
I32 = mybir.dt.int32
U32 = mybir.dt.uint32
ALU = mybir.AluOpType
ACT = mybir.ActivationFunctionType
AX = mybir.AxisListType.X

P = 128
B, T, D = 2, 2048, 128
H, DH = 8, 16
C = 16
NC = T // C
NT = T // P
CPT = P // C
TILES = B * NT
E, F, TOPK = 8, 256, 2
FC = F // P
GT = 4
GROUPS = TILES // GT
GW = GT * P
EPS = 1e-5
LIMIT, ALPHA = 9.0, 1.702
TWO_PI = 2 * math.pi
PI_A = 6.28125
PI_B = float(int((TWO_PI - PI_A) * 2 ** 20)) / 2 ** 20
PI_C = TWO_PI - PI_A - PI_B
PI_LOW = 3.1415925
MAGIC = 1.5 * 2 ** 23


def build(nc, x, w_write, w_read, w_beta, decay, w_k, w_v, w_o, freqs, gate_w, w1, b1, w2, b2, out):
    SMALL = 16640
    WT = SMALL + 8192
    XRES = WT + 26688
    L2 = XRES + 16384
    WORK = L2 + 98304
    END = nc.sbuf_usable_end

    cursor = {"small": SMALL, "wt": WT, "xres": XRES, "l2": L2, "ffn": L2, "nat": L2, "chunk": WORK, "expand": WORK}
    limit = {"small": WT, "wt": XRES, "xres": L2, "l2": WORK, "ffn": WORK, "nat": WORK, "chunk": END, "expand": END}

    def sb(area, name, shape, dt=F32):
        size = 4
        for n in shape[1:]:
            size *= n
        offset = cursor[area]
        cursor[area] += (size + 31) // 32 * 32
        assert cursor[area] <= limit[area], (area, name)
        return nc.alloc_sbuf_tensor_at(name, shape, dt, offset=offset)

    ctx = ExitStack()
    with ctx:
        sems = {}

        def sem(name):
            if name not in sems:
                sems[name] = ctx.enter_context(nc.semaphore(name))
            return sems[name]

        bank = [ctx.enter_context(nc.psum_tensor(f"bank{i}", [P, 512], F32)) for i in range(8)]

        ident = sb("small", "ident", [P, P])
        head_mask = sb("small", "head_mask", [P, H, DH])
        rep = sb("small", "rep", [P, DH])
        gamma_rep = sb("small", "gamma_rep", [P, DH])
        decay_rows = sb("small", "decay_rows", [P, H])
        soft = sb("small", "soft", [P, H])
        steps = sb("small", "steps", [P, 2 * C + 1], I32)
        steps_f = sb("small", "steps_f", [P, 2 * C + 1])
        power = sb("small", "power", [P, 2 * C + 1, H])
        neg_power = sb("small", "neg_power", [P, C + 1, H])
        soft_col = sb("small", "soft_col", [P, H])
        gamma_col = sb("small", "gamma_col", [P, 1])
        wait_holder = sb("small", "wait_holder", [P, 1])
        freq_col = sb("small", "freq_col", [P, 1])
        iota8_i = sb("small", "iota8_i", [P, E], I32)
        iota8 = sb("small", "iota8", [P, E])
        half = sb("small", "half", [P, GT])
        b1_col = sb("small", "b1_col", [P, E, FC, 2])
        b1v_col = sb("small", "b1v_col", [P, E, FC])
        b2_rows = sb("small", "b2_rows", [E, D])
        gate_sb = sb("small", "gate_sb", [D, E])
        stat = sb("small", "stat", [P, TILES, 6])
        mean = sb("small", "mean", [P, TILES])
        dev = sb("small", "dev", [P, TILES])
        sumsq = sb("small", "sumsq", [P, TILES])
        var = sb("small", "var", [P, TILES])
        rstd = sb("small", "rstd", [P, TILES])

        w1t = sb("wt", "w1t", [D, E * FC * 2, P])
        w2t = sb("wt", "w2t", [P, E * FC, D])
        wsmall = sb("wt", "wsmall", [D, 4, D])
        w_write_t, w_read_t, w_v_t, w_o_t = (wsmall[:, i, :] for i in range(4))
        w_beta_t = sb("wt", "w_beta_t", [D, H])

        xres = sb("xres", "xres", [P, TILES, D])

        vk = sb("l2", "vk", [P, B, NC, 2, DH])
        pk = sb("l2", "pk", [P, B, NC, 2, DH])
        tt = sb("l2", "tt", [P, B, NC, C])
        rq = sb("l2", "rq", [P, B, NC, C])

        cursor["nat"] += 65536
        w1n = sb("nat", "w1n", [P, E * FC * 2, D])
        w2n = sb("nat", "w2n", [D, E * FC, P])
        wn = sb("nat", "wn", [D, 4, D])
        wbn = sb("nat", "wbn", [H, D])

        xc = [sb("chunk", f"xc{b}", [NC, C + 1, D]) for b in range(B)]
        sq = sb("chunk", "sq", [NC, C + 1, D])
        tri = sb("chunk", "tri", [NC, C, H, C])
        att = sb("chunk", "att", [NC, C, H, C])
        ca = sb("chunk", "ca", [NC, C, P])
        cb = sb("chunk", "cb", [NC, C, P])
        diag = sb("chunk", "diag", [NC, 2, C, H])
        diag_n = sb("chunk", "diag_n", [NC, C, H])
        beta = sb("chunk", "beta", [NC, C, H])
        bgam = sb("chunk", "bgam", [NC, C, H])
        s17 = sb("chunk", "s17", [NC, C + 1])
        r17 = sb("chunk", "r17", [NC, C + 1])
        s136 = sb("chunk", "s136", [NC, C + 1, H])
        r136 = sb("chunk", "r136", [NC, C + 1, H])

        kinds = ("t", "w", "u", "k", "m", "s")
        ex = [{k: sb("expand", f"ex_{k}{b}", [P, CPT, H, DH]) for k in kinds} for b in range(B)]
        uw = [sb("expand", f"uw{b}", [P, CPT, 2, DH]) for b in range(B)]
        qt = [sb("expand", f"qt{b}", [P, CPT, C]) for b in range(B)]
        mt = [sb("expand", f"mt{b}", [P, CPT, DH]) for b in range(B)]
        state = [sb("expand", f"state{b}", [P, CPT + 1, DH]) for b in range(B)]
        ot = [sb("expand", f"ot{b}", [P, P]) for b in range(B)]

        hrow = sb("ffn", "hrow", [P, GT, D])
        ht = sb("ffn", "ht", [D, GW])
        gates = sb("ffn", "gates", [P, GT, E])
        top = sb("ffn", "top", [P, GT, 8])
        topi = sb("ffn", "topi", [P, GT, 8], U32)
        topf = sb("ffn", "topf", [P, GT, 8])
        gap = sb("ffn", "gap", [P, 2, GT])
        wsel = sb("ffn", "wsel", [P, 2, GT])
        hot = sb("ffn", "hot", [P, 2, GT, E])
        wrow = sb("ffn", "wrow", [P, GT, E])
        wtr = sb("ffn", "wtr", [E, GW])
        gact = [sb("ffn", f"gact{i}", [P, GW]) for i in range(2)]
        vact = [sb("ffn", f"vact{i}", [P, GW]) for i in range(2)]
        sact = [sb("ffn", f"sact{i}", [P, GW]) for i in range(2)]
        gs = [sb("ffn", f"gs{i}", [P, GW]) for i in range(2)]
        hmid = [[sb("ffn", f"hmid{i}{c}", [P, GW]) for c in range(FC)] for i in range(2)]
        cos_t = sb("ffn", "cos_t", [D, T])
        sin_t = sb("ffn", "sin_t", [D, T])
        ang = sb("ffn", "ang", [D, T])
        ang_i = sb("ffn", "ang_i", [D, T], I32)
        turn = sb("ffn", "turn", [D, T])
        ones_row = sb("ffn", "ones_row", [D, GW])
        vc = sb("ffn", "vc", [D, 2, GW])
        trace = sb("ffn", "trace", [D, 2, GW])
        carry = sb("ffn", "carry", [D, 2])
        back = sb("ffn", "back", [D, 2, GW])
        retr = sb("ffn", "retr", [D, GW])

        x_chunk = x.rearrange("b (n i) d -> b n i d", i=C)
        x_tile = x.rearrange("b (t p) d -> p (b t) d", p=P)
        out_tile = out.rearrange("b (t p) d -> p (b t) d", p=P)

        def diagonal(tensor, shift, rows):
            return bass.AP(tensor, shift * H * C, [[C * H * C, NC], [H * C + 1, rows], [C, H]])

        def over_heads(operand):
            return operand.unsqueeze(2).to_broadcast([P, CPT, H, DH])

        def over_width(scale, n):
            return scale.unsqueeze(3).to_broadcast([P, n, H, DH])

        mask = head_mask[:, :, :].unsqueeze(1).to_broadcast([P, CPT, H, DH])

        ORDER = ("v", "kb", "kd", "r", "p", "t")
        UNITS = 4 * len(ORDER)
        L2_BANK = (6, 7)

        def l2_source(kind, i):
            if kind in ("p", "t"):
                return {"p": att, "t": tri}[kind][:, i, :, :].rearrange("p h j -> p (h j)")
            return {"v": cb, "kb": ca, "kd": cb, "r": ca}[kind][:, i, :]

        def l2_dest(unit):
            b, kind, q = unit // UNITS, ORDER[unit % UNITS // 4], unit % 4
            dest = {"v": vk[:, b, :, 0, :], "kb": vk[:, b, :, 1, :], "p": pk[:, b, :, 0, :], "kd": pk[:, b, :, 1, :],
                    "t": tt[:, b, :, :], "r": rq[:, b, :, :]}[kind]
            return dest.rearrange("p n x -> p x n")[:, 4 * q:4 * q + 4, :]

        def l2_bank(unit):
            return bank[L2_BANK[unit % 2]][:, :].rearrange("p (x n) -> p x n", x=4)

        n_w1, n_w2 = E * FC * 2 // 4, E * FC // 4
        W_GROUPS = [(w1n, w1t, 4 * g) for g in range(n_w1)] + [(w2n, w2t, 4 * g) for g in range(n_w2)]
        W_BANK = (5, 4)

        UP = E * FC
        FFN_RUNS = ((0, GROUPS), (GROUPS, 2 * GROUPS))
        BT_K = GROUPS + 1

        def ffn_k(lo):
            return 1 if lo == 0 else GROUPS + 1

        block = ctx.enter_context(nc.Block())

        @block.sync
        def _(sp):
            for b in range(B):
                sp.dma_start(xc[b][:, 1:C + 1, :], x_chunk[b]).then_inc(sem("x_loaded"), 16)
                sp.dma_start(xc[b][1:NC, 0, :], x_chunk[b, 0:NC - 1, C - 1, :]).then_inc(sem("x_loaded"), 16)
            sp.dma_start(xres[:, :, :], x_tile).then_inc(sem("xres_loaded"), 16)
            sp.dma_start(b1_col[:, :, :, :].rearrange("p e c k -> p (e c) k"),
                         b1.rearrange("e (c p k) -> p (e c) k", c=FC, k=2)).then_inc(sem("small_loaded"), 16)
            sp.dma_start(b2_rows[:, :], b2).then_inc(sem("small_loaded"), 16)
            sp.dma_start(gate_sb[:, :], gate_w).then_inc(sem("small_loaded"), 16)
            sp.dma_start(freq_col[:, :], freqs.rearrange("(d a) -> d a", a=1)).then_inc(sem("small_loaded"), 16)
            with sp.Fori(0, GROUPS) as g:
                sp.wait_ge(sem("added"), g * E + (GROUPS + 1) * E + 1)
                sp.dma_start(out_tile[:, bass.ds(g * GT, GT), :],
                             xres[:, bass.ds(g * GT, GT), :]).then_inc(sem("stored"), 16)
            sp.wait_ge(sem("stored"), 16 * GROUPS)

        @block.gpsimd
        def _(pool):
            for name in ("gs",):
                pool.sem_inc(sem(name), 1)
            pool.memset(ident[:, :], 0.0).then_inc(sem("ident_zero"), 1)
            pool.memset(head_mask[:, :, :], 1.0).then_inc(sem("mask_one"), 1)
            for b in range(B):
                pool.memset(xc[b][0:1, 0, :], 0.0).then_inc(sem("pad_zero"), 1)
            pool.wait_ge(sem("ident_zero"), 1)
            pool.affine_select(out=ident[:, :], in_=ident[:, :], compare_op=ALU.not_equal, fill=1.0,
                               base=0, pattern=[[-1, P]], channel_multiplier=1).then_inc(sem("ident"), 1)
            pool.wait_ge(sem("mask_one"), 1)
            pool.affine_select(out=head_mask[:, :, :], in_=head_mask[:, :, :], compare_op=ALU.is_ge, fill=0.0,
                               base=0, pattern=[[-DH, H], [0, DH]], channel_multiplier=1).then_inc(sem("mask_low"), 1)
            pool.wait_ge(sem("mask_low"), 1)
            pool.affine_select(out=head_mask[:, :, :], in_=head_mask[:, :, :], compare_op=ALU.is_ge, fill=0.0,
                               base=DH - 1, pattern=[[DH, H], [0, DH]], channel_multiplier=-1).then_inc(sem("head_mask"), 1)
            pool.iota(steps[:, 0:C + 1], pattern=[[1, C + 1]], base=0, channel_multiplier=0).then_inc(sem("iotas"), 1)
            pool.iota(steps[:, C + 1:2 * C + 1], pattern=[[-1, C]], base=C - 1, channel_multiplier=0).then_inc(sem("iotas"), 1)
            pool.iota(iota8_i[:, :], pattern=[[1, E]], base=0, channel_multiplier=0).then_inc(sem("iotas"), 1)
            pool.memset(half[:, :], -0.5).then_inc(sem("half"), 1)

            for b in range(B):
                if b:
                    pool.wait_ge(sem("l2_mm"), UNITS)
                pool.memset(att[:, :, :, :], 0.0).then_inc(sem("att_zero"), 1)
                pool.memset(tri[:, :, :, :], 0.0).then_inc(sem("tri_zero"), 1)
                pool.wait_ge(sem("att_zero"), b + 1)
                pool.wait_ge(sem("tri_zero"), b + 1)
                pool.memset(diagonal(tri, 0, C), 1.0).then_inc(sem("tri_one"), 1)
                pool.wait_ge(sem("neg_power"), 1)
                pool.wait_ge(sem("beta"), b + 1)
                for delta in range(1, C + 1):
                    rows = C + 1 - delta
                    g = diag[:, delta % 2, :, :]
                    pool.wait_ge(sem("diag"), C * b + delta)
                    if delta < C:
                        low = rows - 1
                        if delta > 1:
                            pool.wait_ge(sem("tri_diag"), (C - 1) * b + delta - 1)
                        pool.tensor_tensor(diag_n[:, 0:low, :], g[:, 0:low, :],
                                           neg_power[:, delta:delta + 1, :].to_broadcast([NC, low, H]),
                                           ALU.mult).then_inc(sem("diag_n"), 1)
                        pool.wait_ge(sem("diag_n"), (C - 1) * b + delta)
                        pool.tensor_tensor(diagonal(tri, delta, low), diag_n[:, 0:low, :], beta[:, delta:C, :],
                                           ALU.mult).then_inc(sem("tri_diag"), 1)
                    pool.tensor_tensor(diagonal(att, delta - 1, rows), g[:, 0:rows, :],
                                       power[:, delta - 1:delta, :].to_broadcast([NC, rows, H]),
                                       ALU.mult).then_inc(sem("diag_used"), 1)

            wide = [P, TILES, D]
            pool.wait_ge(sem("res_scale"), 1)
            pool.tensor_tensor(xres[:, :, :], xres[:, :, :], rstd[:, :].unsqueeze(2).to_broadcast(wide),
                               ALU.mult).then_inc(sem("res_scaled"), 1)
            pool.wait_ge(sem("res_scaled"), 1)
            pool.tensor_tensor(xres[:, :, :], xres[:, :, :], mean[:, :].unsqueeze(2).to_broadcast(wide),
                               ALU.add).then_inc(sem("res_ready"), 1)

            pool.wait_ge(sem("l2_even"), B * UNITS // 2)
            pool.wait_ge(sem("l2_odd"), B * UNITS // 2)
            with pool.Fori(0, NT) as t:
                for b in range(B):
                    chunks = bass.ds(t * CPT, CPT)
                    pool.wait_ge(sem(f"uw_mm{b}"), t + 1)
                    pool.tensor_tensor(ex[b]["t"][:, :, :, :], over_heads(tt[:, b, chunks, :]), mask,
                                       ALU.mult).then_inc(sem(f"ex_t{b}"), 1)
                    pool.wait_ge(sem(f"y_mm{b}"), t + 1)
                    pool.tensor_tensor(ex[b]["k"][:, :, :, :], over_heads(pk[:, b, chunks, 1, :]), mask,
                                       ALU.mult).then_inc(sem(f"ex_k{b}"), 1)
                for b in range(B):
                    pool.wait_ge(sem(f"mt{b}"), t + 2)
                    pool.tensor_tensor(ex[b]["m"][:, :, :, :], over_heads(mt[b][:, :, :]), mask,
                                       ALU.mult).then_inc(sem(f"ex_m{b}"), 1)

            for b in range(B):
                pool.wait_ge(sem(f"x1_{b}"), NT + 1)
            pool.iota(ang_i[:, :], pattern=[[1, T]], base=0, channel_multiplier=0).then_inc(sem("positions"), 1)

            def inverse_deviation(k):
                pool.wait_ge(sem("ln_var"), k + 1)
                pool.tensor_tensor(rstd[:, 0:GT], var[:, 0:GT], half[:, :], ALU.pow).then_inc(sem("ln_rstd"), 1)

            def ffn(lo, hi):
                with pool.Fori(lo, hi) as g:
                    inverse_deviation(g + ffn_k(lo))
                    for n in range(UP):
                        i = n % 2
                        pool.wait_ge(sem("s"), g * UP + n + 1)
                        if n < 2:
                            pool.wait_ge(sem("h"), g * UP + 1)
                        else:
                            pool.wait_ge(sem("h"), g * UP + n)
                        pool.tensor_tensor(gs[i][:, :], gact[i][:, :], sact[i][:, :], ALU.mult).then_inc(sem("gs"), 1)

            ffn(*FFN_RUNS[0])
            for b in range(B):
                with pool.Fori(b * GROUPS // B, (b + 1) * GROUPS // B) as g:
                    inverse_deviation(g + BT_K)
                    for k, table in enumerate((cos_t, sin_t)):
                        pool.wait_ge(sem(f"trace{k}"), g + 1)
                        pool.wait_ge(sem("retr"), g + 1)
                        pool.tensor_tensor(back[:, k, :], trace[:, k, :], table[:, bass.ds(g * GW - b * T, GW)],
                                           ALU.mult).then_inc(sem(f"back{k}"), 1)
            ffn(*FFN_RUNS[1])

        @block.scalar
        def _(act):
            for name in ("v", "uw0", "uw1"):
                act.sem_inc(sem(name), 1)
            act.dma_start(decay_rows[:, :], decay.rearrange("(a h) -> a h", a=1).to_broadcast([P, H])).then_inc(sem("decay_loaded"), 16)
            for i, w in enumerate((w_write, w_read, w_v, w_o)):
                act.dma_start(wn[:, i, :], w).then_inc(sem("wn_loaded"), 16)
            act.dma_start(wbn[:, :], w_beta).then_inc(sem("wn_loaded"), 16)
            act.dma_start(w1n[:, :, :].rearrange("p (m k) d -> p m (k d)", k=2),
                          w1.rearrange("e (c p k) d -> p (e c) (k d)", c=FC, k=2)).then_inc(sem("w1_loaded"), 16)
            act.dma_start(w2n[:, :, :].rearrange("d (e c) p -> d e (c p)", c=FC),
                          w2.rearrange("e d f -> d e f")).then_inc(sem("w2_loaded"), 16)

            act.wait_ge(sem("decay_floor"), 1)
            act.activation(soft[:, :], soft[:, :], ACT.Exp, scale=-1.0).then_inc(sem("exp_decay"), 1)
            act.wait_ge(sem("exp_decay1"), 1)
            act.activation(soft[:, :], soft[:, :], ACT.Ln).then_inc(sem("log"), 1)
            act.wait_ge(sem("power_arg"), 1)
            act.activation(power[:, :, :], power[:, :, :], ACT.Exp, scale=-1.0).then_inc(sem("power"), 1)
            act.wait_ge(sem("soft_col"), 1)
            act.activation(gamma_col[:, :], soft_col[:, 0:1], ACT.Exp, scale=-float(C)).then_inc(sem("gamma_col"), 1)

            act.wait_ge(sem("wsmall_mm"), 1)
            act.activation(wsmall[:, :, :].rearrange("p i d -> p (i d)"), bank[5][:, :], ACT.Copy).then_inc(sem("w_evac"), 1)
            act.wait_ge(sem("wbeta_mm"), 1)
            act.activation(w_beta_t[:, :], bank[4][:, 0:H], ACT.Copy).then_inc(sem("wbeta"), 1)

            for b in range(B):
                act.wait_ge(sem("centred"), b + 1)
                act.activation(sq[:, :, :], xc[b][:, :, :], ACT.Square).then_inc(sem("sq"), 1)
                act.wait_ge(sem("chunk_var"), b + 1)
                act.activation(s17[:, :], s17[:, :], ACT.Sqrt).then_inc(sem("chunk_std"), 1)
                act.wait_ge(sem("normed"), b + 1)
                act.activation(sq[:, :, :], xc[b][:, :, :], ACT.Square).then_inc(sem("sq"), 1)
                act.wait_ge(sem("head_sq"), b + 1)
                act.activation(s136[:, :, :], s136[:, :, :], ACT.Sqrt).then_inc(sem("head_norm"), 1)
                for q in range(4):
                    act.wait_ge(sem("hx_mm"), 4 * b + q + 1)
                    act.activation(ca[:, 4 * q:4 * q + 4, :].rearrange("p i n -> p (i n)"), bank[q][:, :],
                                   ACT.Copy).then_inc(sem("hx"), 1)
                act.wait_ge(sem("beta_mm"), b + 1)
                act.activation(beta[:, :, :].rearrange("p i h -> p (i h)"), bank[4][:, 0:C * H],
                               ACT.Sigmoid).then_inc(sem("beta"), 1)
                if b == 0:
                    for g, (_, dest, at) in enumerate(W_GROUPS):
                        act.wait_ge(sem("w_mm"), g + 1)
                        act.activation(dest[:, at:at + 4, :].rearrange("p m d -> p (m d)"), bank[W_BANK[g % 2]][:, :],
                                       ACT.Copy).then_inc(sem("w_evac"), 1)
                for unit in range(UNITS * b, UNITS * (b + 1), 2):
                    act.wait_ge(sem("l2_mm"), unit + 1)
                    act.activation(l2_dest(unit), l2_bank(unit), ACT.Copy).then_inc(sem("l2_even"), 1)

                if b == 0:
                    act.wait_ge(sem("ln_var"), 1)
                    act.activation(rstd[:, :], var[:, :], ACT.Sqrt).then_inc(sem("ln_rstd"), 1)

            with act.Fori(0, NT) as t:
                for b in range(B):
                    act.wait_ge(sem(f"uw_mm{b}"), t + 2)
                    act.activation(uw[b][:, :, :, :].rearrange("p n k d -> p (n k d)"), bank[4 * b][:, 0:CPT * 2 * DH],
                                   ACT.Copy).then_inc(sem(f"uw{b}"), 1)
                for b in range(B):
                    act.wait_ge(sem(f"o_mm{b}"), t + 1)
                    act.activation(ot[b][:, :], bank[4 * b + 3][:, 0:P], ACT.Copy).then_inc(sem(f"ot{b}"), 1)

            def ffn(lo, hi):
                with act.Fori(lo, hi) as g:
                    act.wait_ge(sem("ht_mm"), g + ffn_k(lo))
                    act.activation(ht[:, :], bank[0][:, :], ACT.Copy).then_inc(sem("ht"), 1)
                    act.wait_ge(sem("gap"), g + 1)
                    act.activation(wsel[:, :, :], gap[:, :, :], ACT.Sigmoid).then_inc(sem("wsel"), 1)
                    act.wait_ge(sem("wt_mm"), g + 1)
                    act.activation(wtr[:, :], bank[1][0:E, :], ACT.Copy).then_inc(sem("wtr"), 1)
                    for n in range(UP):
                        e, c, i = n // FC, n % FC, n % 2
                        act.wait_ge(sem("up"), g * UP + n + 1)
                        if n < 2:
                            act.wait_ge(sem("h"), g * UP + 1)
                        else:
                            act.wait_ge(sem("h"), g * UP + n)
                        act.activation(vact[i][:, :], bank[4 + i][:, :], ACT.Identity,
                                       bias=b1v_col[:, e, c:c + 1]).then_inc(sem("v"), 1)
                        act.wait_ge(sem("g"), g * UP + n + 2)
                        act.activation(sact[i][:, :], gact[i][:, :], ACT.Sigmoid, scale=ALPHA).then_inc(sem("s"), 1)

            ffn(*FFN_RUNS[0])
            act.wait_ge(sem("angles"), 1)
            act.activation(sin_t[:, :], sin_t[:, :], ACT.Sin).then_inc(sem("trig"), 1)
            act.activation(cos_t[:, :], cos_t[:, :], ACT.Sin).then_inc(sem("trig"), 1)
            with act.Fori(0, GROUPS) as g:
                act.wait_ge(sem("ht_mm"), g + BT_K)
                act.activation(ht[:, :], bank[0][:, :], ACT.Copy).then_inc(sem("ht"), 1)
            ffn(*FFN_RUNS[1])

        @block.tensor
        def _(pe):
            for name in ("down", "bt_y_mm", "uw_mm0", "uw_mm1", "y_mm0", "y_mm1"):
                pe.sem_inc(sem(name), 1)
            pe.wait_ge(sem("ident"), 1)
            pe.wait_ge(sem("wn_loaded"), 5 * 16)
            for i in range(4):
                mm = pe.transpose(bank[5][:, i * P:(i + 1) * P], wn[:, i, :], ident[:, :])
            mm.then_inc(sem("wsmall_mm"), 1)
            pe.transpose(bank[4][:, 0:H], wbn[:, :], ident[0:H, 0:H]).then_inc(sem("wbeta_mm"), 1)
            pe.wait_ge(sem("w_evac"), 1)
            pe.wait_ge(sem("wbeta"), 1)

            for b in range(B):
                pe.wait_ge(sem("normed"), b + 1)
                for q in range(4):
                    if b:
                        pe.wait_ge(sem("v_src"), 4 * b)
                    for i in range(4 * q, 4 * q + 4):
                        mm = pe.transpose(bank[q][:, i % 4 * P:(i % 4 + 1) * P], xc[b][:, i + 1, :], ident[:, :])
                    mm.then_inc(sem("hx_mm"), 1)
                for q in range(4):
                    pe.wait_ge(sem("hx"), 4 * b + q + 1)
                    for i in range(4 * q, 4 * q + 4):
                        mm = pe.matmul(bank[q][:, i % 4 * P:(i % 4 + 1) * P], ca[:, i, :], w_write_t, start=True, stop=True)
                    mm.then_inc(sem("v_mm"), 1)
                for i in range(C):
                    mm = pe.matmul(bank[4][:, i * H:(i + 1) * H], ca[:, i, :], w_beta_t[:, :], start=True, stop=True)
                mm.then_inc(sem("beta_mm"), 1)
                if b == 0:
                    pe.wait_ge(sem("w1_loaded"), 16)
                    pe.wait_ge(sem("w2_loaded"), 16)
                    for g, (src, _, at) in enumerate(W_GROUPS):
                        if g == 1:
                            pe.wait_ge(sem("beta"), 1)
                        if g >= 2:
                            pe.wait_ge(sem("w_evac"), g)
                        for m in range(4):
                            mm = pe.transpose(bank[W_BANK[g % 2]][:, m * P:(m + 1) * P], src[:, at + m, :], ident[:, :])
                        mm.then_inc(sem("w_mm"), 1)
                for unit in range(UNITS * b, UNITS * (b + 1)):
                    kind, q = ORDER[unit % UNITS // 4], unit % 4
                    if kind == "v":
                        pe.wait_ge(sem("v_src"), 4 * (b + 1))
                    elif kind == "p":
                        pe.wait_ge(sem("diag_used"), C * (b + 1))
                    elif kind == "t":
                        pe.wait_ge(sem("row_added"), (C - 2) * (b + 1))
                    else:
                        pe.wait_ge(sem(f"{kind}_src"), b + 1)
                    if unit >= 2:
                        pe.wait_ge(sem("l2_odd" if unit % 2 else "l2_even"), unit // 2)
                    for i in range(4 * q, 4 * q + 4):
                        mm = pe.transpose(bank[L2_BANK[unit % 2]][:, i % 4 * P:(i % 4 + 1) * P], l2_source(kind, i), ident[:, :])
                    mm.then_inc(sem("l2_mm"), 1)

            pe.wait_ge(sem("l2_even"), B * UNITS // 2)
            pe.wait_ge(sem("l2_odd"), B * UNITS // 2)
            pe.wait_ge(sem("state_zero"), B)
            with pe.Fori(0, NT) as t:
                def operand(tensor, b, n):
                    return tensor[:, b, bass.ds(t * CPT + n, 1), :, :].rearrange("p a k d -> p (a k d)")

                def tokens(b, n):
                    return pk[:, b, bass.ds(t * CPT + n, 1), 0, :].rearrange("p a d -> p (a d)")

                for b in range(B):
                    pe.wait_ge(sem(f"ex_t{b}"), t + 1)
                    pe.wait_ge(sem(f"uw{b}"), t + 1)
                    for n in range(CPT):
                        mm = pe.matmul(bank[4 * b][:, n * 32:n * 32 + 32], ex[b]["t"][:, n, :, :].rearrange("p h d -> p (h d)"),
                                       operand(vk, b, n), start=True, stop=True)
                    mm.then_inc(sem(f"uw_mm{b}"), 1)
                for b in range(B):
                    pe.wait_ge(sem(f"ex_w{b}"), t + 1)
                    pe.wait_ge(sem(f"mt{b}"), t + 1)
                    for n in range(CPT):
                        mm = pe.matmul(bank[4 * b + 1][:, n * 32:n * 32 + 32], ex[b]["w"][:, n, :, :].rearrange("p h d -> p (h d)"),
                                       operand(pk, b, n), start=True, stop=True)
                    mm.then_inc(sem(f"qm_mm{b}"), 1)
                for n in range(CPT):
                    for b in range(B):
                        if n == 0:
                            pe.wait_ge(sem(f"ex_k{b}"), t + 1)
                        pe.wait_ge(sem(f"state{b}"), t * (CPT + 1) + n + 1)
                        pe.matmul(bank[4 * b + 2][:, n * DH:(n + 1) * DH], ex[b]["k"][:, n, :, :].rearrange("p h d -> p (h d)"),
                                  uw[b][:, n, 0, :], start=True, stop=False)
                        if n == 0:
                            pe.wait_ge(sem(f"ex_m{b}"), t + 1)
                        pe.matmul(bank[4 * b + 2][:, n * DH:(n + 1) * DH], ex[b]["m"][:, n, :, :].rearrange("p h d -> p (h d)"),
                                  state[b][:, n, :], start=False, stop=True).then_inc(sem(f"state_mm{b}"), 1)
                for b in range(B):
                    pe.wait_ge(sem(f"ex_s{b}"), t + 1)
                    pe.wait_ge(sem(f"x1_{b}"), t + 1)
                    for n in range(CPT):
                        dest = bank[4 * b + 3][:, n * C:(n + 1) * C]
                        pe.matmul(dest, ex[b]["u"][:, n, :, :].rearrange("p h d -> p (h d)"), tokens(b, n), start=True, stop=False)
                        mm = pe.matmul(dest, ex[b]["s"][:, n, :, :].rearrange("p h d -> p (h d)"), qt[b][:, n, :], start=False, stop=True)
                    mm.then_inc(sem(f"o_mm{b}"), 1)
                for b in range(B):
                    pe.wait_ge(sem(f"ot{b}"), t + 1)
                    pe.matmul(bank[4 * b + 3][:, P:2 * P], ot[b][:, :], w_read_t, start=True, stop=True).then_inc(sem(f"y_mm{b}"), 1)

            def rows_to_columns(k):
                pe.wait_ge(sem("ln_rows"), k)
                for q in range(GT):
                    mm = pe.transpose(bank[0][:, q * P:(q + 1) * P], hrow[:, q, :], ident[:, :])
                mm.then_inc(sem("ht_mm"), 1)
                pe.wait_ge(sem("ht"), k)

            def ffn(lo, hi):
                with pe.Fori(lo, hi) as g:
                    pe.wait_ge(sem("bias_added"), g + 1)
                    rows_to_columns(g + ffn_k(lo))
                    for q in range(GT):
                        mm = pe.matmul(bank[1][:, q * E:(q + 1) * E], ht[:, q * P:(q + 1) * P], gate_sb[:, :], start=True, stop=True)
                    mm.then_inc(sem("gate_mm"), 1)

                    def up(n):
                        if n < 2:
                            pe.wait_ge(sem("g"), g * UP + 1)
                            pe.wait_ge(sem("v"), g * UP + 1)
                        else:
                            pe.wait_ge(sem("g"), g * UP + n)
                            pe.wait_ge(sem("v"), g * UP + n)
                        pe.matmul(bank[2 + n % 2][:, :], w1t[:, 2 * n, :], ht[:, :], start=True, stop=True)
                        pe.matmul(bank[4 + n % 2][:, :], w1t[:, 2 * n + 1, :], ht[:, :], start=True, stop=True).then_inc(sem("up"), 1)

                    def down(e):
                        pe.wait_ge(sem("h"), g * UP + FC * (e + 1) + 1)
                        if e < 2:
                            pe.wait_ge(sem("added"), g * E + 1)
                        else:
                            pe.wait_ge(sem("added"), g * E + e)
                        for q in range(GT):
                            for c in range(FC):
                                mm = pe.matmul(bank[6 + e % 2][:, q * D:(q + 1) * D], hmid[e % 2][c][:, q * P:(q + 1) * P],
                                               w2t[:, FC * e + c, :], start=(c == 0), stop=(c == FC - 1))
                        mm.then_inc(sem("down"), 1)

                    for n in range(2):
                        up(n)
                    pe.wait_ge(sem("wrow"), g + 1)
                    for q in range(GT):
                        mm = pe.transpose(bank[1][0:E, q * P:(q + 1) * P], wrow[:, q, :], ident[:, :])
                    mm.then_inc(sem("wt_mm"), 1)
                    pe.wait_ge(sem("wtr"), g + 1)
                    for q in range(GT):
                        mm = pe.matmul(bank[0][:, q * D:(q + 1) * D], wtr[:, q * P:(q + 1) * P], b2_rows[:, :], start=True, stop=True)
                    mm.then_inc(sem("bias_mm"), 1)
                    for e in range(E):
                        if e + 1 < E:
                            for c in range(FC):
                                up(FC * (e + 1) + c)
                        down(e)

            pe.wait_ge(sem("small_loaded"), 4 * 16)
            ffn(*FFN_RUNS[0])
            with pe.Fori(0, GROUPS) as g:
                rows_to_columns(g + BT_K)
                pe.wait_ge(sem("rotated"), 2 * g + 1)
                pe.matmul(bank[1][:, :], w_v_t, ht[:, :], start=True, stop=True).then_inc(sem("bt_v_mm"), 1)
                pe.wait_ge(sem("retr"), g + 2)
                pe.wait_ge(sem("x3"), g + 1)
                for q in range(GT):
                    mm = pe.matmul(bank[2][:, q * D:(q + 1) * D], retr[:, q * P:(q + 1) * P], w_o_t, start=True, stop=True)
                mm.then_inc(sem("bt_y_mm"), 1)
            ffn(*FFN_RUNS[1])

        @block.vector
        def _(dve):
            for name in ("h", "g", "added", "rotated", "retr", "x3", "carried", "bias_added", "mt0", "mt1", "state0", "state1", "x1_0", "x1_1"):
                dve.sem_inc(sem(name), 1)
            linked = [0]

            def link(ins):
                linked[0] += 1
                ins.then_inc(sem("vector_link"), 1)
                dve.wait_ge(sem("vector_link"), linked[0])

            dve.wait_ge(sem("decay_loaded"), 16)
            dve.tensor_scalar(soft[:, :], decay_rows[:, :], -40.0, None, ALU.max).then_inc(sem("decay_floor"), 1)
            dve.wait_ge(sem("exp_decay"), 1)
            dve.tensor_scalar(soft[:, :], soft[:, :], 1.0, None, ALU.add).then_inc(sem("exp_decay1"), 1)
            dve.wait_ge(sem("log"), 1)
            dve.scalar_tensor_tensor(out=soft[:, :], in0=decay_rows[:, :], scalar=-1.0, in1=soft[:, :],
                                     op0=ALU.mult, op1=ALU.max).then_inc(sem("soft"), 1)
            dve.wait_ge(sem("iotas"), 3)
            link(dve.tensor_copy(steps_f[:, :], steps[:, :]))
            dve.tensor_copy(iota8[:, :], iota8_i[:, :])
            dve.wait_ge(sem("soft"), 1)
            shape = [P, 2 * C + 1, H]
            dve.tensor_tensor(power[:, :, :], steps_f[:, :].unsqueeze(2).to_broadcast(shape),
                              soft[:, :].unsqueeze(1).to_broadcast(shape), ALU.mult).then_inc(sem("power_arg"), 1)
            dve.wait_ge(sem("head_mask"), 1)
            link(dve.tensor_tensor(neg_power[:, 0, :], soft[:, :], head_mask[:, :, 0], ALU.mult))
            dve.tensor_reduce(soft_col[:, 0:1], neg_power[:, 0, :], AX, ALU.add).then_inc(sem("soft_col"), 1)
            dve.wait_ge(sem("ident"), 1)
            link(dve.tensor_reduce(rep[:, :], ident[:, :].rearrange("p (h d) -> p d h", h=H), AX, ALU.add))
            dve.wait_ge(sem("power"), 1)
            dve.wait_ge(sem("soft_col"), 1)
            dve.tensor_scalar(neg_power[:, :, :], power[:, 0:C + 1, :], -1.0, None, ALU.mult).then_inc(sem("neg_power"), 1)
            dve.wait_ge(sem("gamma_col"), 1)
            link(dve.tensor_scalar(gamma_rep[:, :], rep[:, :], gamma_col[:, :], None, ALU.mult))
            dve.wait_ge(sem("small_loaded"), 4 * 16)
            link(dve.tensor_scalar(b1v_col[:, :, :], b1_col[:, :, :, 1], 1.0, None, ALU.add))

            def variance(rows, k):
                even_m, odd_m = stat[:, 0:rows, 1], stat[:, 0:rows, 4]
                dve.wait_ge(sem("ln_stat"), k + 1)
                dve.tensor_tensor(mean[:, 0:rows], even_m, odd_m, ALU.add)
                dve.tensor_tensor(sumsq[:, 0:rows], stat[:, 0:rows, 2], stat[:, 0:rows, 5], ALU.add)
                dve.tensor_tensor(dev[:, 0:rows], even_m, odd_m, ALU.subtract).then_inc(sem("ln_dev"), 1)
                dve.wait_ge(sem("ln_dev"), k + 1)
                dve.tensor_scalar(mean[:, 0:rows], mean[:, 0:rows], 0.5, None, ALU.mult)
                dve.tensor_tensor(dev[:, 0:rows], dev[:, 0:rows], dev[:, 0:rows], ALU.mult).then_inc(sem("ln_dev_sq"), 1)
                dve.wait_ge(sem("ln_dev_sq"), k + 1)
                dve.scalar_tensor_tensor(out=sumsq[:, 0:rows], in0=dev[:, 0:rows], scalar=D / 4.0, in1=sumsq[:, 0:rows],
                                         op0=ALU.mult, op1=ALU.add).then_inc(sem("ln_sumsq"), 1)
                dve.wait_ge(sem("ln_sumsq"), k + 1)
                dve.tensor_scalar(var[:, 0:rows], sumsq[:, 0:rows], 1.0 / D, EPS, ALU.mult, ALU.add).then_inc(sem("ln_var"), 1)

            def l2_evac(*units):
                for unit in units:
                    dve.wait_ge(sem("l2_mm"), unit + 1)
                    dve.tensor_copy(l2_dest(unit), l2_bank(unit)).then_inc(sem("l2_odd"), 1)

            dve.wait_ge(sem("pad_zero"), B)
            for b in range(B):
                dve.wait_ge(sem("x_loaded"), 4 * 16)
                link(dve.tensor_reduce(s17[:, :], xc[b][:, :, :], AX, ALU.add))
                link(dve.tensor_scalar(r17[:, :], s17[:, :], -1.0 / D, None, ALU.mult))
                dve.tensor_tensor(xc[b][:, :, :], xc[b][:, :, :], r17[:, :].unsqueeze(2).to_broadcast([NC, C + 1, D]),
                                  ALU.add).then_inc(sem("centred"), 1)
                dve.wait_ge(sem("sq"), 2 * b + 1)
                link(dve.tensor_reduce(s17[:, :], sq[:, :, :], AX, ALU.add))
                dve.tensor_scalar(s17[:, :], s17[:, :], 1.0 / D, EPS, ALU.mult, ALU.add).then_inc(sem("chunk_var"), 1)
                dve.wait_ge(sem("chunk_std"), b + 1)
                link(dve.reciprocal(r17[:, :], s17[:, :]))
                dve.tensor_tensor(xc[b][:, :, :], xc[b][:, :, :], r17[:, :].unsqueeze(2).to_broadcast([NC, C + 1, D]),
                                  ALU.mult).then_inc(sem("normed"), 1)
                dve.wait_ge(sem("sq"), 2 * b + 2)
                link(dve.tensor_reduce(s136[:, :, :], sq[:, :, :].rearrange("p i (h d) -> p i h d", h=H), AX, ALU.add))
                dve.tensor_scalar(s136[:, :, :], s136[:, :, :], 1e-24, None, ALU.max).then_inc(sem("head_sq"), 1)
                dve.wait_ge(sem("head_norm"), b + 1)
                link(dve.reciprocal(r136[:, :, :], s136[:, :, :]))
                dve.wait_ge(sem("hx_mm"), 4 * (b + 1))
                keys = xc[b][:, :, :].rearrange("p i (h d) -> p i h d", h=H)
                link(dve.tensor_tensor(keys, keys, over_width(r136[:, :, :], C + 1), ALU.mult))
                dve.wait_ge(sem("beta"), b + 1)
                link(dve.tensor_tensor(bgam[:, :, :], beta[:, :, :], power[:, 1:C + 1, :], ALU.mult))
                turned = [s[:, :, :].rearrange("p d (h i) -> p i h d", h=H) for s in (ca, cb)]
                for q in range(4):
                    dve.wait_ge(sem("v_mm"), 4 * b + q + 1)
                    dve.tensor_tensor(turned[1][:, 4 * q:4 * q + 4, :, :], bank[q][:, :].rearrange("p (i h d) -> p i h d", i=4, h=H),
                                      over_width(beta[:, 4 * q:4 * q + 4, :], 4), ALU.mult).then_inc(sem("v_src"), 1)
                dve.wait_ge(sem("beta_mm"), b + 1)
                dve.tensor_tensor(turned[0], keys[:, 0:C, :, :], over_width(bgam[:, :, :], C), ALU.mult).then_inc(sem("kb_src"), 1)
                first = UNITS * b
                l2_evac(first + 1, first + 3)
                dve.wait_ge(sem("l2_mm"), first + 4)
                dve.tensor_tensor(turned[1], keys[:, 0:C, :, :], over_width(power[:, C + 1:2 * C + 1, :], C), ALU.mult).then_inc(sem("kd_src"), 1)
                l2_evac(first + 5, first + 7)
                dve.wait_ge(sem("l2_mm"), first + 8)
                dve.tensor_tensor(ca[:, :, :].rearrange("p i (h d) -> p i h d", h=H), keys[:, 1:C + 1, :, :],
                                  over_width(power[:, 1:C + 1, :], C), ALU.mult).then_inc(sem("r_src"), 1)
                l2_evac(first + 9, first + 11)
                for delta in range(1, C + 1):
                    rows = C + 1 - delta
                    if delta > 1:
                        dve.wait_ge(sem("diag"), C * b + delta - 1)
                    link(dve.tensor_tensor(sq[:, 0:rows, :], xc[b][:, delta:C + 1, :], xc[b][:, 0:rows, :], ALU.mult))
                    if C * b + delta > 2:
                        dve.wait_ge(sem("diag_used"), C * b + delta - 2)
                    dve.tensor_reduce(diag[:, delta % 2, 0:rows, :], sq[:, 0:rows, :].rearrange("p i (h d) -> p i h d", h=H),
                                      AX, ALU.add).then_inc(sem("diag"), 1)
                l2_evac(first + 13, first + 15)
                dve.wait_ge(sem("tri_diag"), (C - 1) * (b + 1))
                dve.wait_ge(sem("tri_one"), b + 1)
                steps_done = (C - 2) * b
                for k in range(1, C - 1):
                    shape = [NC, C - 1 - k, H, k]
                    a_col = tri[:, k + 1:C, :, k:k + 1].to_broadcast(shape)
                    t_row = tri[:, k:k + 1, :, 0:k].to_broadcast(shape)
                    size = (C - 1 - k) * H * k
                    step = sq[:, :, :].rearrange("p i d -> p (i d)")[:, 0:size].rearrange("p (i h j) -> p i h j", h=H, j=k)
                    if k > 1:
                        dve.wait_ge(sem("row_added"), steps_done + k - 1)
                    link(dve.tensor_tensor(step, a_col, t_row, ALU.mult))
                    last = dve.tensor_tensor(tri[:, k + 1:C, :, 0:k], tri[:, k + 1:C, :, 0:k], step, ALU.add)
                    last.then_inc(sem("row_added"), 1)
                l2_evac(first + 17, first + 19, first + 21, first + 23)

                if b == 0:
                    dve.wait_ge(sem("xres_loaded"), 16)
                    for t in range(TILES):
                        ins = dve.bn_stats(stat[:, t, :], xres[:, t, :])
                    ins.then_inc(sem("ln_stat"), 1)
                    variance(TILES, 0)
                    dve.wait_ge(sem("ln_rstd"), 1)
                    link(dve.reciprocal(var[:, :], rstd[:, :]))
                    dve.scalar_tensor_tensor(out=mean[:, :], in0=mean[:, :], scalar=-1.0, in1=var[:, :],
                                             op0=ALU.mult, op1=ALU.mult)
                    dve.tensor_scalar(rstd[:, :], var[:, :], 1.0, None, ALU.add).then_inc(sem("res_scale"), 1)

            dve.wait_ge(sem("l2_even"), B * UNITS // 2)
            dve.wait_ge(sem("l2_odd"), B * UNITS // 2)
            for b in range(B):
                dve.memset(state[b][:, 0, :], 0.0).then_inc(sem("state_zero"), 1)
            dve.wait_ge(sem("state_zero"), B)
            dve.wait_ge(sem("res_ready"), 1)
            with dve.Fori(0, NT) as t:
                for b in range(B):
                    dve.wait_ge(sem(f"uw{b}"), t + 2)
                    dve.tensor_tensor(ex[b]["w"][:, :, :, :], over_heads(uw[b][:, :, 1, :]), mask, ALU.mult).then_inc(sem(f"ex_w{b}"), 1)
                    dve.tensor_tensor(ex[b]["u"][:, :, :, :], over_heads(uw[b][:, :, 0, :]), mask, ALU.mult)
                for b in range(B):
                    dve.wait_ge(sem(f"qm_mm{b}"), t + 1)
                    qm = bank[4 * b + 1][:, 0:CPT * 2 * DH].rearrange("p (n k d) -> p n k d", n=CPT, k=2)
                    dve.tensor_tensor(qt[b][:, :, :], rq[:, b, bass.ds(t * CPT, CPT), :], qm[:, :, 0, :], ALU.subtract)
                    dve.tensor_tensor(mt[b][:, :, :], gamma_rep[:, :].unsqueeze(1).to_broadcast([P, CPT, DH]), qm[:, :, 1, :],
                                      ALU.subtract).then_inc(sem(f"mt{b}"), 1)
                for n in range(CPT):
                    for b in range(B):
                        dve.wait_ge(sem(f"state_mm{b}"), t * CPT + n + 1)
                        dve.tensor_copy(state[b][:, n + 1, :], bank[4 * b + 2][:, n * DH:(n + 1) * DH]).then_inc(sem(f"state{b}"), 1)
                for b in range(B):
                    dve.wait_ge(sem(f"state{b}"), t * (CPT + 1) + CPT + 1)
                    dve.tensor_tensor(ex[b]["s"][:, :, :, :], over_heads(state[b][:, 0:CPT, :]), mask, ALU.mult).then_inc(sem(f"ex_s{b}"), 1)
                for b in range(B):
                    dve.wait_ge(sem(f"ex_s{b}"), t + 1)
                    dve.tensor_copy(state[b][:, 0, :], state[b][:, CPT, :]).then_inc(sem(f"state{b}"), 1)
                for b in range(B):
                    dve.wait_ge(sem(f"y_mm{b}"), t + 2)
                    here = xres[:, bass.ds(t + b * NT, 1), :].rearrange("p a d -> p (a d)")
                    dve.tensor_tensor(here, here, bank[4 * b + 3][:, P:2 * P], ALU.add).then_inc(sem(f"x1_{b}"), 1)
            for b in range(B):
                dve.wait_ge(sem(f"x1_{b}"), NT + 1)

            def layernorm(k, first_tile):
                for q in range(GT):
                    ins = dve.bn_stats(stat[:, q, :], xres[:, bass.ds(first_tile + q, 1), :].rearrange("p a d -> p (a d)"))
                ins.then_inc(sem("ln_stat"), 1)
                variance(GT, k)
                dve.wait_ge(sem("ln_rstd"), k + 1)
                for q in range(GT):
                    ins = dve.tensor_scalar(hrow[:, q, :], xres[:, bass.ds(first_tile + q, 1), :].rearrange("p a d -> p (a d)"),
                                            mean[:, q:q + 1], rstd[:, q:q + 1], ALU.subtract, ALU.mult)
                ins.then_inc(sem("ln_rows"), 1)

            def ffn(lo, hi):
                with dve.Fori(lo, hi) as g:
                    tile = (g - lo) * GT
                    layernorm(g + ffn_k(lo), tile)
                    dve.wait_ge(sem("gate_mm"), g + 1)
                    dve.tensor_copy(gates[:, :, :].rearrange("p q e -> p (q e)"), bank[1][:, 0:GT * E]).then_inc(sem("gates"), 1)
                    dve.wait_ge(sem("gates"), g + 1)
                    dve.memset(wait_holder[:, :], 0.0)
                    for q in range(GT):
                        ins = dve.max(top[:, q, :], gates[:, q, :])
                    ins.then_inc(sem("top"), 1)
                    dve.wait_ge(sem("top"), g + 1)
                    for k in range(TOPK):
                        ins = dve.tensor_tensor(gap[:, k, :], top[:, :, k], top[:, :, 1 - k], ALU.subtract)
                    ins.then_inc(sem("gap"), 1)
                    for q in range(GT):
                        ins = dve.max_index(topi[:, q, :], top[:, q, :], gates[:, q, :])
                    ins.then_inc(sem("topi"), 1)
                    dve.wait_ge(sem("topi"), g + 1)
                    dve.tensor_copy(topf[:, :, :], topi[:, :, :]).then_inc(sem("topf"), 1)
                    dve.wait_ge(sem("topf"), g + 1)
                    shape = [P, GT, E]
                    for k in range(TOPK):
                        ins = dve.tensor_tensor(hot[:, k, :, :], iota8[:, :].unsqueeze(1).to_broadcast(shape),
                                                topf[:, :, k:k + 1].to_broadcast(shape), ALU.is_equal)
                    ins.then_inc(sem("hot"), 1)
                    dve.wait_ge(sem("wsel"), g + 1)
                    dve.wait_ge(sem("hot"), g + 1)
                    for k in range(TOPK):
                        ins = dve.tensor_tensor(hot[:, k, :, :], hot[:, k, :, :], wsel[:, k, :].unsqueeze(2).to_broadcast(shape), ALU.mult)
                    ins.then_inc(sem("hot_w"), 1)
                    dve.wait_ge(sem("hot_w"), g + 1)
                    dve.tensor_tensor(wrow[:, :, :], hot[:, 0, :, :], hot[:, 1, :, :], ALU.add).then_inc(sem("wrow"), 1)

                    def gate_side(n):
                        e, c, i = n // FC, n % FC, n % 2
                        dve.wait_ge(sem("up"), g * UP + n + 1)
                        if n < 2:
                            dve.wait_ge(sem("gs"), g * UP + 1)
                        else:
                            dve.wait_ge(sem("gs"), g * UP + n)
                        dve.tensor_scalar(gact[i][:, :], bank[2 + i][:, :], b1_col[:, e, c, 0:1], LIMIT, ALU.add, ALU.min).then_inc(sem("g"), 1)

                    def hidden(n):
                        e, c, i = n // FC, n % FC, n % 2
                        dve.wait_ge(sem("v"), g * UP + n + 2)
                        dve.tensor_scalar(vact[i][:, :], vact[i][:, :], 1 + LIMIT, 1 - LIMIT, ALU.min, ALU.max).then_inc(sem("clip"), 1)
                        if c == 0:
                            if e < 2:
                                dve.wait_ge(sem("down"), g * E + 1)
                            else:
                                dve.wait_ge(sem("down"), g * E + e)
                        dve.wait_ge(sem("clip"), g * UP + n + 1)
                        dve.wait_ge(sem("gs"), g * UP + n + 2)
                        dve.tensor_tensor(hmid[e % 2][c][:, :], vact[i][:, :], gs[i][:, :], ALU.mult).then_inc(sem("h"), 1)

                    def add_expert(e):
                        dve.wait_ge(sem("down"), g * E + e + 2)
                        if e == 0:
                            dve.wait_ge(sem("bias_added"), g + 2)
                        else:
                            dve.wait_ge(sem("added"), g * E + e + 1)
                        for q in range(GT):
                            here = xres[:, bass.ds(tile + q, 1), :].rearrange("p a d -> p (a d)")
                            ins = dve.scalar_tensor_tensor(out=here, in0=bank[6 + e % 2][:, q * D:(q + 1) * D], scalar=wrow[:, q, e:e + 1],
                                                           in1=here, op0=ALU.mult, op1=ALU.add)
                        ins.then_inc(sem("added"), 1)

                    for n in range(UP + 1):
                        if n < UP:
                            gate_side(n)
                        if n == 1:
                            dve.wait_ge(sem("bias_mm"), g + 1)
                            here = xres[:, bass.ds(tile, GT), :].rearrange("p q d -> p (q d)")
                            dve.tensor_tensor(here, here, bank[0][:, :], ALU.add).then_inc(sem("bias_added"), 1)
                        if n:
                            hidden(n - 1)
                        if n >= 2 * FC and n % FC == 0:
                            add_expert(n // FC - 2)
                    add_expert(E - 1)

            dve.wait_ge(sem("half"), 1)
            ffn(*FFN_RUNS[0])

            dve.wait_ge(sem("positions"), 1)
            link(dve.tensor_copy(ang[:, :], ang_i[:, :]))
            link(dve.tensor_scalar(ang[:, :], ang[:, :], freq_col[:, :], None, ALU.mult))
            link(dve.tensor_scalar(turn[:, :], ang[:, :], 1 / TWO_PI, MAGIC, ALU.mult, ALU.add))
            link(dve.tensor_scalar(turn[:, :], turn[:, :], MAGIC, None, ALU.subtract))
            for k, part in enumerate((PI_A, PI_B, PI_C)):
                link(dve.scalar_tensor_tensor(out=ang[:, :], in0=turn[:, :], scalar=-part, in1=ang[:, :],
                                         op0=ALU.mult, op1=ALU.add))
            link(dve.tensor_scalar(sin_t[:, :], ang[:, :], PI_LOW, -PI_LOW, ALU.min, ALU.max))
            link(dve.scalar_tensor_tensor(out=cos_t[:, :], in0=sin_t[:, :], scalar=-1.0, in1=sin_t[:, :],
                                     op0=ALU.mult, op1=ALU.max))
            dve.tensor_scalar(cos_t[:, :], cos_t[:, :], -1.0, math.pi / 2, ALU.mult, ALU.add).then_inc(sem("angles"), 1)
            link(dve.memset(ones_row[:, :], 1.0))
            dve.wait_ge(sem("trig"), 2)
            for b in range(B):
                if b:
                    dve.wait_ge(sem("carried"), b * GROUPS // B + 1)
                link(dve.memset(carry[:, :], 0.0))
                with dve.Fori(b * GROUPS // B, (b + 1) * GROUPS // B) as g:
                    layernorm(g + BT_K, g * GT)
                    dve.wait_ge(sem("bt_v_mm"), g + 1)
                    for k, table in enumerate((cos_t, sin_t)):
                        dve.tensor_tensor(vc[:, k, :], bank[1][:, :], table[:, bass.ds(g * GW - b * T, GW)], ALU.mult).then_inc(sem("rotated"), 1)
                    dve.wait_ge(sem("rotated"), 2 * g + 2 + 1)
                    dve.wait_ge(sem("carried"), g + 1)
                    dve.wait_ge(sem("retr"), g + 1)
                    for k in range(2):
                        dve.tensor_tensor_scan(trace[:, k, :], ones_row[:, :], vc[:, k, :], carry[:, k:k + 1],
                                               ALU.mult, ALU.add).then_inc(sem(f"trace{k}"), 1)
                    dve.wait_ge(sem("trace1"), g + 1)
                    dve.tensor_copy(carry[:, :], trace[:, :, GW - 1]).then_inc(sem("carried"), 1)
                    dve.wait_ge(sem("back0"), g + 1)
                    dve.wait_ge(sem("back1"), g + 1)
                    dve.wait_ge(sem("bt_y_mm"), g + 1)
                    dve.tensor_tensor(retr[:, :], back[:, 0, :], back[:, 1, :], ALU.add).then_inc(sem("retr"), 1)
                    dve.wait_ge(sem("bt_y_mm"), g + 2)
                    here = xres[:, bass.ds(g * GT, GT), :].rearrange("p q d -> p (q d)")
                    dve.tensor_tensor(here, here, bank[2][:, :], ALU.add).then_inc(sem("x3"), 1)
            dve.wait_ge(sem("x3"), GROUPS + 1)
            ffn(*FFN_RUNS[1])


_INS = ["L0_attn_a_out", "L0_attn_a_W_write", "L0_attn_a_W_read", "L0_attn_a_W_beta", "L0_attn_a_decay",
        "L0_attn_b_Wk", "L0_attn_b_Wv", "L0_attn_b_Wo", "L0_attn_b_freqs", "L0_ffn_gate_w",
        "L0_ffn_dense_1_w", "L0_ffn_dense_1_b", "L0_ffn_dense_2_w", "L0_ffn_dense_2_b"]


def kernel(**inputs):
    import numpy as _np
    import concourse.bacc as _bacc
    from concourse import mybir as _mybir
    from concourse.bass_utils import run_bass_kernel_spmd as _run

    nc = _bacc.Bacc("TRN2", target_bir_lowering=False, num_devices=1)
    arrays, args = {}, []
    for name in _INS:
        a = _np.ascontiguousarray(inputs[name])
        arrays[f"in_{name}_dram"] = a
        args.append(nc.dram_tensor(f"in_{name}_dram", a.shape, _mybir.dt.from_np(a.dtype), kind="ExternalInput").ap())
    args.append(nc.dram_tensor("out_0_dram", (B, T, D), F32, kind="ExternalOutput").ap())
    build(nc, *args)
    r = _run(nc, [arrays], core_ids=[0])
    return r.results[0]["out_0_dram"]
```

```python
import math
from contextlib import ExitStack

import concourse.bass as bass
from concourse import mybir

F32 = mybir.dt.float32
F32R = mybir.dt.float32r
I32 = mybir.dt.int32
U32 = mybir.dt.uint32
ALU = mybir.AluOpType
ACT = mybir.ActivationFunctionType
AX = mybir.AxisListType.X

P = 128
B, T, D = 2, 2048, 128
H, DH = 8, 16
C = 16
NC = T // C
NT = T // P
CPT = P // C
TILES = B * NT
E, F, TOPK = 8, 256, 2
FC = F // P
GT = 4
GROUPS = TILES // GT
GW = GT * P
EPS = 1e-5
LIMIT, ALPHA = 9.0, 1.702
GATE_LIMIT = LIMIT / (1 + math.exp(-ALPHA * LIMIT))
TWO_PI = 2 * math.pi
PI_A = 6.28125
PI_B = float(int((TWO_PI - PI_A) * 2 ** 20)) / 2 ** 20
PI_C = TWO_PI - PI_A - PI_B
PI_LOW = 3.1415925
MAGIC = 1.5 * 2 ** 23


def build(nc, x, w_write, w_read, w_beta, decay, w_k, w_v, w_o, freqs, gate_w, w1, b1, w2, b2, out):
    SMALL = 16640
    WT = SMALL + 8192
    XRES = WT + 26688
    L2 = XRES + 16384
    WORK = L2 + 98304
    END = nc.sbuf_usable_end

    cursor = {"small": SMALL, "wt": WT, "xres": XRES, "l2": L2, "ffn": L2, "nat": L2, "chunk": WORK, "expand": WORK, "split": WORK + 25600}
    limit = {"small": WT, "wt": XRES, "xres": L2, "l2": WORK, "ffn": WORK, "nat": WORK, "chunk": END, "expand": WORK + 25600, "split": END}

    def sb(area, name, shape, dt=F32):
        size = 4
        for n in shape[1:]:
            size *= n
        offset = cursor[area]
        cursor[area] += (size + 31) // 32 * 32
        assert cursor[area] <= limit[area], (area, name)
        return nc.alloc_sbuf_tensor_at(name, shape, dt, offset=offset)

    ctx = ExitStack()
    with ctx:
        sems = {}

        def sem(name):
            if name not in sems:
                sems[name] = ctx.enter_context(nc.semaphore(name))
            return sems[name]

        bank = [ctx.enter_context(nc.psum_tensor(f"bank{i}", [P, 512], F32)) for i in range(8)]

        ident = sb("small", "ident", [P, P])
        head_mask = sb("small", "head_mask", [P, H, DH])
        pair_mask = sb("small", "pair_mask", [P, 2, DH])
        rep = sb("small", "rep", [P, DH])
        gamma_rep = sb("small", "gamma_rep", [P, DH])
        decay_rows = sb("small", "decay_rows", [P, H])
        soft = sb("small", "soft", [P, H])
        steps = sb("small", "steps", [P, 2 * C + 1], I32)
        steps_f = sb("small", "steps_f", [P, 2 * C + 1])
        power = sb("small", "power", [P, 2 * C + 1, H])
        neg_power = sb("small", "neg_power", [P, C + 1, H])
        soft_col = sb("small", "soft_col", [P, H])
        gamma_col = sb("small", "gamma_col", [P, 1])
        wait_holder = sb("small", "wait_holder", [P, 1])
        freq_col = sb("small", "freq_col", [P, 1])
        iota8_i = sb("small", "iota8_i", [P, E], I32)
        iota8 = sb("small", "iota8", [P, E])
        half = sb("small", "half", [P, GT])
        b1_col = sb("small", "b1_col", [P, E, FC, 2])
        b1v_col = sb("small", "b1v_col", [P, E, FC])
        b2_rows = sb("small", "b2_rows", [E, D])
        gate_sb = sb("small", "gate_sb", [D, E])
        stat = sb("small", "stat", [P, TILES, 6])
        mean = sb("small", "mean", [P, TILES])
        dev = sb("small", "dev", [P, TILES])
        sumsq = sb("small", "sumsq", [P, TILES])
        var = sb("small", "var", [P, TILES])
        rstd = sb("small", "rstd", [P, TILES])

        w1t = sb("wt", "w1t", [D, E * FC * 2, P])
        w2t = sb("wt", "w2t", [P, E * FC, D])
        wsmall = sb("wt", "wsmall", [D, 4, D])
        w_write_t, w_read_t, w_v_t, w_o_t = (wsmall[:, i, :] for i in range(4))
        w_beta_t = sb("wt", "w_beta_t", [D, H])

        xres = sb("xres", "xres", [P, TILES, D])

        vk = sb("l2", "vk", [P, B, NC, 2, DH])
        pk = sb("l2", "pk", [P, B, NC, 2, DH])
        tt = sb("l2", "tt", [P, B, NC, C])
        rq = sb("l2", "rq", [P, B, NC, C])

        cursor["nat"] += 65536
        w1n = sb("nat", "w1n", [P, E * FC * 2, D])
        w2n = sb("nat", "w2n", [D, E * FC, P])
        wn = sb("nat", "wn", [D, 4, D])
        wbn = sb("nat", "wbn", [H, D])

        xc = [sb("chunk", f"xc{b}", [NC, C + 1, D]) for b in range(B)]
        sq = sb("chunk", "sq", [NC, C + 1, D])
        tri = sb("chunk", "tri", [NC, C, H, C])
        att = sb("chunk", "att", [NC, C, H, C])
        ca = sb("chunk", "ca", [NC, C, P])
        cb = sb("chunk", "cb", [NC, C, P])
        diag = sb("chunk", "diag", [NC, 2, C, H])
        diag_n = sb("chunk", "diag_n", [NC, C, H])
        beta = sb("chunk", "beta", [NC, C, H])
        bgam = sb("chunk", "bgam", [NC, C, H])
        s17 = sb("chunk", "s17", [NC, C + 1])
        r17 = sb("chunk", "r17", [NC, C + 1])
        s136 = sb("chunk", "s136", [NC, C + 1, H])
        r136 = sb("chunk", "r136", [NC, C + 1, H])

        kinds = ("t", "w", "u", "k", "m", "s")
        ex = [{k: sb("expand", f"ex_{k}{b}", [P, CPT, 2, DH]) for k in kinds} for b in range(B)]
        uw = [sb("expand", f"uw{b}", [P, CPT, 2, DH]) for b in range(B)]
        qt = [sb("expand", f"qt{b}", [P, CPT, C]) for b in range(B)]
        mt = [sb("expand", f"mt{b}", [P, CPT, DH]) for b in range(B)]
        state = [sb("expand", f"state{b}", [P, CPT + 1, DH]) for b in range(B)]
        ot = [sb("expand", f"ot{b}", [P, P]) for b in range(B)]
        vk_tile = [sb("expand", f"vk_tile{b}", [P, CPT, 2, DH]) for b in range(B)]
        pk_tile = [sb("expand", f"pk_tile{b}", [P, CPT, 2, DH]) for b in range(B)]
        p_tile = [sb("expand", f"p_tile{b}", [P, CPT, 2, DH]) for b in range(B)]

        w1_hi = sb("split", "w1_hi", [D, E * FC * 2, P], F32R)
        w1_lo = sb("split", "w1_lo", [D, E * FC * 2, P], F32R)

        hrow = sb("ffn", "hrow", [P, GT, D])
        ht = [sb("ffn", f"ht{i}", [D, GW]) for i in range(2)]
        ht_hi = [sb("ffn", f"ht_hi{i}", [D, GW], F32R) for i in range(2)]
        ht_lo = [sb("ffn", f"ht_lo{i}", [D, GW], F32R) for i in range(2)]
        gates = sb("ffn", "gates", [P, GT, E])
        top = sb("ffn", "top", [P, GT, 8])
        topi = sb("ffn", "topi", [P, GT, 8], U32)
        topf = sb("ffn", "topf", [P, GT, 8])
        gap = sb("ffn", "gap", [P, 2, GT])
        wsel = sb("ffn", "wsel", [P, 2, GT])
        hot = sb("ffn", "hot", [P, 2, GT, E])
        wrow = [sb("ffn", f"wrow{i}", [P, GT, E]) for i in range(2)]
        wtr = sb("ffn", "wtr", [E, GW])
        vact = [sb("ffn", f"vact{i}", [P, GW]) for i in range(2)]
        gs = [sb("ffn", f"gs{i}", [P, GW]) for i in range(2)]
        hmid = [[sb("ffn", f"hmid{i}{c}", [P, GW]) for c in range(FC)] for i in range(2)]
        cos_t = sb("ffn", "cos_t", [D, T])
        sin_t = sb("ffn", "sin_t", [D, T])
        ang = sb("ffn", "ang", [D, T])
        ang_i = sb("ffn", "ang_i", [D, T], I32)
        turn = sb("ffn", "turn", [D, T])
        ones_row = sb("ffn", "ones_row", [D, GW])
        vc = sb("ffn", "vc", [D, 2, GW])
        trace = sb("ffn", "trace", [D, 2, GW])
        carry = sb("ffn", "carry", [D, 2])
        back = sb("ffn", "back", [D, 2, GW])
        retr = sb("ffn", "retr", [D, GW])

        x_chunk = x.rearrange("b (n i) d -> b n i d", i=C)
        x_tile = x.rearrange("b (t p) d -> p (b t) d", p=P)
        out_tile = out.rearrange("b (t p) d -> p (b t) d", p=P)

        def diagonal(tensor, shift, rows):
            return bass.AP(tensor, shift * H * C, [[C * H * C, NC], [H * C + 1, rows], [C, H]])

        def over_pair(operand):
            return operand.unsqueeze(2).to_broadcast([P, CPT, 2, DH])

        def over_width(scale, n):
            return scale.unsqueeze(3).to_broadcast([P, n, H, DH])

        mask = pair_mask[:, :, :].unsqueeze(1).to_broadcast([P, CPT, 2, DH])

        ORDER = ("v", "kb", "kd", "r", "p", "t")
        UNITS = 4 * len(ORDER)
        L2_BANK = (6, 7)

        def l2_source(kind, i):
            if kind in ("p", "t"):
                return {"p": att, "t": tri}[kind][:, i, :, :].rearrange("p h j -> p (h j)")
            return {"v": cb, "kb": ca, "kd": cb, "r": ca}[kind][:, i, :]

        def l2_dest(unit):
            b, kind, q = unit // UNITS, ORDER[unit % UNITS // 4], unit % 4
            dest = {"v": vk[:, b, :, 0, :], "kb": vk[:, b, :, 1, :], "p": pk[:, b, :, 0, :], "kd": pk[:, b, :, 1, :],
                    "t": tt[:, b, :, :], "r": rq[:, b, :, :]}[kind]
            return dest.rearrange("p n x -> p x n")[:, 4 * q:4 * q + 4, :]

        def l2_bank(unit):
            return bank[L2_BANK[unit % 2]][:, :].rearrange("p (x n) -> p x n", x=4)

        n_w1, n_w2 = E * FC * 2 // 4, E * FC // 4
        W_GROUPS = [(w1n, w1t, 4 * g) for g in range(n_w1)] + [(w2n, w2t, 4 * g) for g in range(n_w2)]
        W_BANK = (5, 4)

        def unit_after(t, b, ahead):
            return t + (b + ahead) // B, (b + ahead) % B

        def exists(t):
            return not isinstance(t, int) or 0 <= t < NT

        def run_slots(engine, slot):
            for t in (-2, -1, 0):
                for b in range(B):
                    slot(t, b)
            with engine.Fori(1, NT - 2) as t:
                for b in range(B):
                    slot(t, b)
            for t in (NT - 2, NT - 1, NT):
                for b in range(B):
                    slot(t, b)

        def unrolled_slots(slot):
            for t in range(-2, NT + 1):
                for b in range(B):
                    slot(t, b)

        UP = E * FC
        BT_K = GROUPS + 1

        def ffn_groups(engine, lo, first, group):
            first(lo)
            with engine.Fori(lo // 2, (lo + GROUPS) // 2 - 1) as pair:
                for i in range(2):
                    group(pair * 2 + i, i, False)
            for i in range(2):
                group(lo + GROUPS - 2 + i, i, i == 1)

        def ffn_k(lo):
            return 1 if lo == 0 else GROUPS + 1

        block = ctx.enter_context(nc.Block())

        @block.sync
        def _(sp):
            for b in range(B):
                sp.dma_start(xc[b][:, 1:C + 1, :], x_chunk[b]).then_inc(sem("x_loaded"), 16)
                sp.dma_start(xc[b][1:NC, 0, :], x_chunk[b, 0:NC - 1, C - 1, :]).then_inc(sem("x_loaded"), 16)
            sp.dma_start(xres[:, :, :], x_tile).then_inc(sem("xres_loaded"), 16)
            sp.dma_start(b1_col[:, :, :, :].rearrange("p e c k -> p (e c) k"),
                         b1.rearrange("e (c p k) -> p (e c) k", c=FC, k=2)).then_inc(sem("small_loaded"), 16)
            sp.dma_start(b2_rows[:, :], b2).then_inc(sem("small_loaded"), 16)
            sp.dma_start(gate_sb[:, :], gate_w).then_inc(sem("small_loaded"), 16)
            sp.dma_start(freq_col[:, :], freqs.rearrange("(d a) -> d a", a=1)).then_inc(sem("small_loaded"), 16)
            sp.wait_ge(sem("l2_even"), B * UNITS // 2)
            sp.wait_ge(sem("l2_odd"), B * UNITS // 2)

            def slot(t, b):
                (t3, b3), t2 = unit_after(t, b, 3), unit_after(t, b, 2)[0]
                if exists(t3):
                    sp.wait_ge(sem(f"uw_mm{b3}"), t3 + 1)
                    sp.dma_start(vk_tile[b3][:, :, :, :], vk[:, b3, bass.ds(t3 * CPT, CPT), :, :]).then_inc(sem(f"vk_tile{b3}"), 16)
                if exists(t2):
                    sp.wait_ge(sem(f"qm_mm{b}"), t2 + 1)
                    sp.dma_start(pk_tile[b][:, :, :, :], pk[:, b, bass.ds(t2 * CPT, CPT), :, :]).then_inc(sem(f"pk_tile{b}"), 16)
                if exists(t):
                    sp.wait_ge(sem(f"o_mm{b}"), t + 1)
                    sp.dma_start(p_tile[b][:, :, :, :], pk[:, b, bass.ds(t * CPT, CPT), :, :]).then_inc(sem(f"p_tile{b}"), 16)

            unrolled_slots(slot)
            with sp.Fori(0, GROUPS) as g:
                sp.wait_ge(sem("added"), g * E + (GROUPS + 1) * E + 1)
                sp.dma_start(out_tile[:, bass.ds(g * GT, GT), :],
                             xres[:, bass.ds(g * GT, GT), :]).then_inc(sem("stored"), 16)
            sp.wait_ge(sem("stored"), 16 * GROUPS)

        @block.gpsimd
        def _(pool):
            pool.memset(ident[:, :], 0.0).then_inc(sem("ident_zero"), 1)
            pool.memset(head_mask[:, :, :], 1.0).then_inc(sem("mask_one"), 1)
            for b in range(B):
                pool.memset(xc[b][0:1, 0, :], 0.0).then_inc(sem("pad_zero"), 1)
            pool.wait_ge(sem("ident_zero"), 1)
            pool.affine_select(out=ident[:, :], in_=ident[:, :], compare_op=ALU.not_equal, fill=1.0,
                               base=0, pattern=[[-1, P]], channel_multiplier=1).then_inc(sem("ident"), 1)
            pool.wait_ge(sem("mask_one"), 1)
            pool.affine_select(out=head_mask[:, :, :], in_=head_mask[:, :, :], compare_op=ALU.is_ge, fill=0.0,
                               base=0, pattern=[[-DH, H], [0, DH]], channel_multiplier=1).then_inc(sem("mask_low"), 1)
            pool.wait_ge(sem("mask_low"), 1)
            pool.affine_select(out=head_mask[:, :, :], in_=head_mask[:, :, :], compare_op=ALU.is_ge, fill=0.0,
                               base=DH - 1, pattern=[[DH, H], [0, DH]], channel_multiplier=-1).then_inc(sem("head_mask"), 1)
            pool.iota(steps[:, 0:C + 1], pattern=[[1, C + 1]], base=0, channel_multiplier=0).then_inc(sem("iotas"), 1)
            pool.iota(steps[:, C + 1:2 * C + 1], pattern=[[-1, C]], base=C - 1, channel_multiplier=0).then_inc(sem("iotas"), 1)
            pool.iota(iota8_i[:, :], pattern=[[1, E]], base=0, channel_multiplier=0).then_inc(sem("iotas"), 1)
            pool.memset(half[:, :], -0.5).then_inc(sem("half"), 1)

            for b in range(B):
                if b:
                    pool.wait_ge(sem("l2_mm"), UNITS)
                pool.memset(att[:, :, :, :], 0.0).then_inc(sem("att_zero"), 1)
                pool.memset(tri[:, :, :, :], 0.0).then_inc(sem("tri_zero"), 1)
                pool.wait_ge(sem("att_zero"), b + 1)
                pool.wait_ge(sem("tri_zero"), b + 1)
                pool.memset(diagonal(tri, 0, C), 1.0).then_inc(sem("tri_one"), 1)
                pool.wait_ge(sem("neg_power"), 1)
                pool.wait_ge(sem("beta"), b + 1)
                for delta in range(1, C + 1):
                    rows = C + 1 - delta
                    g = diag[:, delta % 2, :, :]
                    pool.wait_ge(sem("diag"), C * b + delta)
                    if delta < C:
                        low = rows - 1
                        if delta > 1:
                            pool.wait_ge(sem("tri_diag"), (C - 1) * b + delta - 1)
                        pool.tensor_tensor(diag_n[:, 0:low, :], g[:, 0:low, :],
                                           neg_power[:, delta:delta + 1, :].to_broadcast([NC, low, H]),
                                           ALU.mult).then_inc(sem("diag_n"), 1)
                        pool.wait_ge(sem("diag_n"), (C - 1) * b + delta)
                        pool.tensor_tensor(diagonal(tri, delta, low), diag_n[:, 0:low, :], beta[:, delta:C, :],
                                           ALU.mult).then_inc(sem("tri_diag"), 1)
                    pool.tensor_tensor(diagonal(att, delta - 1, rows), g[:, 0:rows, :],
                                       power[:, delta - 1:delta, :].to_broadcast([NC, rows, H]),
                                       ALU.mult).then_inc(sem("diag_used"), 1)

            wide = [P, TILES, D]
            pool.wait_ge(sem("res_scale"), 1)
            pool.tensor_tensor(xres[:, :, :], xres[:, :, :], rstd[:, :].unsqueeze(2).to_broadcast(wide),
                               ALU.mult).then_inc(sem("res_scaled"), 1)
            pool.wait_ge(sem("res_scaled"), 1)
            pool.tensor_tensor(xres[:, :, :], xres[:, :, :], mean[:, :].unsqueeze(2).to_broadcast(wide),
                               ALU.add).then_inc(sem("res_ready"), 1)

            pool.wait_ge(sem("l2_even"), B * UNITS // 2)
            pool.wait_ge(sem("l2_odd"), B * UNITS // 2)

            def slot(t, b):
                (t1, b1), (t3, b3) = unit_after(t, b, 1), unit_after(t, b, 3)
                if exists(t1):
                    pool.wait_ge(sem(f"state_mm{b1}"), t1 * CPT + 1)
                    pool.tensor_tensor(ex[b1]["k"][:, :, :, :], over_pair(pk[:, b1, bass.ds(t1 * CPT, CPT), 1, :]), mask,
                                       ALU.mult).then_inc(sem(f"ex_k{b1}"), 1)
                if exists(t3):
                    pool.wait_ge(sem(f"uw_mm{b3}"), t3 + 1)
                    pool.tensor_tensor(ex[b3]["t"][:, :, :, :], over_pair(tt[:, b3, bass.ds(t3 * CPT, CPT), :]), mask,
                                       ALU.mult).then_inc(sem(f"ex_t{b3}"), 1)
                if exists(t1):
                    pool.wait_ge(sem(f"mt{b1}"), t1 + 2)
                    pool.tensor_tensor(ex[b1]["m"][:, :, :, :], over_pair(mt[b1][:, :, :]), mask,
                                       ALU.mult).then_inc(sem(f"ex_m{b1}"), 1)

            run_slots(pool, slot)

            for b in range(B):
                pool.wait_ge(sem(f"x1_{b}"), NT + 1)
            pool.iota(ang_i[:, :], pattern=[[1, T]], base=0, channel_multiplier=0).then_inc(sem("positions"), 1)

            def inverse_deviation(k):
                pool.wait_ge(sem("ln_var"), k + 1)
                pool.tensor_tensor(rstd[:, 0:GT], var[:, 0:GT], half[:, :], ALU.pow).then_inc(sem("ln_rstd"), 1)

            def ffn(lo):
                with pool.Fori(lo, lo + GROUPS) as g:
                    inverse_deviation(g + ffn_k(lo))

            ffn(0)
            for b in range(B):
                with pool.Fori(b * GROUPS // B, (b + 1) * GROUPS // B) as g:
                    inverse_deviation(g + BT_K)
                    for k, table in enumerate((cos_t, sin_t)):
                        pool.wait_ge(sem(f"trace{k}"), g + 1)
                        pool.wait_ge(sem("retr"), g + 1)
                        pool.tensor_tensor(back[:, k, :], trace[:, k, :], table[:, bass.ds(g * GW - b * T, GW)],
                                           ALU.mult).then_inc(sem(f"back{k}"), 1)
            ffn(GROUPS)

        @block.scalar
        def _(act):
            for name in ("v", "s", "wtr", "uw0", "uw1", "state0", "state1"):
                act.sem_inc(sem(name), 1)
            act.dma_start(decay_rows[:, :], decay.rearrange("(a h) -> a h", a=1).to_broadcast([P, H])).then_inc(sem("decay_loaded"), 16)
            for i, w in enumerate((w_write, w_read, w_v, w_o)):
                act.dma_start(wn[:, i, :], w).then_inc(sem("wn_loaded"), 16)
            act.dma_start(wbn[:, :], w_beta).then_inc(sem("wn_loaded"), 16)
            act.dma_start(w1n[:, :, :].rearrange("p (m k) d -> p m (k d)", k=2),
                          w1.rearrange("e (c p k) d -> p (e c) (k d)", c=FC, k=2)).then_inc(sem("w1_loaded"), 16)
            act.dma_start(w2n[:, :, :].rearrange("d (e c) p -> d e (c p)", c=FC),
                          w2.rearrange("e d f -> d e f")).then_inc(sem("w2_loaded"), 16)

            act.wait_ge(sem("decay_floor"), 1)
            act.activation(soft[:, :], soft[:, :], ACT.Exp, scale=-1.0).then_inc(sem("exp_decay"), 1)
            act.wait_ge(sem("exp_decay1"), 1)
            act.activation(soft[:, :], soft[:, :], ACT.Ln).then_inc(sem("log"), 1)
            act.wait_ge(sem("power_arg"), 1)
            act.activation(power[:, :, :], power[:, :, :], ACT.Exp, scale=-1.0).then_inc(sem("power"), 1)
            act.wait_ge(sem("soft_col"), 1)
            act.activation(gamma_col[:, :], soft_col[:, 0:1], ACT.Exp, scale=-float(C)).then_inc(sem("gamma_col"), 1)

            act.wait_ge(sem("wsmall_mm"), 1)
            act.activation(wsmall[:, :, :].rearrange("p i d -> p (i d)"), bank[5][:, :], ACT.Copy).then_inc(sem("w_evac"), 1)
            act.wait_ge(sem("wbeta_mm"), 1)
            act.activation(w_beta_t[:, :], bank[4][:, 0:H], ACT.Copy).then_inc(sem("wbeta"), 1)

            for b in range(B):
                act.wait_ge(sem("centred"), b + 1)
                act.activation(sq[:, :, :], xc[b][:, :, :], ACT.Square).then_inc(sem("sq"), 1)
                act.wait_ge(sem("chunk_var"), b + 1)
                act.activation(s17[:, :], s17[:, :], ACT.Sqrt).then_inc(sem("chunk_std"), 1)
                act.wait_ge(sem("normed"), b + 1)
                act.activation(sq[:, :, :], xc[b][:, :, :], ACT.Square).then_inc(sem("sq"), 1)
                act.wait_ge(sem("head_sq"), b + 1)
                act.activation(s136[:, :, :], s136[:, :, :], ACT.Sqrt).then_inc(sem("head_norm"), 1)
                for q in range(4):
                    act.wait_ge(sem("hx_mm"), 4 * b + q + 1)
                    act.activation(ca[:, 4 * q:4 * q + 4, :].rearrange("p i n -> p (i n)"), bank[q][:, :],
                                   ACT.Copy).then_inc(sem("hx"), 1)
                act.wait_ge(sem("beta_mm"), b + 1)
                act.activation(beta[:, :, :].rearrange("p i h -> p (i h)"), bank[4][:, 0:C * H],
                               ACT.Sigmoid).then_inc(sem("beta"), 1)
                if b == 0:
                    for g, (_, dest, at) in enumerate(W_GROUPS):
                        act.wait_ge(sem("w_mm"), g + 1)
                        act.activation(dest[:, at:at + 4, :].rearrange("p m d -> p (m d)"), bank[W_BANK[g % 2]][:, :],
                                       ACT.Copy).then_inc(sem("w_evac"), 1)
                for unit in range(UNITS * b, UNITS * (b + 1), 2):
                    act.wait_ge(sem("l2_mm"), unit + 1)
                    act.activation(l2_dest(unit), l2_bank(unit), ACT.Copy).then_inc(sem("l2_even"), 1)

                if b == 0:
                    act.wait_ge(sem("ln_var"), 1)
                    act.activation(rstd[:, :], var[:, :], ACT.Sqrt).then_inc(sem("ln_rstd"), 1)

            def slot(t, b):
                t2 = unit_after(t, b, 2)[0]
                before = unit_after(t, b, -2)[0]
                for n in range(CPT):
                    if exists(t):
                        act.wait_ge(sem(f"state_mm{b}"), t * CPT + n + 2)
                        act.activation(state[b][:, n + 1, :], bank[4 + n % 2][:, n * DH:(n + 1) * DH],
                                       ACT.Copy).then_inc(sem(f"state{b}"), 1)
                    if n == 1 and exists(before):
                        act.wait_ge(sem(f"o_mm{b}"), before + 2)
                        act.activation(ot[b][:, :], bank[6 + b][:, 0:P], ACT.Copy).then_inc(sem(f"ot{b}"), 1)
                if exists(t2):
                    act.wait_ge(sem(f"uw_mm{b}"), t2 + 2)
                    act.wait_ge(sem(f"ex_u{b}"), t2 + 1)
                    act.activation(uw[b][:, :, :, :].rearrange("p n k d -> p (n k d)"), bank[b][:, 0:CPT * 2 * DH],
                                   ACT.Copy).then_inc(sem(f"uw{b}"), 1)

            run_slots(act, slot)

            def ffn(lo):
                def columns(g, i):
                    act.wait_ge(sem("ht_mm"), g + ffn_k(lo))
                    act.activation(ht_hi[i][:, :], bank[0][:, :], ACT.Copy).then_inc(sem("ht_hi"), 1)
                    act.activation(ht[i][:, :], bank[0][:, :], ACT.Copy).then_inc(sem("ht"), 1)

                def softmax(g):
                    act.wait_ge(sem("gap"), g + 1)
                    act.activation(wsel[:, :, :], gap[:, :, :], ACT.Sigmoid).then_inc(sem("wsel"), 1)

                def first(g):
                    columns(g, 0)
                    softmax(g)

                def group(g, i, last):
                    for n in range(UP):
                        e, c, k = n // FC, n % FC, n % 2
                        if n == 1:
                            act.wait_ge(sem("wt_mm"), g + 1)
                            act.activation(wtr[:, :], bank[1][0:E, :], ACT.Copy).then_inc(sem("wtr"), 1)
                        if n == 8 and not last:
                            columns(g + 1, 1 - i)
                        if n == 14 and not last:
                            softmax(g + 1)
                        act.wait_ge(sem("up"), g * UP + n + 1)
                        act.wait_ge(sem("h"), g * UP + max(n, 1))
                        act.activation(vact[k][:, :], bank[4 + k][:, :], ACT.Identity,
                                       bias=b1v_col[:, e, c:c + 1]).then_inc(sem("v"), 1)
                        act.activation(gs[k][:, :], bank[2 + k][:, :], ACT.Gelu_apprx_sigmoid,
                                       bias=b1_col[:, e, c, 0:1]).then_inc(sem("s"), 1)

                ffn_groups(act, lo, first, group)

            ffn(0)
            act.wait_ge(sem("angles"), 1)
            act.activation(sin_t[:, :], sin_t[:, :], ACT.Sin).then_inc(sem("trig"), 1)
            act.activation(cos_t[:, :], cos_t[:, :], ACT.Sin).then_inc(sem("trig"), 1)
            with act.Fori(0, GROUPS) as g:
                act.wait_ge(sem("ht_mm"), g + BT_K)
                act.activation(ht[0][:, :], bank[0][:, :], ACT.Copy).then_inc(sem("ht"), 1)
            ffn(GROUPS)

        @block.tensor
        def _(pe):
            for name in ("down", "bt_y_mm", "uw_mm0", "uw_mm1", "qm_mm0", "qm_mm1", "state_mm0", "state_mm1", "o_mm0", "o_mm1"):
                pe.sem_inc(sem(name), 1)
            pe.wait_ge(sem("ident"), 1)
            pe.wait_ge(sem("wn_loaded"), 5 * 16)
            for i in range(4):
                mm = pe.transpose(bank[5][:, i * P:(i + 1) * P], wn[:, i, :], ident[:, :])
            mm.then_inc(sem("wsmall_mm"), 1)
            pe.transpose(bank[4][:, 0:H], wbn[:, :], ident[0:H, 0:H]).then_inc(sem("wbeta_mm"), 1)
            pe.wait_ge(sem("w_evac"), 1)
            pe.wait_ge(sem("wbeta"), 1)

            for b in range(B):
                pe.wait_ge(sem("normed"), b + 1)
                for q in range(4):
                    if b:
                        pe.wait_ge(sem("v_src"), 4 * b)
                    for i in range(4 * q, 4 * q + 4):
                        mm = pe.transpose(bank[q][:, i % 4 * P:(i % 4 + 1) * P], xc[b][:, i + 1, :], ident[:, :])
                    mm.then_inc(sem("hx_mm"), 1)
                for q in range(4):
                    pe.wait_ge(sem("hx"), 4 * b + q + 1)
                    for i in range(4 * q, 4 * q + 4):
                        mm = pe.matmul(bank[q][:, i % 4 * P:(i % 4 + 1) * P], ca[:, i, :], w_write_t, start=True, stop=True)
                    mm.then_inc(sem("v_mm"), 1)
                for i in range(C):
                    mm = pe.matmul(bank[4][:, i * H:(i + 1) * H], ca[:, i, :], w_beta_t[:, :], start=True, stop=True)
                mm.then_inc(sem("beta_mm"), 1)
                if b == 0:
                    pe.wait_ge(sem("w1_loaded"), 16)
                    pe.wait_ge(sem("w2_loaded"), 16)
                    for g, (src, _, at) in enumerate(W_GROUPS):
                        if g == 1:
                            pe.wait_ge(sem("beta"), 1)
                        if g >= 2:
                            pe.wait_ge(sem("w_evac"), g)
                        for m in range(4):
                            mm = pe.transpose(bank[W_BANK[g % 2]][:, m * P:(m + 1) * P], src[:, at + m, :], ident[:, :])
                        mm.then_inc(sem("w_mm"), 1)
                for unit in range(UNITS * b, UNITS * (b + 1)):
                    kind, q = ORDER[unit % UNITS // 4], unit % 4
                    if kind == "v":
                        pe.wait_ge(sem("v_src"), 4 * (b + 1))
                    elif kind == "p":
                        pe.wait_ge(sem("diag_used"), C * (b + 1))
                    elif kind == "t":
                        pe.wait_ge(sem("row_added"), (C - 2) * (b + 1))
                    else:
                        pe.wait_ge(sem(f"{kind}_src"), b + 1)
                    if unit >= 2:
                        pe.wait_ge(sem("l2_odd" if unit % 2 else "l2_even"), unit // 2)
                    for i in range(4 * q, 4 * q + 4):
                        mm = pe.transpose(bank[L2_BANK[unit % 2]][:, i % 4 * P:(i % 4 + 1) * P], l2_source(kind, i), ident[:, :])
                    mm.then_inc(sem("l2_mm"), 1)

            pe.wait_ge(sem("l2_even"), B * UNITS // 2)
            pe.wait_ge(sem("l2_odd"), B * UNITS // 2)

            PAIRS = [slice(q * 2 * DH, (q + 1) * 2 * DH) for q in range(H // 2)]

            def product(dest, stationary, moving, start=True, stop=True):
                for q in PAIRS:
                    mm = pe.matmul(dest[q, :], stationary[q, :, :].rearrange("p k d -> p (k d)"), moving[q, :], start=start, stop=stop)
                return mm

            def uw_products(t, b, lo, hi):
                if lo == 0:
                    pe.wait_ge(sem(f"ex_t{b}"), t + 1)
                    pe.wait_ge(sem(f"vk_tile{b}"), 16 * (t + 1))
                    pe.wait_ge(sem(f"uw{b}"), t + 1)
                for n in range(lo, hi):
                    mm = product(bank[b][:, n * 32:n * 32 + 32], ex[b]["t"][:, n, :, :],
                                 vk_tile[b][:, n, :, :].rearrange("p k d -> p (k d)"))
                if hi == CPT:
                    mm.then_inc(sem(f"uw_mm{b}"), 1)

            def qm_products(t, b, lo, hi):
                if lo == 0:
                    pe.wait_ge(sem(f"ex_w{b}"), t + 1)
                    pe.wait_ge(sem(f"pk_tile{b}"), 16 * (t + 1))
                    pe.wait_ge(sem(f"qt{b}"), t + 1)
                for n in range(lo, hi):
                    mm = product(bank[2 + b][:, n * 32:n * 32 + 32], ex[b]["w"][:, n, :, :],
                                 pk_tile[b][:, n, :, :].rearrange("p k d -> p (k d)"))
                if hi == CPT:
                    mm.then_inc(sem(f"qm_mm{b}"), 1)

            def state_step(t, b, n):
                dest = bank[4 + n % 2][:, n * DH:(n + 1) * DH]
                if n == 0:
                    pe.wait_ge(sem(f"ex_k{b}"), t + 1)
                    pe.wait_ge(sem(f"uw{b}"), t + 2)
                if n == 1:
                    pe.wait_ge(sem(f"state{1 - b}"), (t + b) * CPT + 1)
                product(dest, ex[b]["k"][:, n, :, :], uw[b][:, n, 0, :], stop=False)
                if n == 0:
                    pe.wait_ge(sem(f"ex_m{b}"), t + 1)
                    pe.wait_ge(sem(f"first{b}"), t + 1)
                else:
                    pe.wait_ge(sem(f"state{b}"), t * CPT + n + 1)
                product(dest, ex[b]["m"][:, n, :, :], state[b][:, n, :], start=False).then_inc(sem(f"state_mm{b}"), 1)

            def o_products(t, b, lo, hi):
                if lo == 0:
                    pe.wait_ge(sem(f"ex_s{b}"), t + 1)
                    pe.wait_ge(sem(f"ex_u{b}"), t + 2)
                    pe.wait_ge(sem(f"p_tile{b}"), 16 * (t + 1))
                    pe.wait_ge(sem(f"x1_{b}"), t + 1)
                for n in range(lo, hi):
                    dest = bank[6 + b][:, n * C:(n + 1) * C]
                    product(dest, ex[b]["u"][:, n, :, :], p_tile[b][:, n, 0, :], stop=False)
                    mm = product(dest, ex[b]["s"][:, n, :, :], qt[b][:, n, :], start=False)
                if hi == CPT:
                    mm.then_inc(sem(f"o_mm{b}"), 1)

            def slot(t, b):
                (t1, b1), (tb, bb) = unit_after(t, b, 1), unit_after(t, b, -1)
                t2, before = unit_after(t, b, 2)[0], unit_after(t, b, -2)[0]
                half_tile, pair = CPT // 2, CPT // 4
                for n in range(CPT):
                    if exists(t):
                        state_step(t, b, n)
                    if n < 2 and exists(t2):
                        uw_products(t2, b, n * half_tile, (n + 1) * half_tile)
                    if n in (2, 3) and exists(t1):
                        qm_products(t1, b1, (n - 2) * half_tile, (n - 1) * half_tile)
                    if n == 3 and exists(before):
                        pe.wait_ge(sem(f"ot{b}"), before + 1)
                        pe.matmul(bank[6 + b][:, P:2 * P], ot[b][:, :], w_read_t, start=True, stop=True).then_inc(sem(f"y_mm{b}"), 1)
                    if n >= 4 and exists(tb):
                        o_products(tb, bb, (n - 4) * pair, (n - 3) * pair)

            unrolled_slots(slot)

            def rows_to_columns(k):
                pe.wait_ge(sem("ln_rows"), k)
                for q in range(GT):
                    mm = pe.transpose(bank[0][:, q * P:(q + 1) * P], hrow[:, q, :], ident[:, :])
                mm.then_inc(sem("ht_mm"), 1)

            def ffn(lo):
                def columns(g):
                    pe.wait_ge(sem("bias_added"), g + 1)
                    rows_to_columns(g + ffn_k(lo))

                def gates_of(g, i):
                    pe.wait_ge(sem("ht"), g + ffn_k(lo))
                    pe.wait_ge(sem("wtr"), g + 1)
                    for q in range(GT):
                        mm = pe.matmul(bank[1][:, q * E:(q + 1) * E], ht[i][:, q * P:(q + 1) * P], gate_sb[:, :], start=True, stop=True)
                    mm.then_inc(sem("gate_mm"), 1)

                def up(g, i, n):
                    pe.wait_ge(sem("v"), g * UP + max(n, 1))
                    pe.wait_ge(sem("s"), g * UP + max(n, 1))
                    for at, dest in ((2 * n, bank[2 + n % 2]), (2 * n + 1, bank[4 + n % 2])):
                        pe.matmul(dest[:, :], w1_hi[:, at, :], ht_hi[i][:, :], start=True, stop=False)
                        pe.matmul(dest[:, :], w1_hi[:, at, :], ht_lo[i][:, :], start=False, stop=False)
                        mm = pe.matmul(dest[:, :], w1_lo[:, at, :], ht_hi[i][:, :], start=False, stop=True)
                    mm.then_inc(sem("up"), 1)

                def down(g, e):
                    pe.wait_ge(sem("h"), g * UP + FC * (e + 1) + 1)
                    pe.wait_ge(sem("added"), g * E + max(e, 1))
                    for q in range(GT):
                        for c in range(FC):
                            mm = pe.matmul(bank[6 + e % 2][:, q * D:(q + 1) * D], hmid[e % 2][c][:, q * P:(q + 1) * P],
                                           w2t[:, FC * e + c, :], start=(c == 0), stop=(c == FC - 1))
                    mm.then_inc(sem("down"), 1)

                def first_units(g, i):
                    pe.wait_ge(sem("ht_lo"), g + 1)
                    for n in range(FC):
                        up(g, i, n)

                def first(g):
                    columns(g)
                    gates_of(g, 0)
                    first_units(g, 0)

                def group(g, i, last):
                    pe.wait_ge(sem("wrow"), g + 1)
                    for q in range(GT):
                        mm = pe.transpose(bank[1][0:E, q * P:(q + 1) * P], wrow[i][:, q, :], ident[:, :])
                    mm.then_inc(sem("wt_mm"), 1)
                    for e in range(E):
                        if e + 1 < E:
                            for c in range(FC):
                                up(g, i, FC * (e + 1) + c)
                                if e == 0 and c == 0:
                                    pe.wait_ge(sem("wtr"), g + 2)
                                    for q in range(GT):
                                        mm = pe.matmul(bank[0][:, q * D:(q + 1) * D], wtr[:, q * P:(q + 1) * P], b2_rows[:, :], start=True, stop=True)
                                    mm.then_inc(sem("bias_mm"), 1)
                        elif not last:
                            first_units(g + 1, 1 - i)
                        if e == 3 and not last:
                            columns(g + 1)
                        if e == 5 and not last:
                            gates_of(g + 1, 1 - i)
                        down(g, e)

                ffn_groups(pe, lo, first, group)

            pe.wait_ge(sem("small_loaded"), 4 * 16)
            pe.wait_ge(sem("w1_lo"), 4)
            ffn(0)
            with pe.Fori(0, GROUPS) as g:
                rows_to_columns(g + BT_K)
                pe.wait_ge(sem("ht"), g + BT_K)
                pe.wait_ge(sem("rotated"), 2 * g + 1)
                pe.matmul(bank[1][:, :], w_v_t, ht[0][:, :], start=True, stop=True).then_inc(sem("bt_v_mm"), 1)
                pe.wait_ge(sem("retr"), g + 2)
                pe.wait_ge(sem("x3"), g + 1)
                for q in range(GT):
                    mm = pe.matmul(bank[2][:, q * D:(q + 1) * D], retr[:, q * P:(q + 1) * P], w_o_t, start=True, stop=True)
                mm.then_inc(sem("bt_y_mm"), 1)
            ffn(GROUPS)

        @block.vector
        def _(dve):
            for name in ("h", "added", "rotated", "retr", "x3", "carried", "bias_added", "mt0", "mt1", "qt0", "qt1", "ex_u0", "ex_u1", "x1_0", "x1_1"):
                dve.sem_inc(sem(name), 1)
            linked = [0]

            def link(ins):
                linked[0] += 1
                ins.then_inc(sem("vector_link"), 1)
                dve.wait_ge(sem("vector_link"), linked[0])

            dve.wait_ge(sem("decay_loaded"), 16)
            dve.tensor_scalar(soft[:, :], decay_rows[:, :], -40.0, None, ALU.max).then_inc(sem("decay_floor"), 1)
            dve.wait_ge(sem("exp_decay"), 1)
            dve.tensor_scalar(soft[:, :], soft[:, :], 1.0, None, ALU.add).then_inc(sem("exp_decay1"), 1)
            dve.wait_ge(sem("log"), 1)
            dve.scalar_tensor_tensor(out=soft[:, :], in0=decay_rows[:, :], scalar=-1.0, in1=soft[:, :],
                                     op0=ALU.mult, op1=ALU.max).then_inc(sem("soft"), 1)
            dve.wait_ge(sem("iotas"), 3)
            link(dve.tensor_copy(steps_f[:, :], steps[:, :]))
            dve.tensor_copy(iota8[:, :], iota8_i[:, :])
            dve.wait_ge(sem("soft"), 1)
            shape = [P, 2 * C + 1, H]
            dve.tensor_tensor(power[:, :, :], steps_f[:, :].unsqueeze(2).to_broadcast(shape),
                              soft[:, :].unsqueeze(1).to_broadcast(shape), ALU.mult).then_inc(sem("power_arg"), 1)
            dve.wait_ge(sem("head_mask"), 1)
            link(dve.tensor_tensor(neg_power[:, 0, :], soft[:, :], head_mask[:, :, 0], ALU.mult))
            dve.tensor_reduce(soft_col[:, 0:1], neg_power[:, 0, :], AX, ALU.add).then_inc(sem("soft_col"), 1)
            dve.wait_ge(sem("ident"), 1)
            link(dve.tensor_reduce(pair_mask[:, :, :], head_mask[:, :, :].rearrange("p (q k) d -> p k d q", k=2), AX, ALU.add))
            link(dve.tensor_reduce(rep[:, :], ident[:, :].rearrange("p (h d) -> p d h", h=H), AX, ALU.add))
            dve.wait_ge(sem("power"), 1)
            dve.wait_ge(sem("soft_col"), 1)
            dve.tensor_scalar(neg_power[:, :, :], power[:, 0:C + 1, :], -1.0, None, ALU.mult).then_inc(sem("neg_power"), 1)
            dve.wait_ge(sem("gamma_col"), 1)
            link(dve.tensor_scalar(gamma_rep[:, :], rep[:, :], gamma_col[:, :], None, ALU.mult))
            dve.wait_ge(sem("small_loaded"), 4 * 16)
            link(dve.tensor_scalar(b1v_col[:, :, :], b1_col[:, :, :, 1], 1.0, None, ALU.add))

            def variance(rows, k):
                even_m, odd_m = stat[:, 0:rows, 1], stat[:, 0:rows, 4]
                dve.wait_ge(sem("ln_stat"), k + 1)
                dve.tensor_tensor(mean[:, 0:rows], even_m, odd_m, ALU.add)
                dve.tensor_tensor(sumsq[:, 0:rows], stat[:, 0:rows, 2], stat[:, 0:rows, 5], ALU.add)
                dve.tensor_tensor(dev[:, 0:rows], even_m, odd_m, ALU.subtract).then_inc(sem("ln_dev"), 1)
                dve.wait_ge(sem("ln_dev"), k + 1)
                dve.tensor_scalar(mean[:, 0:rows], mean[:, 0:rows], 0.5, None, ALU.mult)
                dve.tensor_tensor(dev[:, 0:rows], dev[:, 0:rows], dev[:, 0:rows], ALU.mult).then_inc(sem("ln_dev_sq"), 1)
                dve.wait_ge(sem("ln_dev_sq"), k + 1)
                dve.scalar_tensor_tensor(out=sumsq[:, 0:rows], in0=dev[:, 0:rows], scalar=D / 4.0, in1=sumsq[:, 0:rows],
                                         op0=ALU.mult, op1=ALU.add).then_inc(sem("ln_sumsq"), 1)
                dve.wait_ge(sem("ln_sumsq"), k + 1)
                dve.tensor_scalar(var[:, 0:rows], sumsq[:, 0:rows], 1.0 / D, EPS, ALU.mult, ALU.add).then_inc(sem("ln_var"), 1)

            def l2_evac(*units):
                for unit in units:
                    dve.wait_ge(sem("l2_mm"), unit + 1)
                    dve.tensor_copy(l2_dest(unit), l2_bank(unit)).then_inc(sem("l2_odd"), 1)

            dve.wait_ge(sem("pad_zero"), B)
            for b in range(B):
                dve.wait_ge(sem("x_loaded"), 4 * 16)
                link(dve.tensor_reduce(s17[:, :], xc[b][:, :, :], AX, ALU.add))
                link(dve.tensor_scalar(r17[:, :], s17[:, :], -1.0 / D, None, ALU.mult))
                dve.tensor_tensor(xc[b][:, :, :], xc[b][:, :, :], r17[:, :].unsqueeze(2).to_broadcast([NC, C + 1, D]),
                                  ALU.add).then_inc(sem("centred"), 1)
                dve.wait_ge(sem("sq"), 2 * b + 1)
                link(dve.tensor_reduce(s17[:, :], sq[:, :, :], AX, ALU.add))
                dve.tensor_scalar(s17[:, :], s17[:, :], 1.0 / D, EPS, ALU.mult, ALU.add).then_inc(sem("chunk_var"), 1)
                dve.wait_ge(sem("chunk_std"), b + 1)
                link(dve.reciprocal(r17[:, :], s17[:, :]))
                dve.tensor_tensor(xc[b][:, :, :], xc[b][:, :, :], r17[:, :].unsqueeze(2).to_broadcast([NC, C + 1, D]),
                                  ALU.mult).then_inc(sem("normed"), 1)
                dve.wait_ge(sem("sq"), 2 * b + 2)
                link(dve.tensor_reduce(s136[:, :, :], sq[:, :, :].rearrange("p i (h d) -> p i h d", h=H), AX, ALU.add))
                dve.tensor_scalar(s136[:, :, :], s136[:, :, :], 1e-24, None, ALU.max).then_inc(sem("head_sq"), 1)
                dve.wait_ge(sem("head_norm"), b + 1)
                link(dve.reciprocal(r136[:, :, :], s136[:, :, :]))
                dve.wait_ge(sem("hx_mm"), 4 * (b + 1))
                keys = xc[b][:, :, :].rearrange("p i (h d) -> p i h d", h=H)
                link(dve.tensor_tensor(keys, keys, over_width(r136[:, :, :], C + 1), ALU.mult))
                dve.wait_ge(sem("beta"), b + 1)
                link(dve.tensor_tensor(bgam[:, :, :], beta[:, :, :], power[:, 1:C + 1, :], ALU.mult))
                turned = [s[:, :, :].rearrange("p d (h i) -> p i h d", h=H) for s in (ca, cb)]
                for q in range(4):
                    dve.wait_ge(sem("v_mm"), 4 * b + q + 1)
                    dve.tensor_tensor(turned[1][:, 4 * q:4 * q + 4, :, :], bank[q][:, :].rearrange("p (i h d) -> p i h d", i=4, h=H),
                                      over_width(beta[:, 4 * q:4 * q + 4, :], 4), ALU.mult).then_inc(sem("v_src"), 1)
                dve.wait_ge(sem("beta_mm"), b + 1)
                dve.tensor_tensor(turned[0], keys[:, 0:C, :, :], over_width(bgam[:, :, :], C), ALU.mult).then_inc(sem("kb_src"), 1)
                first = UNITS * b
                l2_evac(first + 1, first + 3)
                dve.wait_ge(sem("l2_mm"), first + 4)
                dve.tensor_tensor(turned[1], keys[:, 0:C, :, :], over_width(power[:, C + 1:2 * C + 1, :], C), ALU.mult).then_inc(sem("kd_src"), 1)
                l2_evac(first + 5, first + 7)
                dve.wait_ge(sem("l2_mm"), first + 8)
                dve.tensor_tensor(ca[:, :, :].rearrange("p i (h d) -> p i h d", h=H), keys[:, 1:C + 1, :, :],
                                  over_width(power[:, 1:C + 1, :], C), ALU.mult).then_inc(sem("r_src"), 1)
                l2_evac(first + 9, first + 11)
                for delta in range(1, C + 1):
                    rows = C + 1 - delta
                    if delta > 1:
                        dve.wait_ge(sem("diag"), C * b + delta - 1)
                    link(dve.tensor_tensor(sq[:, 0:rows, :], xc[b][:, delta:C + 1, :], xc[b][:, 0:rows, :], ALU.mult))
                    if C * b + delta > 2:
                        dve.wait_ge(sem("diag_used"), C * b + delta - 2)
                    dve.tensor_reduce(diag[:, delta % 2, 0:rows, :], sq[:, 0:rows, :].rearrange("p i (h d) -> p i h d", h=H),
                                      AX, ALU.add).then_inc(sem("diag"), 1)
                l2_evac(first + 13, first + 15)
                dve.wait_ge(sem("tri_diag"), (C - 1) * (b + 1))
                dve.wait_ge(sem("tri_one"), b + 1)
                steps_done = (C - 2) * b
                for k in range(1, C - 1):
                    shape = [NC, C - 1 - k, H, k]
                    a_col = tri[:, k + 1:C, :, k:k + 1].to_broadcast(shape)
                    t_row = tri[:, k:k + 1, :, 0:k].to_broadcast(shape)
                    size = (C - 1 - k) * H * k
                    step = sq[:, :, :].rearrange("p i d -> p (i d)")[:, 0:size].rearrange("p (i h j) -> p i h j", h=H, j=k)
                    if k > 1:
                        dve.wait_ge(sem("row_added"), steps_done + k - 1)
                    link(dve.tensor_tensor(step, a_col, t_row, ALU.mult))
                    last = dve.tensor_tensor(tri[:, k + 1:C, :, 0:k], tri[:, k + 1:C, :, 0:k], step, ALU.add)
                    last.then_inc(sem("row_added"), 1)
                l2_evac(first + 17, first + 19, first + 21, first + 23)

                if b == 0:
                    dve.wait_ge(sem("xres_loaded"), 16)
                    for t in range(TILES):
                        ins = dve.bn_stats(stat[:, t, :], xres[:, t, :])
                    ins.then_inc(sem("ln_stat"), 1)
                    variance(TILES, 0)
                    dve.wait_ge(sem("ln_rstd"), 1)
                    link(dve.reciprocal(var[:, :], rstd[:, :]))
                    dve.scalar_tensor_tensor(out=mean[:, :], in0=mean[:, :], scalar=-1.0, in1=var[:, :],
                                             op0=ALU.mult, op1=ALU.mult)
                    dve.tensor_scalar(rstd[:, :], var[:, :], 1.0, None, ALU.add).then_inc(sem("res_scale"), 1)

            dve.wait_ge(sem("l2_even"), B * UNITS // 2)
            dve.wait_ge(sem("l2_odd"), B * UNITS // 2)
            for b in range(B):
                dve.memset(state[b][:, 0, :], 0.0).then_inc(sem(f"first{b}"), 1)
            dve.wait_ge(sem("res_ready"), 1)

            def slot(t, b):
                (t1, b1), (tb, bb) = unit_after(t, b, 1), unit_after(t, b, -1)
                before = unit_after(t, b, -2)[0]
                if isinstance(t, int) and NT - 2 <= t < NT:
                    size = E * FC // 2
                    part = slice((B * (t + 2 - NT) + b) * size, (B * (t + 2 - NT) + b + 1) * size)
                    dve.tensor_copy(w1_hi[:, part, :], w1t[:, part, :]).then_inc(sem("w1_hi"), 1)
                    dve.wait_ge(sem("w1_hi"), B * (t + 2 - NT) + b + 1)
                    dve.tensor_tensor(w1_lo[:, part, :], w1t[:, part, :], w1_hi[:, part, :].bitcast(F32),
                                      ALU.subtract).then_inc(sem("w1_lo"), 1)
                if exists(t1):
                    dve.wait_ge(sem(f"uw{b1}"), t1 + 2)
                    dve.wait_ge(sem(f"qm_mm{b1}"), t1 + 1)
                    dve.tensor_tensor(ex[b1]["w"][:, :, :, :], over_pair(uw[b1][:, :, 1, :]), mask, ALU.mult).then_inc(sem(f"ex_w{b1}"), 1)
                if exists(tb):
                    dve.wait_ge(sem(f"state{bb}"), (tb + 1) * CPT + 1)
                    dve.tensor_tensor(ex[bb]["s"][:, :, :, :], over_pair(state[bb][:, 0:CPT, :]), mask, ALU.mult).then_inc(sem(f"ex_s{bb}"), 1)
                    dve.wait_ge(sem(f"ex_s{bb}"), tb + 1)
                    dve.tensor_copy(state[bb][:, 0, :], state[bb][:, CPT, :]).then_inc(sem(f"first{bb}"), 1)
                if exists(t1):
                    qm = bank[2 + b1][:, 0:CPT * 2 * DH].rearrange("p (n k d) -> p n k d", n=CPT, k=2)
                    dve.wait_ge(sem(f"qm_mm{b1}"), t1 + 2)
                    dve.tensor_tensor(mt[b1][:, :, :], gamma_rep[:, :].unsqueeze(1).to_broadcast([P, CPT, DH]), qm[:, :, 1, :],
                                      ALU.subtract).then_inc(sem(f"mt{b1}"), 1)
                if exists(t):
                    qm = bank[2 + b][:, 0:CPT * 2 * DH].rearrange("p (n k d) -> p n k d", n=CPT, k=2)
                    dve.wait_ge(sem(f"o_mm{b}"), t + 1)
                    dve.tensor_tensor(qt[b][:, :, :], rq[:, b, bass.ds(t * CPT, CPT), :], qm[:, :, 0, :],
                                      ALU.subtract).then_inc(sem(f"qt{b}"), 1)
                    dve.tensor_tensor(ex[b]["u"][:, :, :, :], over_pair(uw[b][:, :, 0, :]), mask, ALU.mult).then_inc(sem(f"ex_u{b}"), 1)
                if exists(before):
                    dve.wait_ge(sem(f"y_mm{b}"), before + 1)
                    here = xres[:, bass.ds(before + b * NT, 1), :].rearrange("p a d -> p (a d)")
                    dve.tensor_tensor(here, here, bank[6 + b][:, P:2 * P], ALU.add).then_inc(sem(f"x1_{b}"), 1)

            run_slots(dve, slot)
            for b in range(B):
                dve.wait_ge(sem(f"x1_{b}"), NT + 1)

            def layernorm_statistics(k, first_tile):
                for q in range(GT):
                    ins = dve.bn_stats(stat[:, q, :], xres[:, bass.ds(first_tile + q, 1), :].rearrange("p a d -> p (a d)"))
                ins.then_inc(sem("ln_stat"), 1)
                variance(GT, k)

            def layernorm_rows(k, first_tile):
                dve.wait_ge(sem("ln_rstd"), k + 1)
                for q in range(GT):
                    ins = dve.tensor_scalar(hrow[:, q, :], xres[:, bass.ds(first_tile + q, 1), :].rearrange("p a d -> p (a d)"),
                                            mean[:, q:q + 1], rstd[:, q:q + 1], ALU.subtract, ALU.mult)
                ins.then_inc(sem("ln_rows"), 1)

            def layernorm(k, first_tile):
                layernorm_statistics(k, first_tile)
                layernorm_rows(k, first_tile)

            def ffn(lo):
                def group_rows(g):
                    return (g - lo) * GT

                def best_two(g):
                    dve.wait_ge(sem("gate_mm"), g + 1)
                    dve.tensor_copy(gates[:, :, :].rearrange("p q e -> p (q e)"), bank[1][:, 0:GT * E]).then_inc(sem("gates"), 1)
                    dve.wait_ge(sem("gates"), g + 1)
                    dve.memset(wait_holder[:, :], 0.0)
                    for q in range(GT):
                        ins = dve.max(top[:, q, :], gates[:, q, :])
                    ins.then_inc(sem("top"), 1)
                    dve.wait_ge(sem("top"), g + 1)
                    for k in range(TOPK):
                        ins = dve.tensor_tensor(gap[:, k, :], top[:, :, k], top[:, :, 1 - k], ALU.subtract)
                    ins.then_inc(sem("gap"), 1)
                    for q in range(GT):
                        ins = dve.max_index(topi[:, q, :], top[:, q, :], gates[:, q, :])
                    ins.then_inc(sem("topi"), 1)
                    dve.wait_ge(sem("topi"), g + 1)
                    dve.tensor_copy(topf[:, :, :], topi[:, :, :]).then_inc(sem("topf"), 1)

                def expert_weights(g, i):
                    dve.wait_ge(sem("topf"), g + 1)
                    shape = [P, GT, E]
                    for k in range(TOPK):
                        ins = dve.tensor_tensor(hot[:, k, :, :], iota8[:, :].unsqueeze(1).to_broadcast(shape),
                                                topf[:, :, k:k + 1].to_broadcast(shape), ALU.is_equal)
                    ins.then_inc(sem("hot"), 1)
                    dve.wait_ge(sem("wsel"), g + 1)
                    dve.wait_ge(sem("hot"), g + 1)
                    for k in range(TOPK):
                        ins = dve.tensor_tensor(hot[:, k, :, :], hot[:, k, :, :], wsel[:, k, :].unsqueeze(2).to_broadcast(shape), ALU.mult)
                    ins.then_inc(sem("hot_w"), 1)
                    dve.wait_ge(sem("hot_w"), g + 1)
                    dve.tensor_tensor(wrow[i][:, :, :], hot[:, 0, :, :], hot[:, 1, :, :], ALU.add).then_inc(sem("wrow"), 1)

                def columns_low(g, i):
                    dve.wait_ge(sem("ht"), g + ffn_k(lo))
                    dve.tensor_tensor(ht_lo[i][:, :], ht[i][:, :], ht_hi[i][:, :].bitcast(F32), ALU.subtract).then_inc(sem("ht_lo"), 1)

                def first(g):
                    layernorm(g + ffn_k(lo), group_rows(g))
                    columns_low(g, 0)
                    best_two(g)
                    expert_weights(g, 0)

                def group(g, i, last):
                    tile = group_rows(g)

                    def hidden(n):
                        e, c, k = n // FC, n % FC, n % 2
                        dve.wait_ge(sem("v"), g * UP + n + 2)
                        dve.tensor_scalar(vact[k][:, :], vact[k][:, :], 1 + LIMIT, 1 - LIMIT, ALU.min, ALU.max).then_inc(sem("clip"), 1)
                        if c == 0:
                            dve.wait_ge(sem("down"), g * E + max(e, 1))
                        dve.wait_ge(sem("clip"), g * UP + n + 1)
                        dve.wait_ge(sem("s"), g * UP + n + 2)
                        dve.scalar_tensor_tensor(out=hmid[e % 2][c][:, :], in0=gs[k][:, :], scalar=GATE_LIMIT, in1=vact[k][:, :],
                                                 op0=ALU.min, op1=ALU.mult).then_inc(sem("h"), 1)

                    def add_expert(e):
                        dve.wait_ge(sem("down"), g * E + e + 2)
                        if e == 0:
                            dve.wait_ge(sem("bias_added"), g + 2)
                        else:
                            dve.wait_ge(sem("added"), g * E + e + 1)
                        for q in range(GT):
                            here = xres[:, bass.ds(tile + q, 1), :].rearrange("p a d -> p (a d)")
                            ins = dve.scalar_tensor_tensor(out=here, in0=bank[6 + e % 2][:, q * D:(q + 1) * D], scalar=wrow[i][:, q, e:e + 1],
                                                           in1=here, op0=ALU.mult, op1=ALU.add)
                        ins.then_inc(sem("added"), 1)

                    for n in range(UP):
                        hidden(n)
                        if n == 2:
                            dve.wait_ge(sem("bias_mm"), g + 1)
                            here = xres[:, bass.ds(tile, GT), :].rearrange("p q d -> p (q d)")
                            dve.tensor_tensor(here, here, bank[0][:, :], ALU.add).then_inc(sem("bias_added"), 1)
                        if n > FC and n % FC == 1:
                            add_expert(n // FC - 1)
                        if not last:
                            if n == 3:
                                layernorm_statistics(g + 1 + ffn_k(lo), tile + GT)
                            if n == 5:
                                layernorm_rows(g + 1 + ffn_k(lo), tile + GT)
                            if n == 9:
                                columns_low(g + 1, 1 - i)
                            if n == 12:
                                best_two(g + 1)
                            if n == 14:
                                expert_weights(g + 1, 1 - i)
                    add_expert(E - 1)

                ffn_groups(dve, lo, first, group)

            dve.wait_ge(sem("half"), 1)
            ffn(0)

            dve.wait_ge(sem("positions"), 1)
            link(dve.tensor_copy(ang[:, :], ang_i[:, :]))
            link(dve.tensor_scalar(ang[:, :], ang[:, :], freq_col[:, :], None, ALU.mult))
            link(dve.tensor_scalar(turn[:, :], ang[:, :], 1 / TWO_PI, MAGIC, ALU.mult, ALU.add))
            link(dve.tensor_scalar(turn[:, :], turn[:, :], MAGIC, None, ALU.subtract))
            for k, part in enumerate((PI_A, PI_B, PI_C)):
                link(dve.scalar_tensor_tensor(out=ang[:, :], in0=turn[:, :], scalar=-part, in1=ang[:, :],
                                         op0=ALU.mult, op1=ALU.add))
            link(dve.tensor_scalar(sin_t[:, :], ang[:, :], PI_LOW, -PI_LOW, ALU.min, ALU.max))
            link(dve.scalar_tensor_tensor(out=cos_t[:, :], in0=sin_t[:, :], scalar=-1.0, in1=sin_t[:, :],
                                     op0=ALU.mult, op1=ALU.max))
            dve.tensor_scalar(cos_t[:, :], cos_t[:, :], -1.0, math.pi / 2, ALU.mult, ALU.add).then_inc(sem("angles"), 1)
            link(dve.memset(ones_row[:, :], 1.0))
            dve.wait_ge(sem("trig"), 2)
            for b in range(B):
                if b:
                    dve.wait_ge(sem("carried"), b * GROUPS // B + 1)
                link(dve.memset(carry[:, :], 0.0))
                with dve.Fori(b * GROUPS // B, (b + 1) * GROUPS // B) as g:
                    layernorm(g + BT_K, g * GT)
                    dve.wait_ge(sem("bt_v_mm"), g + 1)
                    for k, table in enumerate((cos_t, sin_t)):
                        dve.tensor_tensor(vc[:, k, :], bank[1][:, :], table[:, bass.ds(g * GW - b * T, GW)], ALU.mult).then_inc(sem("rotated"), 1)
                    dve.wait_ge(sem("rotated"), 2 * g + 2 + 1)
                    dve.wait_ge(sem("carried"), g + 1)
                    dve.wait_ge(sem("retr"), g + 1)
                    for k in range(2):
                        dve.tensor_tensor_scan(trace[:, k, :], ones_row[:, :], vc[:, k, :], carry[:, k:k + 1],
                                               ALU.mult, ALU.add).then_inc(sem(f"trace{k}"), 1)
                    dve.wait_ge(sem("trace1"), g + 1)
                    dve.tensor_copy(carry[:, :], trace[:, :, GW - 1]).then_inc(sem("carried"), 1)
                    dve.wait_ge(sem("back0"), g + 1)
                    dve.wait_ge(sem("back1"), g + 1)
                    dve.wait_ge(sem("bt_y_mm"), g + 1)
                    dve.tensor_tensor(retr[:, :], back[:, 0, :], back[:, 1, :], ALU.add).then_inc(sem("retr"), 1)
                    dve.wait_ge(sem("bt_y_mm"), g + 2)
                    here = xres[:, bass.ds(g * GT, GT), :].rearrange("p q d -> p (q d)")
                    dve.tensor_tensor(here, here, bank[2][:, :], ALU.add).then_inc(sem("x3"), 1)
            dve.wait_ge(sem("x3"), GROUPS + 1)
            ffn(GROUPS)


_INS = ["L0_attn_a_out", "L0_attn_a_W_write", "L0_attn_a_W_read", "L0_attn_a_W_beta", "L0_attn_a_decay",
        "L0_attn_b_Wk", "L0_attn_b_Wv", "L0_attn_b_Wo", "L0_attn_b_freqs", "L0_ffn_gate_w",
        "L0_ffn_dense_1_w", "L0_ffn_dense_1_b", "L0_ffn_dense_2_w", "L0_ffn_dense_2_b"]


def kernel(**inputs):
    import numpy as _np
    import concourse.bacc as _bacc
    from concourse import mybir as _mybir
    from concourse.bass_utils import run_bass_kernel_spmd as _run

    nc = _bacc.Bacc("TRN2", target_bir_lowering=False, num_devices=1)
    arrays, args = {}, []
    for name in _INS:
        a = _np.ascontiguousarray(inputs[name])
        arrays[f"in_{name}_dram"] = a
        args.append(nc.dram_tensor(f"in_{name}_dram", a.shape, _mybir.dt.from_np(a.dtype), kind="ExternalInput").ap())
    args.append(nc.dram_tensor("out_0_dram", (B, T, D), F32, kind="ExternalOutput").ap())
    build(nc, *args)
    r = _run(nc, [arrays], core_ids=[0])
    return r.results[0]["out_0_dram"]
```

```python
import math
from contextlib import ExitStack

import concourse.bass as bass
from concourse import mybir

F32 = mybir.dt.float32
F32R = mybir.dt.float32r
I32 = mybir.dt.int32
U32 = mybir.dt.uint32
ALU = mybir.AluOpType
ACT = mybir.ActivationFunctionType
AX = mybir.AxisListType.X

P = 128
B, T, D = 2, 2048, 128
H, DH = 8, 16
C = 16
NC = T // C
NT = T // P
CPT = P // C
TILES = B * NT
E, F, TOPK = 8, 256, 2
FC = F // P
GT = 4
GROUPS = TILES // GT
GW = GT * P
EPS = 1e-5
LIMIT, ALPHA = 9.0, 1.702
GATE_LIMIT = LIMIT / (1 + math.exp(-ALPHA * LIMIT))
TWO_PI = 2 * math.pi
PI_A = 6.28125
PI_B = float(int((TWO_PI - PI_A) * 2 ** 20)) / 2 ** 20
PI_C = TWO_PI - PI_A - PI_B
PI_LOW = 3.1415925
MAGIC = 1.5 * 2 ** 23


def build(nc, x, w_write, w_read, w_beta, decay, w_k, w_v, w_o, freqs, gate_w, w1, b1, w2, b2, out):
    SMALL = 16640
    WT = SMALL + 8192
    XRES = WT + 26688
    L2 = XRES + 16384
    WORK = L2 + 98304
    END = nc.sbuf_usable_end

    cursor = {"small": SMALL, "wt": WT, "xres": XRES, "l2": L2, "trig": L2, "turn": L2 + 24576, "ffn": L2 + 32768, "nat": L2, "chunk": WORK, "early": WORK, "expand": WORK, "split": WORK + 25600}
    limit = {"small": WT, "wt": XRES, "xres": L2, "l2": WORK, "trig": L2 + 32768, "turn": L2 + 32768, "ffn": WORK, "nat": WORK, "chunk": END, "early": WORK + 8704, "expand": WORK + 25600, "split": END}

    def sb(area, name, shape, dt=F32):
        size = 4
        for n in shape[1:]:
            size *= n
        offset = cursor[area]
        cursor[area] += (size + 31) // 32 * 32
        assert cursor[area] <= limit[area], (area, name)
        return nc.alloc_sbuf_tensor_at(name, shape, dt, offset=offset)

    ctx = ExitStack()
    with ctx:
        sems = {}

        def sem(name):
            if name not in sems:
                sems[name] = ctx.enter_context(nc.semaphore(name))
            return sems[name]

        bank = [ctx.enter_context(nc.psum_tensor(f"bank{i}", [P, 512], F32)) for i in range(8)]

        ident = sb("small", "ident", [P, P])
        head_mask = sb("small", "head_mask", [P, H, DH])
        pair_mask = sb("small", "pair_mask", [P, 2, DH])
        rep = sb("small", "rep", [P, DH])
        gamma_rep = sb("small", "gamma_rep", [P, DH])
        decay_rows = sb("small", "decay_rows", [P, H])
        soft = sb("small", "soft", [P, H])
        steps = sb("small", "steps", [P, 2 * C + 1], I32)
        steps_f = sb("small", "steps_f", [P, 2 * C + 1])
        power = sb("small", "power", [P, 2 * C + 1, H])
        neg_power = sb("small", "neg_power", [P, C + 1, H])
        soft_col = sb("small", "soft_col", [P, H])
        gamma_col = sb("small", "gamma_col", [P, 1])
        wait_holder = sb("small", "wait_holder", [P, 1])
        freq_col = sb("small", "freq_col", [P, 1])
        iota8_i = sb("small", "iota8_i", [P, E], I32)
        iota8 = sb("small", "iota8", [P, E])
        half = sb("small", "half", [P, TILES])
        b1_col = sb("small", "b1_col", [P, E, FC, 2])
        b1v_col = sb("small", "b1v_col", [P, E, FC])
        b2_rows = sb("small", "b2_rows", [E, D])
        gate_sb = sb("small", "gate_sb", [D, E])
        stat = sb("small", "stat", [P, TILES, 6])
        mean = sb("small", "mean", [P, TILES])
        dev = sb("small", "dev", [P, TILES])
        sumsq = sb("small", "sumsq", [P, TILES])
        var = sb("small", "var", [P, TILES])
        rstd = sb("small", "rstd", [P, TILES])

        w1t = sb("wt", "w1t", [D, E * FC * 2, P])
        w2t = sb("wt", "w2t", [P, E * FC, D])
        wsmall = sb("wt", "wsmall", [D, 4, D])
        w_write_t, w_read_t, w_v_t, w_o_t = (wsmall[:, i, :] for i in range(4))
        w_beta_t = sb("wt", "w_beta_t", [D, H])

        xres = sb("xres", "xres", [P, TILES, D])

        vk = sb("l2", "vk", [P, B, NC, 2, DH])
        pk = sb("l2", "pk", [P, B, NC, 2, DH])
        tt = sb("l2", "tt", [P, B, NC, C])
        rq = sb("l2", "rq", [P, B, NC, C])

        cursor["nat"] += 65536
        w1n = sb("nat", "w1n", [P, E * FC * 2, D])
        w2n = sb("nat", "w2n", [D, E * FC, P])
        wn = sb("nat", "wn", [D, 4, D])
        wbn = sb("nat", "wbn", [H, D])

        xc = [sb("chunk", f"xc{b}", [NC, C + 1, D]) for b in range(B)]
        sq = sb("chunk", "sq", [NC, C + 1, D])
        tri = sb("chunk", "tri", [NC, C, H, C])
        att = sb("chunk", "att", [NC, C, H, C])
        ca = sb("chunk", "ca", [NC, C, P])
        cb = sb("chunk", "cb", [NC, C, P])
        diag = sb("chunk", "diag", [NC, 2, C, H])
        diag_n = sb("chunk", "diag_n", [NC, C, H])
        beta = sb("chunk", "beta", [NC, C, H])
        bgam = sb("chunk", "bgam", [NC, C, H])
        s17 = sb("chunk", "s17", [NC, C + 1])
        r17 = sb("chunk", "r17", [NC, C + 1])
        s136 = sb("chunk", "s136", [NC, C + 1, H])
        r136 = sb("chunk", "r136", [NC, C + 1, H])

        early_t = [sb("early", f"early_t{i}", [P, CPT, 2, DH]) for i in range(2)]
        early_w = [sb("early", f"early_w{i}", [P, CPT, 2, DH]) for i in range(2)]

        kinds = ("t", "w", "u")
        ex = [{k: sb("expand", f"ex_{k}{b}", [P, CPT, 2, DH]) for k in kinds} for b in range(B)]
        uw = [sb("expand", f"uw{b}", [P, CPT, 2, DH]) for b in range(B)]
        step = [sb("expand", f"step{b}", [P, CPT, 2, DH]) for b in range(B)]
        wide = [sb("expand", f"wide{b}", [P, 2, DH]) for b in range(B)]
        state = [sb("expand", f"state{b}", [P, CPT, 2, DH]) for b in range(B)]
        ot = [sb("expand", f"ot{b}", [P, P]) for b in range(B)]
        vk_tile = [sb("expand", f"vk_tile{b}", [P, CPT, 2, DH]) for b in range(B)]
        pk_tile = [sb("expand", f"pk_tile{b}", [P, CPT, 2, DH]) for b in range(B)]
        p_tile = [sb("expand", f"p_tile{b}", [P, CPT, 2, DH]) for b in range(B)]

        w1_hi = sb("split", "w1_hi", [D, E * FC * 2, P], F32R)
        w1_lo = sb("split", "w1_lo", [D, E * FC * 2, P], F32R)

        cos_t = sb("trig", "cos_t", [D, T])
        sin_t = sb("trig", "sin_t", [D, T])
        ang = sb("trig", "ang", [D, T])
        turn = sb("trig", "turn", [D, T])
        position = sb("turn", "position", [D, T], I32)

        hrow = sb("ffn", "hrow", [P, GT, D])
        ht = [sb("ffn", f"ht{i}", [D, GW]) for i in range(2)]
        ht_hi = [sb("ffn", f"ht_hi{i}", [D, GW], F32R) for i in range(2)]
        ht_lo = [sb("ffn", f"ht_lo{i}", [D, GW], F32R) for i in range(2)]
        gates = sb("ffn", "gates", [P, GT, E])
        top = sb("ffn", "top", [P, GT, 8])
        topi = sb("ffn", "topi", [P, GT, 8], U32)
        topf = sb("ffn", "topf", [P, GT, 8])
        gap = sb("ffn", "gap", [P, GT])
        odds = sb("ffn", "odds", [P, GT])
        euler = sb("ffn", "euler", [P, GT])
        half_pi = sb("ffn", "half_pi", [P, 1])
        wsel = sb("ffn", "wsel", [P, 2, GT])
        hot = sb("ffn", "hot", [P, 2, GT, E])
        wrow = [sb("ffn", f"wrow{i}", [P, GT, E]) for i in range(2)]
        wtr = sb("ffn", "wtr", [E, GW])
        vact = [sb("ffn", f"vact{i}", [P, GW]) for i in range(2)]
        gs = [sb("ffn", f"gs{i}", [P, GW]) for i in range(2)]
        hmid = [[sb("ffn", f"hmid{i}{c}", [P, GW]) for c in range(FC)] for i in range(2)]
        htr = sb("ffn", "htr", [D, GW])
        hrow_r = sb("ffn", "hrow_r", [P, GT, D])
        ones_row = sb("ffn", "ones_row", [D, GW])
        vc = sb("ffn", "vc", [D, 2, GW])
        trace = sb("ffn", "trace", [D, 2, GW])
        carry = sb("ffn", "carry", [D, 2])
        keep = sb("ffn", "keep", [D, GROUPS])
        back = sb("ffn", "back", [D, 2, GW])
        retr = sb("ffn", "retr", [D, GW])

        x_chunk = x.rearrange("b (n i) d -> b n i d", i=C)
        x_tile = x.rearrange("b (t p) d -> p (b t) d", p=P)
        out_tile = out.rearrange("b (t p) d -> p (b t) d", p=P)

        def diagonal(tensor, shift, rows):
            return bass.AP(tensor, shift * H * C, [[C * H * C, NC], [H * C + 1, rows], [C, H]])

        def over_pair(operand):
            return operand.unsqueeze(2).to_broadcast([P, CPT, 2, DH])

        def over_width(scale, n):
            return scale.unsqueeze(3).to_broadcast([P, n, H, DH])

        mask = pair_mask[:, :, :].unsqueeze(1).to_broadcast([P, CPT, 2, DH])

        ORDER = ("v", "kb", "kd", "r", "p", "t")
        UNITS = 4 * len(ORDER)
        VECTOR_FROM = 4 * ORDER.index("t")
        L2_BANK = (6, 7)

        def l2_source(kind, i):
            if kind in ("p", "t"):
                return {"p": att, "t": tri}[kind][:, i, :, :].rearrange("p h j -> p (h j)")
            return {"v": cb, "kb": ca, "kd": cb, "r": ca}[kind][:, i, :]

        def l2_dest(unit):
            b, kind, q = unit // UNITS, ORDER[unit % UNITS // 4], unit % 4
            dest = {"v": vk[:, b, :, 0, :], "kb": vk[:, b, :, 1, :], "p": pk[:, b, :, 0, :], "kd": pk[:, b, :, 1, :],
                    "t": tt[:, b, :, :], "r": rq[:, b, :, :]}[kind]
            return dest.rearrange("p n x -> p x n")[:, 4 * q:4 * q + 4, :]

        def l2_bank(unit):
            return bank[L2_BANK[unit % 2]][:, :].rearrange("p (x n) -> p x n", x=4)

        EARLY_ROUNDS = range(NT + 1)
        EARLY_SPLIT = 4

        def early_tile(r):
            return slice(r * CPT, (r + 1) * CPT)

        n_w1, n_w2 = E * FC * 2 // 4, E * FC // 4
        W_GROUPS = [(w1n, w1t, 4 * g) for g in range(n_w1)] + [(w2n, w2t, 4 * g) for g in range(n_w2)]
        W_BANK = (5, 4)

        def unit_after(t, b, ahead):
            return t + (b + ahead) // B, (b + ahead) % B

        def exists(t):
            return not isinstance(t, int) or 0 <= t < NT

        def run_slots(engine, slot):
            for t in (-2, -1, 0):
                for b in range(B):
                    slot(t, b)
            with engine.Fori(1, NT - 2) as t:
                for b in range(B):
                    slot(t, b)
            for t in (NT - 2, NT - 1, NT):
                for b in range(B):
                    slot(t, b)

        SPLIT_AT = ((0, 0), (0, 1), (NT - 2, 1), (NT - 1, 0))

        def quarter_of_w1(t, b):
            size = E * FC * 2 // len(SPLIT_AT)
            at = SPLIT_AT.index((t, b))
            return slice(at * size, (at + 1) * size)

        def unrolled_slots(slot):
            for t in range(-2, NT + 1):
                for b in range(B):
                    slot(t, b)

        QUARTERS = 4

        def quarter_positions(quarter):
            return slice(quarter * T // QUARTERS, (quarter + 1) * T // QUARTERS)

        ANGLE_STEPS = 11
        UP = E * FC
        ALL = 2 * GROUPS

        def group_pair(g, group):
            for i in range(2):
                rotor = not isinstance(g, int) or 1 <= g + i <= GROUPS
                group(g + i, i, rotor, g + i == ALL - 1 if isinstance(g, int) else False)

        def all_groups(engine, first, group):
            first()
            group_pair(0, group)
            with engine.Fori(1, GROUPS // 2) as pair:
                group_pair(pair * 2, group)
            group_pair(GROUPS, group)
            with engine.Fori(GROUPS // 2 + 1, GROUPS - 1) as pair:
                for i in range(2):
                    group(pair * 2 + i, i, False, False)
            group_pair(ALL - 2, group)

        def rotor_k(g):
            return 2 * g + 1

        def next_k(g, rotor):
            return 2 * g + 2 if rotor or isinstance(g, int) and g == 0 else g + GROUPS + 2

        def positive(count):
            return max(count, 1) if isinstance(count, int) else count

        def tile_of(g):
            return (g % GROUPS) * GT

        block = ctx.enter_context(nc.Block())

        @block.sync
        def _(sp):
            for b in range(B):
                sp.dma_start(xc[b][:, 1:C + 1, :], x_chunk[b]).then_inc(sem(f"x_loaded{b}"), 16)
                sp.dma_start(xc[b][1:NC, 0, :], x_chunk[b, 0:NC - 1, C - 1, :]).then_inc(sem(f"x_loaded{b}"), 16)
                if b == 0:
                    sp.wait_ge(sem("x_loaded0"), 2 * 16)
            sp.dma_start(xres[:, :, :], x_tile).then_inc(sem("xres_loaded"), 16)
            sp.dma_start(b1_col[:, :, :, :].rearrange("p e c k -> p (e c) k"),
                         b1.rearrange("e (c p k) -> p (e c) k", c=FC, k=2)).then_inc(sem("small_loaded"), 16)
            sp.dma_start(b2_rows[:, :], b2).then_inc(sem("small_loaded"), 16)
            sp.dma_start(gate_sb[:, :], gate_w).then_inc(sem("small_loaded"), 16)
            sp.dma_start(freq_col[:, :], freqs.rearrange("(d a) -> d a", a=1)).then_inc(sem("small_loaded"), 16)
            sp.wait_ge(sem("l2_even"), B * UNITS // 2)
            sp.wait_ge(sem("l2_odd"), B * UNITS // 2)

            sp.wait_ge(sem("early_uw"), NT)
            sp.wait_ge(sem("early_qm"), 2 * NT)

            def slot(t, b):
                (t1, b1), t2, t3, t4 = unit_after(t, b, 1), *(unit_after(t, b, ahead)[0] for ahead in (2, 3, 4))
                if exists(t1):
                    sp.wait_ge(sem(f"state_mm{b1}"), t1 * CPT + 1)
                    sp.dma_start(p_tile[b1][:, :, :, :], pk[:, b1, bass.ds(t1 * CPT, CPT), :, :]).then_inc(sem(f"p_tile{b1}"), 16)
                if exists(t2) and not b:
                    sp.wait_ge(sem("ex_u0"), t2 + 1)
                    sp.wait_ge(sem("step0"), t2 + 1)
                    sp.dma_start(vk_tile[0][:, :, :, :], vk[:, 0, bass.ds(t2 * CPT, CPT), :, :]).then_inc(sem("vk_tile0"), 16)
                if exists(t4) and b:
                    sp.wait_ge(sem("uw_mm1"), t4 + 1)
                    sp.dma_start(vk_tile[1][:, :, :, :], vk[:, 1, bass.ds(t4 * CPT, CPT), :, :]).then_inc(sem("vk_tile1"), 16)
                if exists(t3) and not b:
                    sp.wait_ge(sem("qm_mm1"), t3 + 1)
                    sp.dma_start(pk_tile[1][:, :, :, :], pk[:, 1, bass.ds(t3 * CPT, CPT), :, :]).then_inc(sem("pk_tile1"), 16)

            unrolled_slots(slot)
            with sp.Fori(0, GROUPS) as g:
                sp.wait_ge(sem("added"), g * E + (GROUPS + 1) * E + 1)
                sp.dma_start(out_tile[:, bass.ds(g * GT, GT), :],
                             xres[:, bass.ds(g * GT, GT), :]).then_inc(sem("stored"), 16)
            sp.wait_ge(sem("stored"), 16 * GROUPS)

        @block.gpsimd
        def _(pool):
            for name in ("retr", "ex_u0", "ex_u1"):
                pool.sem_inc(sem(name), 1)
            pool.memset(ident[:, :], 0.0).then_inc(sem("ident_zero"), 1)
            pool.memset(head_mask[:, :, :], 1.0).then_inc(sem("mask_one"), 1)
            for b in range(B):
                pool.memset(xc[b][0:1, 0, :], 0.0).then_inc(sem("pad_zero"), 1)
            pool.wait_ge(sem("ident_zero"), 1)
            pool.affine_select(out=ident[:, :], in_=ident[:, :], compare_op=ALU.not_equal, fill=1.0,
                               base=0, pattern=[[-1, P]], channel_multiplier=1).then_inc(sem("ident"), 1)
            pool.wait_ge(sem("mask_one"), 1)
            pool.affine_select(out=head_mask[:, :, :], in_=head_mask[:, :, :], compare_op=ALU.is_ge, fill=0.0,
                               base=0, pattern=[[-DH, H], [0, DH]], channel_multiplier=1).then_inc(sem("mask_low"), 1)
            pool.wait_ge(sem("mask_low"), 1)
            pool.affine_select(out=head_mask[:, :, :], in_=head_mask[:, :, :], compare_op=ALU.is_ge, fill=0.0,
                               base=DH - 1, pattern=[[DH, H], [0, DH]], channel_multiplier=-1).then_inc(sem("head_mask"), 1)
            pool.iota(steps[:, 0:C + 1], pattern=[[1, C + 1]], base=0, channel_multiplier=0).then_inc(sem("iotas"), 1)
            pool.iota(steps[:, C + 1:2 * C + 1], pattern=[[-1, C]], base=C - 1, channel_multiplier=0).then_inc(sem("iotas"), 1)
            pool.iota(iota8_i[:, :], pattern=[[1, E]], base=0, channel_multiplier=0).then_inc(sem("iotas"), 1)
            pool.memset(half[:, :], -0.5).then_inc(sem("half"), 1)

            def early_round(r):
                if r < NT:
                    if r >= 2:
                        pool.wait_ge(sem("early_uw_mm"), r - 1)
                    pool.tensor_tensor(early_t[r % 2][:, :, :, :], over_pair(tt[:, 0, early_tile(r), :]), mask,
                                       ALU.mult).then_inc(sem("early_t"), 1)
                if r >= 1:
                    pool.wait_ge(sem("early_uw"), r)
                    if r >= 3:
                        pool.wait_ge(sem("early_qm_mm"), r - 2)
                    pool.tensor_tensor(early_w[(r - 1) % 2][:, :, :, :], over_pair(vk[:, 0, early_tile(r - 1), 1, :]), mask,
                                       ALU.mult).then_inc(sem("early_w"), 1)

            for b in range(B):
                if b:
                    pool.wait_ge(sem("l2_mm"), UNITS)
                pool.memset(att[:, :, :, :], 0.0).then_inc(sem("blocks_zero"), 1)
                pool.memset(tri[:, :, :, :], 0.0).then_inc(sem("blocks_zero"), 1)
                pool.wait_ge(sem("blocks_zero"), 2 * (b + 1))
                pool.memset(diagonal(tri, 0, C), 1.0).then_inc(sem("tri_one"), 1)
                if b:
                    pool.wait_ge(sem("l2_even"), UNITS // 2)
                    pool.wait_ge(sem("l2_odd"), UNITS // 2)
                    pool.wait_ge(sem("row_added"), C - 2)
                    for r in EARLY_ROUNDS[:EARLY_SPLIT]:
                        early_round(r)
                pool.wait_ge(sem("neg_power"), 1)
                pool.wait_ge(sem("beta"), b + 1)
                if b:
                    early_round(EARLY_SPLIT)
                for delta in range(1, C + 1):
                    rows = C + 1 - delta
                    g = diag[:, delta % 2, :, :]
                    pool.wait_ge(sem("diag"), C * b + delta)
                    if delta < C:
                        low = rows - 1
                        if delta > 1:
                            pool.wait_ge(sem("tri_diag"), (C - 1) * b + delta - 1)
                        pool.tensor_tensor(diag_n[:, 0:low, :], g[:, 0:low, :],
                                           neg_power[:, delta:delta + 1, :].to_broadcast([NC, low, H]),
                                           ALU.mult).then_inc(sem("diag_n"), 1)
                        pool.wait_ge(sem("diag_n"), (C - 1) * b + delta)
                        pool.tensor_tensor(diagonal(tri, delta, low), diag_n[:, 0:low, :], beta[:, delta:C, :],
                                           ALU.mult).then_inc(sem("tri_diag"), 1)
                    pool.tensor_tensor(diagonal(att, delta - 1, rows), g[:, 0:rows, :],
                                       power[:, delta - 1:delta, :].to_broadcast([NC, rows, H]),
                                       ALU.mult).then_inc(sem("diag_used"), 1)
                    if b and EARLY_SPLIT + delta in EARLY_ROUNDS:
                        early_round(EARLY_SPLIT + delta)

            pool.wait_ge(sem("ln_var"), 1)
            pool.tensor_tensor(rstd[:, :], var[:, :], half[:, :], ALU.pow).then_inc(sem("ln_rstd"), 1)


            def angle_steps(first_count, end):
                for count in range(first_count, end):
                    angle_step(count)

            def angle_step(count):
                part, at = quarter_positions(2 + count // ANGLE_STEPS), count % ANGLE_STEPS
                a, turns, sine, cosine = ang[:, part], turn[:, part], sin_t[:, part], cos_t[:, part]
                if count == 0:
                    pool.wait_ge(sem("positions"), 1)
                else:
                    pool.wait_ge(sem("angle_step"), count)
                if at == 0:
                    step = pool.tensor_copy(a, position[:, part])
                elif at == 1:
                    step = pool.tensor_scalar(a, a, freq_col[:, :], None, ALU.mult)
                elif at == 2:
                    step = pool.tensor_scalar(turns, a, 1 / TWO_PI, MAGIC, ALU.mult, ALU.add)
                elif at == 3:
                    step = pool.tensor_scalar(turns, turns, MAGIC, None, ALU.subtract)
                elif at in (4, 6, 8):
                    step = pool.tensor_scalar(cosine, turns, -(PI_A, PI_B, PI_C)[at // 2 - 2], None, ALU.mult)
                elif at in (5, 7, 9):
                    step = pool.tensor_tensor(a, a, cosine, ALU.add)
                else:
                    step = pool.tensor_scalar(sine, a, PI_LOW, -PI_LOW, ALU.min, ALU.max)
                step.then_inc(sem("angle_step"), 1)

            pool.wait_ge(sem("l2_even"), B * UNITS // 2)
            pool.wait_ge(sem("l2_odd"), B * UNITS // 2)

            def slot(t, b):
                (t1, b1), t2, t4 = unit_after(t, b, 1), *(unit_after(t, b, ahead)[0] for ahead in (2, 4))
                if exists(t2) and b:
                    pool.wait_ge(sem("uw1"), t2 + 2)
                    pool.wait_ge(sem("qm_mm1"), t2 + 1)
                    pool.tensor_tensor(ex[1]["w"][:, :, :, :], over_pair(uw[1][:, :, 1, :]), mask, ALU.mult).then_inc(sem("ex_w1"), 1)
                if exists(t1):
                    if b1:
                        u_part = uw[1][:, :, 0, :]
                    else:
                        u_part = vk_tile[0][:, :, 0, :]
                        pool.wait_ge(sem("vk_tile0"), 16 * (t1 + 1))
                    pool.wait_ge(sem(f"state_mm{b1}"), t1 * CPT + 1)
                    pool.tensor_tensor(ex[b1]["u"][:, :, :, :], over_pair(u_part), mask, ALU.mult).then_inc(sem(f"ex_u{b1}"), 1)
                if exists(t4) and b:
                    pool.wait_ge(sem("uw_mm1"), t4 + 1)
                    pool.tensor_tensor(ex[1]["t"][:, :, :, :], over_pair(tt[:, 1, bass.ds(t4 * CPT, CPT), :]), mask,
                                       ALU.mult).then_inc(sem("ex_t1"), 1)
                if isinstance(t, int) and (t, b) in SPLIT_AT:
                    part = quarter_of_w1(t, b)
                    pool.wait_ge(sem("w1_hi"), SPLIT_AT.index((t, b)) + 1)
                    pool.tensor_tensor(w1_lo[:, part, :], w1t[:, part, :], w1_hi[:, part, :].bitcast(F32),
                                       ALU.subtract).then_inc(sem("w1_lo"), 1)
                if isinstance(t, int) and (t, b) == (NT - 2, 0):
                    for side in range(B):
                        pool.wait_ge(sem(f"vk_tile{side}"), 16 * NT)
                    pool.iota(position[:, :], pattern=[[1, T]], base=0, channel_multiplier=0).then_inc(sem("positions"), 1)

            run_slots(pool, slot)

            def inverse_deviation(k):
                pool.wait_ge(sem("ln_var"), k + 1)
                pool.tensor_tensor(rstd[:, 0:GT], var[:, 0:GT], half[:, 0:GT], ALU.pow).then_inc(sem("ln_rstd"), 1)

            def exponential(g):
                pool.wait_ge(sem("gap"), g + 1)
                pool.tensor_tensor(odds[:, :], euler[:, :], gap[:, :], ALU.pow).then_inc(sem("odds"), 1)

            def first():
                pool.memset(euler[:, :], math.e).then_inc(sem("half"), 1)
                pool.wait_ge(sem("half"), 2)
                inverse_deviation(1)
                exponential(0)

            def group(g, i, rotor, last):
                if rotor:
                    inverse_deviation(rotor_k(g))
                if isinstance(g, int) and g == 0:
                    angle_steps(0, 4)
                if not last:
                    inverse_deviation(next_k(g, rotor))
                if isinstance(g, int) and g < 2:
                    angle_steps(*((4, 12), (17, 20))[g])
                if rotor:
                    for k, table in enumerate((cos_t, sin_t)):
                        pool.wait_ge(sem(f"trace{k}"), g)
                        pool.wait_ge(sem("retr"), g)
                        pool.tensor_tensor(back[:, k, :], trace[:, k, :], table[:, bass.ds((g - 1) % (GROUPS // B) * GW, GW)],
                                           ALU.mult).then_inc(sem("back"), 1)
                    pool.wait_ge(sem("back"), 2 * g)
                    pool.wait_ge(sem("bt_y_mm"), g)
                    pool.tensor_tensor(retr[:, :], back[:, 0, :], back[:, 1, :], ALU.add).then_inc(sem("retr"), 1)
                if isinstance(g, int) and g == 1:
                    angle_steps(20, 21)
                if not last:
                    exponential(g + 1)
                if isinstance(g, int) and g < 2:
                    angle_steps(*((12, 17), (21, 2 * ANGLE_STEPS))[g])

            all_groups(pool, first, group)

        @block.scalar
        def _(act):
            for name in ("v", "s", "wtr", "uw1", "o_part0", "o_part1"):
                act.sem_inc(sem(name), 1)
            act.dma_start(decay_rows[:, :], decay.rearrange("(a h) -> a h", a=1).to_broadcast([P, H])).then_inc(sem("decay_loaded"), 16)
            for i, w in enumerate((w_write, w_read, w_v, w_o)):
                act.dma_start(wn[:, i, :], w).then_inc(sem("wn_loaded"), 16)
            act.dma_start(wbn[:, :], w_beta).then_inc(sem("wn_loaded"), 16)
            act.wait_ge(sem("decay_floor"), 1)
            act.activation(soft[:, :], soft[:, :], ACT.Exp, scale=-1.0).then_inc(sem("exp_decay"), 1)
            act.wait_ge(sem("exp_decay1"), 1)
            act.activation(soft[:, :], soft[:, :], ACT.Ln).then_inc(sem("log"), 1)
            act.wait_ge(sem("power_arg"), 1)
            act.activation(power[:, :, :], power[:, :, :], ACT.Exp, scale=-1.0).then_inc(sem("power"), 1)
            act.wait_ge(sem("soft_col"), 1)
            act.activation(gamma_col[:, :], soft_col[:, 0:1], ACT.Exp, scale=-float(C)).then_inc(sem("gamma_col"), 1)

            act.wait_ge(sem("x_loaded0"), 2 * 16)
            act.dma_start(w1n[:, :, :].rearrange("p (m k) d -> p m (k d)", k=2),
                          w1.rearrange("e (c p k) d -> p (e c) (k d)", c=FC, k=2)).then_inc(sem("w1_loaded"), 16)
            act.dma_start(w2n[:, :, :].rearrange("d (e c) p -> d e (c p)", c=FC),
                          w2.rearrange("e d f -> d e f")).then_inc(sem("w2_loaded"), 16)

            act.wait_ge(sem("wsmall_mm"), 1)
            act.activation(wsmall[:, :, :].rearrange("p i d -> p (i d)"), bank[5][:, :], ACT.Copy).then_inc(sem("w_evac"), 1)
            act.wait_ge(sem("wbeta_mm"), 1)
            act.activation(w_beta_t[:, :], bank[4][:, 0:H], ACT.Copy).then_inc(sem("wbeta"), 1)

            def early_round(r):
                if r < NT:
                    act.wait_ge(sem("early_uw_mm"), r + 1)
                    act.activation(vk[:, 0, early_tile(r), :, :].rearrange("p n k d -> p (n k d)"), bank[r % 2][:, 0:CPT * 2 * DH],
                                   ACT.Copy).then_inc(sem("early_uw"), 1)
                if r >= 1:
                    qm = bank[2 + (r - 1) % 2][:, 0:CPT * 2 * DH].rearrange("p (n k d) -> p n k d", n=CPT, k=2)
                    act.wait_ge(sem("early_qm_mm"), r)
                    act.activation(tt[:, 0, early_tile(r - 1), :], qm[:, :, 0, :], ACT.Copy).then_inc(sem("early_qm"), 1)
                    act.activation(vk[:, 0, early_tile(r - 1), 1, :], qm[:, :, 1, :], ACT.Copy).then_inc(sem("early_qm"), 1)

            for b in range(B):
                act.wait_ge(sem("centred"), b + 1)
                act.activation(sq[:, :, :], xc[b][:, :, :], ACT.Square).then_inc(sem("sq"), 1)
                if b:
                    early_round(0)
                act.wait_ge(sem("chunk_var"), b + 1)
                act.activation(s17[:, :], s17[:, :], ACT.Sqrt).then_inc(sem("chunk_std"), 1)
                if b:
                    early_round(1)
                act.wait_ge(sem("normed"), b + 1)
                act.activation(sq[:, :, :], xc[b][:, :, :], ACT.Square).then_inc(sem("sq"), 1)
                if b:
                    early_round(2)
                act.wait_ge(sem("head_sq"), b + 1)
                act.activation(s136[:, :, :], s136[:, :, :], ACT.Sqrt).then_inc(sem("head_norm"), 1)
                if b:
                    for r in EARLY_ROUNDS[3:EARLY_SPLIT]:
                        early_round(r)
                for q in range(4):
                    act.wait_ge(sem("hx_mm"), 4 * b + q + 1)
                    act.activation(ca[:, 4 * q:4 * q + 4, :].rearrange("p i n -> p (i n)"), bank[q][:, :],
                                   ACT.Copy).then_inc(sem("hx"), 1)
                act.wait_ge(sem("beta_mm"), b + 1)
                act.activation(beta[:, :, :].rearrange("p i h -> p (i h)"), bank[4][:, 0:C * H],
                               ACT.Sigmoid).then_inc(sem("beta"), 1)
                for unit in range(UNITS * b, UNITS * (b + 1)):
                    if unit % 2 and unit % UNITS >= VECTOR_FROM:
                        continue
                    if unit == 4 * ORDER.index("r"):
                        for g, (_, dest, at) in enumerate(W_GROUPS):
                            act.wait_ge(sem("w_mm"), g + 1)
                            act.activation(dest[:, at:at + 4, :].rearrange("p m d -> p (m d)"), bank[W_BANK[g % 2]][:, :],
                                           ACT.Copy).then_inc(sem("w_evac"), 1)
                    if unit == UNITS + 4 * ORDER.index("p"):
                        for r in EARLY_ROUNDS[EARLY_SPLIT:]:
                            early_round(r)
                    act.wait_ge(sem("l2_mm"), unit + 1)
                    act.activation(l2_dest(unit), l2_bank(unit), ACT.Copy).then_inc(sem("l2_odd" if unit % 2 else "l2_even"), 1)


            def slot(t, b):
                t3 = unit_after(t, b, 3)[0]
                for n in range(CPT):
                    if exists(t):
                        if n == 0:
                            act.wait_ge(sem(f"y_mm{b}"), t + 1)
                        act.wait_ge(sem(f"wide{b}"), t * CPT + n + 1)
                        act.activation(ot[b][:, n * C:(n + 1) * C], bank[4 + n % 2][:, n // 2 * 32:n // 2 * 32 + C],
                                       ACT.Copy).then_inc(sem(f"o_part{b}"), 1)
                    if n == 6 and isinstance(t, int) and (t, b) in SPLIT_AT:
                        part = quarter_of_w1(t, b)
                        act.activation(w1_hi[:, part, :], w1t[:, part, :], ACT.Copy).then_inc(sem("w1_hi"), 1)
                    if n == CPT - 1 and exists(t3) and not b:
                        act.wait_ge(sem("uw_mm1"), t3 + 2)
                        act.wait_ge(sem("ex_u1"), t3 + 1)
                        act.activation(uw[1][:, :, :, :].rearrange("p n k d -> p (n k d)"), bank[1][:, 0:CPT * 2 * DH],
                                       ACT.Copy).then_inc(sem("uw1"), 1)

            run_slots(act, slot)
            def columns(k, i):
                act.wait_ge(sem("ht_mm"), k)
                act.activation(ht_hi[i][:, :], bank[0][:, :], ACT.Copy).then_inc(sem("ht_hi"), 1)
                act.activation(ht[i][:, :], bank[0][:, :], ACT.Copy).then_inc(sem("ht"), 1)

            def first_rotors():
                act.wait_ge(sem("half_pi"), 1)
                act.wait_ge(sem("angles"), 2)
                rotors(slice(0, T // 2), 1)

            def later_rotors(quarter):
                act.wait_ge(sem("angle_step"), (quarter - 1) * ANGLE_STEPS)
                rotors(quarter_positions(quarter), quarter)

            def rotors(part, count):
                act.activation(cos_t[:, part], sin_t[:, part], ACT.Abs).then_inc(sem("angle_size"), 1)
                act.wait_ge(sem("angle_size"), count)
                act.activation(sin_t[:, part], sin_t[:, part], ACT.Sin).then_inc(sem("trig"), 1)
                act.activation(cos_t[:, part], cos_t[:, part], ACT.Sin, scale=-1.0, bias=half_pi[:, 0:1]).then_inc(sem("trig"), 1)

            def first():
                columns(1, 0)
                first_rotors()

            def group(g, i, rotor, last):
                for n in range(UP):
                    e, c, k = n // FC, n % FC, n % 2
                    if n == 1:
                        act.wait_ge(sem("wt_mm"), g + 1)
                        act.activation(wtr[:, :], bank[1][0:E, :], ACT.Copy).then_inc(sem("wtr"), 1)
                    if n == 7 and rotor:
                        act.wait_ge(sem("ht_mm"), rotor_k(g))
                        act.activation(htr[:, :], bank[0][:, :], ACT.Copy).then_inc(sem("ht"), 1)
                    if n == 11 and not last:
                        columns(next_k(g, rotor), 1 - i)
                    act.wait_ge(sem("up"), g * UP + n + 1)
                    act.wait_ge(sem("h"), positive(g * UP + n))
                    act.activation(vact[k][:, :], bank[4 + k][:, :], ACT.Identity,
                                   bias=b1v_col[:, e, c:c + 1]).then_inc(sem("v"), 1)
                    act.activation(gs[k][:, :], bank[2 + k][:, :], ACT.Gelu_apprx_sigmoid,
                                   bias=b1_col[:, e, c, 0:1]).then_inc(sem("s"), 1)
                    if isinstance(g, int) and g == 1 and n in (5, UP - 1):
                        later_rotors(2 if n == 5 else 3)

            all_groups(act, first, group)

        @block.tensor
        def _(pe):
            for name in ("down", "bt_y_mm", "uw_mm1", "qm_mm1", "state_mm0", "state_mm1", "y_mm0", "y_mm1"):
                pe.sem_inc(sem(name), 1)
            pe.wait_ge(sem("ident"), 1)
            pe.wait_ge(sem("wn_loaded"), 5 * 16)
            for i in range(4):
                mm = pe.transpose(bank[5][:, i * P:(i + 1) * P], wn[:, i, :], ident[:, :])
            mm.then_inc(sem("wsmall_mm"), 1)
            pe.transpose(bank[4][:, 0:H], wbn[:, :], ident[0:H, 0:H]).then_inc(sem("wbeta_mm"), 1)
            pe.wait_ge(sem("w_evac"), 1)
            pe.wait_ge(sem("wbeta"), 1)

            UW_UP_TO = (0, 1, 2, 2, 3, 4, 5, 7, 8)
            QM_UP_TO = (0, 0, 1, 2, 3, 5, 6, 8, 8)
            PAIRS = [slice(q * 2 * DH, (q + 1) * 2 * DH) for q in range(H // 2)]

            def product(dest, stationary, moving, start=True, stop=True):
                for q in PAIRS:
                    mm = pe.matmul(dest[q, :], stationary[q, :, :].rearrange("p k d -> p (k d)"), moving[q, :], start=start, stop=stop)
                return mm

            def early_round(r):
                if r < NT:
                    pe.wait_ge(sem("early_t"), r + 1)
                    if r >= 2:
                        pe.wait_ge(sem("early_uw"), r - 1)
                    for n in range(CPT):
                        mm = product(bank[r % 2][:, n * 32:n * 32 + 32], early_t[r % 2][:, n, :, :],
                                     vk[:, 0, r * CPT + n, :, :].rearrange("p k d -> p (k d)"))
                    mm.then_inc(sem("early_uw_mm"), 1)
                if r >= 1:
                    pe.wait_ge(sem("early_w"), r)
                    if r >= 3:
                        pe.wait_ge(sem("early_qm"), 2 * (r - 2))
                    for n in range(CPT):
                        mm = product(bank[2 + (r - 1) % 2][:, n * 32:n * 32 + 32], early_w[(r - 1) % 2][:, n, :, :],
                                     pk[:, 0, (r - 1) * CPT + n, :, :].rearrange("p k d -> p (k d)"))
                    mm.then_inc(sem("early_qm_mm"), 1)

            for b in range(B):
                if b:
                    pe.wait_ge(sem("v_src"), 4)
                    for r in EARLY_ROUNDS[:EARLY_SPLIT]:
                        early_round(r)
                    pe.wait_ge(sem("early_uw"), EARLY_SPLIT)
                    pe.wait_ge(sem("early_qm"), 2 * (EARLY_SPLIT - 1))
                pe.wait_ge(sem("normed"), b + 1)
                for q in range(4):
                    if b:
                        pe.wait_ge(sem("v_src"), 4 * b)
                    for i in range(4 * q, 4 * q + 4):
                        mm = pe.transpose(bank[q][:, i % 4 * P:(i % 4 + 1) * P], xc[b][:, i + 1, :], ident[:, :])
                    mm.then_inc(sem("hx_mm"), 1)
                for q in range(4):
                    pe.wait_ge(sem("hx"), 4 * b + q + 1)
                    for i in range(4 * q, 4 * q + 4):
                        mm = pe.matmul(bank[q][:, i % 4 * P:(i % 4 + 1) * P], ca[:, i, :], w_write_t, start=True, stop=True)
                    mm.then_inc(sem("v_mm"), 1)
                for i in range(C):
                    mm = pe.matmul(bank[4][:, i * H:(i + 1) * H], ca[:, i, :], w_beta_t[:, :], start=True, stop=True)
                mm.then_inc(sem("beta_mm"), 1)
                for unit in range(UNITS * b, UNITS * (b + 1)):
                    kind, q = ORDER[unit % UNITS // 4], unit % 4
                    if unit == 4 * ORDER.index("r"):
                        pe.wait_ge(sem("w1_loaded"), 16)
                        pe.wait_ge(sem("w2_loaded"), 16)
                        for g, (src, _, at) in enumerate(W_GROUPS):
                            if g == 1:
                                pe.wait_ge(sem("beta"), 1)
                            if g >= 2:
                                pe.wait_ge(sem("w_evac"), g)
                            for m in range(4):
                                mm = pe.transpose(bank[W_BANK[g % 2]][:, m * P:(m + 1) * P], src[:, at + m, :], ident[:, :])
                            mm.then_inc(sem("w_mm"), 1)
                    if unit == UNITS + 4 * ORDER.index("p"):
                        for r in EARLY_ROUNDS[EARLY_SPLIT:]:
                            early_round(r)
                    if kind == "v":
                        pe.wait_ge(sem("v_src"), 4 * (b + 1))
                    elif kind == "p":
                        pe.wait_ge(sem("diag_used"), C * (b + 1))
                    elif kind == "t":
                        pe.wait_ge(sem("row_added"), (C - 2) * (b + 1))
                    else:
                        pe.wait_ge(sem(f"{kind}_src"), b + 1)
                    if unit >= 2:
                        pe.wait_ge(sem("l2_odd" if unit % 2 else "l2_even"), unit // 2)
                    for i in range(4 * q, 4 * q + 4):
                        mm = pe.transpose(bank[L2_BANK[unit % 2]][:, i % 4 * P:(i % 4 + 1) * P], l2_source(kind, i), ident[:, :])
                    mm.then_inc(sem("l2_mm"), 1)

            pe.wait_ge(sem("l2_even"), B * UNITS // 2)
            pe.wait_ge(sem("l2_odd"), B * UNITS // 2)
            pe.wait_ge(sem("early_qm"), 2 * NT)

            def uw_products(t, b, lo, hi):
                if lo == 0 and hi:
                    pe.wait_ge(sem(f"ex_t{b}"), t + 1)
                    pe.wait_ge(sem(f"vk_tile{b}"), 16 * (t + 1))
                    pe.wait_ge(sem(f"uw{b}"), t + 1)
                for n in range(lo, hi):
                    mm = product(bank[b][:, n * 32:n * 32 + 32], ex[b]["t"][:, n, :, :],
                                 vk_tile[b][:, n, :, :].rearrange("p k d -> p (k d)"))
                if lo < hi == CPT:
                    mm.then_inc(sem(f"uw_mm{b}"), 1)

            def qm_products(t, b, lo, hi):
                if lo == 0 and hi:
                    pe.wait_ge(sem(f"ex_w{b}"), t + 1)
                    pe.wait_ge(sem(f"pk_tile{b}"), 16 * (t + 1))
                    pe.wait_ge(sem(f"step{b}"), t + 1)
                for n in range(lo, hi):
                    mm = product(bank[2 + b][:, n * 32:n * 32 + 32], ex[b]["w"][:, n, :, :],
                                 pk_tile[b][:, n, :, :].rearrange("p k d -> p (k d)"))
                if lo < hi == CPT:
                    mm.then_inc(sem(f"qm_mm{b}"), 1)

            def chunk_step(t, b, n):
                dest = bank[4 + n % 2][:, n // 2 * 32:n // 2 * 32 + 32]
                if n == 0:
                    pe.wait_ge(sem(f"ex_u{b}"), t + 2)
                    pe.wait_ge(sem(f"p_tile{b}"), 16 * (t + 1))
                if n >= 2:
                    pe.wait_ge(sem(f"o_part{b}"), t * CPT + n)
                else:
                    pe.wait_ge(sem(f"o_part{1 - b}"), positive((t + b) * CPT + n))
                product(dest, ex[b]["u"][:, n, :, :], p_tile[b][:, n, :, :].rearrange("p k d -> p (k d)"), stop=False)
                if n == 0:
                    pe.wait_ge(sem(f"step{b}"), t + 2)
                pe.wait_ge(sem(f"state{b}"), t * CPT + n + 1)
                product(dest, state[b][:, n, :, :], step[b][:, n, :, :].rearrange("p k d -> p (k d)"),
                        start=False).then_inc(sem(f"state_mm{b}"), 1)

            def slot(t, b):
                (t1, b1), (tb, bb) = unit_after(t, b, 1), unit_after(t, b, -1)
                t2, t3 = (unit_after(t, b, ahead)[0] for ahead in (2, 3))
                for n in range(CPT):
                    if exists(t):
                        chunk_step(t, b, n)
                    if exists(t3) and not b:
                        uw_products(t3, 1, UW_UP_TO[n], UW_UP_TO[n + 1])
                    if exists(t2) and b:
                        qm_products(t2, 1, QM_UP_TO[n], QM_UP_TO[n + 1])
                    if n == 2 and exists(tb):
                        pe.wait_ge(sem(f"o_part{bb}"), (tb + 1) * CPT + 1)
                        pe.wait_ge(sem(f"x1_{bb}"), tb + 1)
                        pe.matmul(bank[6 + bb][:, 0:P], ot[bb][:, :], w_read_t, start=True, stop=True).then_inc(sem(f"y_mm{bb}"), 1)

            unrolled_slots(slot)

            def rows_to_columns(k, rows):
                pe.wait_ge(sem("ln_rows"), k)
                for q in range(GT):
                    mm = pe.transpose(bank[0][:, q * P:(q + 1) * P], rows[:, q, :], ident[:, :])
                mm.then_inc(sem("ht_mm"), 1)

            def gates_of(g, i, k, rotor):
                pe.wait_ge(sem("ht"), k)
                pe.wait_ge(sem("wtr"), g + 1)
                if rotor:
                    pe.wait_ge(sem("rotated"), 2 * g - 1)
                for q in range(GT):
                    mm = pe.matmul(bank[1][:, q * E:(q + 1) * E], ht[i][:, q * P:(q + 1) * P], gate_sb[:, :], start=True, stop=True)
                mm.then_inc(sem("gate_mm"), 1)

            def up(g, i, n):
                pe.wait_ge(sem("v"), positive(g * UP + n))
                pe.wait_ge(sem("s"), positive(g * UP + n))
                for at, dest in ((2 * n, bank[2 + n % 2]), (2 * n + 1, bank[4 + n % 2])):
                    pe.matmul(dest[:, :], w1_hi[:, at, :], ht_hi[i][:, :], start=True, stop=False)
                    pe.matmul(dest[:, :], w1_hi[:, at, :], ht_lo[i][:, :], start=False, stop=False)
                    mm = pe.matmul(dest[:, :], w1_lo[:, at, :], ht_hi[i][:, :], start=False, stop=True)
                mm.then_inc(sem("up"), 1)

            def down(g, e):
                pe.wait_ge(sem("h"), g * UP + FC * (e + 1) + 1)
                pe.wait_ge(sem("added"), positive(g * E + e))
                for q in range(GT):
                    for c in range(FC):
                        mm = pe.matmul(bank[6 + e % 2][:, q * D:(q + 1) * D], hmid[e % 2][c][:, q * P:(q + 1) * P],
                                       w2t[:, FC * e + c, :], start=(c == 0), stop=(c == FC - 1))
                mm.then_inc(sem("down"), 1)

            def first_units(g, i):
                pe.wait_ge(sem("ht_lo"), g + 1)
                for n in range(FC):
                    up(g, i, n)

            def first():
                rows_to_columns(1, hrow)
                gates_of(0, 0, 1, False)
                first_units(0, 0)

            def group(g, i, rotor, last):
                pe.wait_ge(sem("wrow"), g + 1)
                for q in range(GT):
                    mm = pe.transpose(bank[1][0:E, q * P:(q + 1) * P], wrow[i][:, q, :], ident[:, :])
                mm.then_inc(sem("wt_mm"), 1)
                for e in range(E):
                    if e + 1 < E:
                        for c in range(FC):
                            up(g, i, FC * (e + 1) + c)
                            if e == 0 and c == 0:
                                pe.wait_ge(sem("wtr"), g + 2)
                                if rotor or isinstance(g, int) and g == GROUPS + 1:
                                    pe.wait_ge(sem("x3"), g)
                                for q in range(GT):
                                    mm = pe.matmul(bank[0][:, q * D:(q + 1) * D], wtr[:, q * P:(q + 1) * P], b2_rows[:, :], start=True, stop=True)
                                mm.then_inc(sem("bias_mm"), 1)
                    elif not last:
                        first_units(g + 1, 1 - i)
                    if e == 2 and rotor:
                        pe.wait_ge(sem("bias_added"), g + 2)
                        rows_to_columns(rotor_k(g), hrow_r)
                    if e == 3 and rotor:
                        pe.wait_ge(sem("ht"), rotor_k(g))
                        pe.matmul(bank[1][:, :], w_v_t, htr[:, :], start=True, stop=True).then_inc(sem("bt_v_mm"), 1)
                    if e == 4 and not last:
                        pe.wait_ge(sem("bias_added"), g + 2)
                        rows_to_columns(next_k(g, rotor), hrow)
                    if e == 6 and not last:
                        gates_of(g + 1, 1 - i, next_k(g, rotor), rotor)
                    if e == E - 1 and rotor:
                        pe.wait_ge(sem("retr"), g + 1)
                        for q in range(GT):
                            mm = pe.matmul(bank[0][:, q * D:(q + 1) * D], retr[:, q * P:(q + 1) * P], w_o_t, start=True, stop=True)
                        mm.then_inc(sem("bt_y_mm"), 1)
                    down(g, e)

            all_groups(pe, first, group)

        @block.vector
        def _(dve):
            for name in ("h", "added", "rotated", "x3", "carried", "bias_added", "step0", "step1", "x1_0", "x1_1"):
                dve.sem_inc(sem(name), 1)
            linked = [0]

            def link(ins):
                linked[0] += 1
                ins.then_inc(sem("vector_link"), 1)
                dve.wait_ge(sem("vector_link"), linked[0])

            dve.wait_ge(sem("decay_loaded"), 16)
            dve.tensor_scalar(soft[:, :], decay_rows[:, :], -40.0, None, ALU.max).then_inc(sem("decay_floor"), 1)
            dve.wait_ge(sem("exp_decay"), 1)
            dve.tensor_scalar(soft[:, :], soft[:, :], 1.0, None, ALU.add).then_inc(sem("exp_decay1"), 1)
            dve.wait_ge(sem("log"), 1)
            dve.scalar_tensor_tensor(out=soft[:, :], in0=decay_rows[:, :], scalar=-1.0, in1=soft[:, :],
                                     op0=ALU.mult, op1=ALU.max).then_inc(sem("soft"), 1)
            dve.wait_ge(sem("iotas"), 3)
            link(dve.tensor_copy(steps_f[:, :], steps[:, :]))
            dve.tensor_copy(iota8[:, :], iota8_i[:, :])
            dve.wait_ge(sem("soft"), 1)
            shape = [P, 2 * C + 1, H]
            dve.tensor_tensor(power[:, :, :], steps_f[:, :].unsqueeze(2).to_broadcast(shape),
                              soft[:, :].unsqueeze(1).to_broadcast(shape), ALU.mult).then_inc(sem("power_arg"), 1)
            dve.wait_ge(sem("head_mask"), 1)
            link(dve.tensor_tensor(neg_power[:, 0, :], soft[:, :], head_mask[:, :, 0], ALU.mult))
            dve.tensor_reduce(soft_col[:, 0:1], neg_power[:, 0, :], AX, ALU.add).then_inc(sem("soft_col"), 1)
            dve.wait_ge(sem("ident"), 1)
            link(dve.tensor_reduce(pair_mask[:, :, :], head_mask[:, :, :].rearrange("p (q k) d -> p k d q", k=2), AX, ALU.add))
            link(dve.tensor_reduce(rep[:, :], ident[:, :].rearrange("p (h d) -> p d h", h=H), AX, ALU.add))
            dve.wait_ge(sem("power"), 1)
            dve.wait_ge(sem("soft_col"), 1)
            dve.tensor_scalar(neg_power[:, :, :], power[:, 0:C + 1, :], -1.0, None, ALU.mult).then_inc(sem("neg_power"), 1)
            dve.wait_ge(sem("gamma_col"), 1)
            link(dve.tensor_scalar(gamma_rep[:, :], rep[:, :], gamma_col[:, :], None, ALU.mult))

            def variance(rows, k):
                even_m, odd_m = stat[:, 0:rows, 1], stat[:, 0:rows, 4]
                dve.wait_ge(sem("ln_stat"), k + 1)
                dve.tensor_tensor(mean[:, 0:rows], even_m, odd_m, ALU.add)
                dve.tensor_tensor(sumsq[:, 0:rows], stat[:, 0:rows, 2], stat[:, 0:rows, 5], ALU.add)
                dve.tensor_tensor(dev[:, 0:rows], even_m, odd_m, ALU.subtract).then_inc(sem("ln_dev"), 1)
                dve.wait_ge(sem("ln_dev"), k + 1)
                dve.tensor_scalar(mean[:, 0:rows], mean[:, 0:rows], 0.5, None, ALU.mult)
                dve.tensor_tensor(dev[:, 0:rows], dev[:, 0:rows], dev[:, 0:rows], ALU.mult).then_inc(sem("ln_dev_sq"), 1)
                dve.wait_ge(sem("ln_dev_sq"), k + 1)
                dve.scalar_tensor_tensor(out=sumsq[:, 0:rows], in0=dev[:, 0:rows], scalar=D / 4.0, in1=sumsq[:, 0:rows],
                                         op0=ALU.mult, op1=ALU.add).then_inc(sem("ln_sumsq"), 1)
                dve.wait_ge(sem("ln_sumsq"), k + 1)
                dve.tensor_scalar(var[:, 0:rows], sumsq[:, 0:rows], 1.0 / D, EPS, ALU.mult, ALU.add).then_inc(sem("ln_var"), 1)

            def l2_evac(*units):
                for unit in units:
                    dve.wait_ge(sem("l2_mm"), unit + 1)
                    dve.tensor_copy(l2_dest(unit), l2_bank(unit)).then_inc(sem("l2_odd"), 1)

            dve.wait_ge(sem("pad_zero"), B)
            for b in range(B):
                dve.wait_ge(sem(f"x_loaded{b}"), 2 * 16)
                link(dve.tensor_reduce(s17[:, :], xc[b][:, :, :], AX, ALU.add))
                link(dve.tensor_scalar(r17[:, :], s17[:, :], -1.0 / D, None, ALU.mult))
                dve.tensor_tensor(xc[b][:, :, :], xc[b][:, :, :], r17[:, :].unsqueeze(2).to_broadcast([NC, C + 1, D]),
                                  ALU.add).then_inc(sem("centred"), 1)
                dve.wait_ge(sem("sq"), 2 * b + 1)
                link(dve.tensor_reduce(s17[:, :], sq[:, :, :], AX, ALU.add))
                dve.tensor_scalar(s17[:, :], s17[:, :], 1.0 / D, EPS, ALU.mult, ALU.add).then_inc(sem("chunk_var"), 1)
                dve.wait_ge(sem("chunk_std"), b + 1)
                link(dve.reciprocal(r17[:, :], s17[:, :]))
                dve.tensor_tensor(xc[b][:, :, :], xc[b][:, :, :], r17[:, :].unsqueeze(2).to_broadcast([NC, C + 1, D]),
                                  ALU.mult).then_inc(sem("normed"), 1)
                dve.wait_ge(sem("sq"), 2 * b + 2)
                link(dve.tensor_reduce(s136[:, :, :], sq[:, :, :].rearrange("p i (h d) -> p i h d", h=H), AX, ALU.add))
                dve.tensor_scalar(s136[:, :, :], s136[:, :, :], 1e-24, None, ALU.max).then_inc(sem("head_sq"), 1)
                dve.wait_ge(sem("head_norm"), b + 1)
                link(dve.reciprocal(r136[:, :, :], s136[:, :, :]))
                dve.wait_ge(sem("hx_mm"), 4 * (b + 1))
                keys = xc[b][:, :, :].rearrange("p i (h d) -> p i h d", h=H)
                link(dve.tensor_tensor(keys, keys, over_width(r136[:, :, :], C + 1), ALU.mult))

                def diagonal_sums(delta):
                    rows = C + 1 - delta
                    if delta > 1:
                        dve.wait_ge(sem("diag"), C * b + delta - 1)
                    link(dve.tensor_tensor(sq[:, 0:rows, :], xc[b][:, delta:C + 1, :], xc[b][:, 0:rows, :], ALU.mult))
                    if C * b + delta > 2:
                        dve.wait_ge(sem("diag_used"), C * b + delta - 2)
                    dve.tensor_reduce(diag[:, delta % 2, 0:rows, :], sq[:, 0:rows, :].rearrange("p i (h d) -> p i h d", h=H),
                                      AX, ALU.add).then_inc(sem("diag"), 1)

                for delta in (1, 2):
                    diagonal_sums(delta)
                dve.wait_ge(sem("beta"), b + 1)
                link(dve.tensor_tensor(bgam[:, :, :], beta[:, :, :], power[:, 1:C + 1, :], ALU.mult))
                turned = [s[:, :, :].rearrange("p d (h i) -> p i h d", h=H) for s in (ca, cb)]
                for q in range(4):
                    dve.wait_ge(sem("v_mm"), 4 * b + q + 1)
                    dve.tensor_tensor(turned[1][:, 4 * q:4 * q + 4, :, :], bank[q][:, :].rearrange("p (i h d) -> p i h d", i=4, h=H),
                                      over_width(beta[:, 4 * q:4 * q + 4, :], 4), ALU.mult).then_inc(sem("v_src"), 1)
                dve.wait_ge(sem("beta_mm"), b + 1)
                dve.tensor_tensor(turned[0], keys[:, 0:C, :, :], over_width(bgam[:, :, :], C), ALU.mult).then_inc(sem("kb_src"), 1)
                first = UNITS * b
                dve.wait_ge(sem("l2_mm"), first + 4)
                dve.tensor_tensor(turned[1], keys[:, 0:C, :, :], over_width(power[:, C + 1:2 * C + 1, :], C), ALU.mult).then_inc(sem("kd_src"), 1)
                dve.wait_ge(sem("l2_mm"), first + 8)
                dve.tensor_tensor(ca[:, :, :].rearrange("p i (h d) -> p i h d", h=H), keys[:, 1:C + 1, :, :],
                                  over_width(power[:, 1:C + 1, :], C), ALU.mult).then_inc(sem("r_src"), 1)
                for delta in range(3, C + 1):
                    diagonal_sums(delta)
                dve.wait_ge(sem("diag"), C * (b + 1))
                dve.wait_ge(sem("tri_diag"), (C - 1) * (b + 1))
                dve.wait_ge(sem("tri_one"), b + 1)
                steps_done = (C - 2) * b
                for k in range(1, C - 1):
                    shape = [NC, C - 1 - k, H, k]
                    a_col = tri[:, k + 1:C, :, k:k + 1].to_broadcast(shape)
                    t_row = tri[:, k:k + 1, :, 0:k].to_broadcast(shape)
                    size = (C - 1 - k) * H * k
                    terms = sq[:, :, :].rearrange("p i d -> p (i d)")[:, 0:size].rearrange("p (i h j) -> p i h j", h=H, j=k)
                    if k > 1:
                        dve.wait_ge(sem("row_added"), steps_done + k - 1)
                    link(dve.tensor_tensor(terms, a_col, t_row, ALU.mult))
                    last = dve.tensor_tensor(tri[:, k + 1:C, :, 0:k], tri[:, k + 1:C, :, 0:k], terms, ALU.add)
                    last.then_inc(sem("row_added"), 1)
                if b:
                    dve.wait_ge(sem("xres_loaded"), 16)
                    for tile in range(TILES):
                        ins = dve.bn_stats(stat[:, tile, :], xres[:, tile, :])
                    ins.then_inc(sem("ln_stat"), 1)
                    variance(TILES, 0)
                l2_evac(first + VECTOR_FROM + 1, first + VECTOR_FROM + 3)
            dve.wait_ge(sem("ln_rstd"), 1)
            dve.scalar_tensor_tensor(out=mean[:, :], in0=mean[:, :], scalar=-1.0, in1=rstd[:, :],
                                     op0=ALU.mult, op1=ALU.mult)
            dve.tensor_scalar(var[:, :], rstd[:, :], 1.0, None, ALU.add).then_inc(sem("res_scale"), 1)
            dve.wait_ge(sem("res_scale"), 1)
            for tile in range(TILES):
                dve.tensor_scalar(xres[:, tile, :], xres[:, tile, :], var[:, tile:tile + 1], mean[:, tile:tile + 1],
                                  ALU.mult, ALU.add).then_inc(sem("res_ready"), 1)

            dve.wait_ge(sem("l2_even"), B * UNITS // 2)
            dve.wait_ge(sem("l2_odd"), B * UNITS // 2)
            for b in range(B):
                dve.memset(state[b][:, 0, :, :], 0.0).then_inc(sem(f"state{b}"), 1)
            dve.wait_ge(sem("early_qm"), 2 * NT)

            def angle_step(count):
                quarter, at = count // 8, count % 8
                part = quarter_positions(quarter)
                a, turns = ang[:, part], turn[:, part]
                if count == 0:
                    dve.wait_ge(sem("positions"), 1)
                if at == 0:
                    link(dve.tensor_copy(a, position[:, part]))
                elif at == 1:
                    link(dve.tensor_scalar(a, a, freq_col[:, :], None, ALU.mult))
                elif at == 2:
                    link(dve.tensor_scalar(turns, a, 1 / TWO_PI, MAGIC, ALU.mult, ALU.add))
                elif at == 3:
                    link(dve.tensor_scalar(turns, turns, MAGIC, None, ALU.subtract))
                elif at < 7:
                    link(dve.scalar_tensor_tensor(out=a, in0=turns, scalar=-(PI_A, PI_B, PI_C)[at - 4], in1=a,
                                                  op0=ALU.mult, op1=ALU.add))
                else:
                    dve.tensor_scalar(sin_t[:, part], a, PI_LOW, -PI_LOW, ALU.min, ALU.max).then_inc(sem("angles"), 1)

            def slot(t, b):
                (t1, b1), (tb, bb) = unit_after(t, b, 1), unit_after(t, b, -1)
                for n in range(CPT):
                    if isinstance(t, int) and (t, b) in ((NT - 2, 1), (NT - 1, 0)):
                        angle_step((t - NT + 2) * CPT + n)
                    if exists(t):
                        dve.wait_ge(sem(f"state_mm{b}"), t * CPT + n + 2)
                        dve.tensor_tensor(wide[b][:, :, :], bank[4 + n % 2][:, n // 2 * 32 + DH:n // 2 * 32 + 2 * DH].unsqueeze(1).to_broadcast([P, 2, DH]),
                                          pair_mask[:, :, :], ALU.mult).then_inc(sem(f"wide{b}"), 1)
                        dve.wait_ge(sem(f"wide{b}"), t * CPT + n + 1)
                        dve.transpose(state[b][:, (n + 1) % CPT, :, :].rearrange("p k d -> p (k d)"),
                                      wide[b][:, :, :].rearrange("p k d -> p (k d)")).then_inc(sem(f"state{b}"), 1)
                    if n == 3 and exists(tb):
                        if isinstance(tb, int) and tb == 0:
                            dve.wait_ge(sem("res_ready"), TILES)
                        dve.wait_ge(sem(f"y_mm{bb}"), tb + 2)
                        here = xres[:, bass.ds(tb + bb * NT, 1), :].rearrange("p a d -> p (a d)")
                        dve.tensor_tensor(here, here, bank[6 + bb][:, 0:P], ALU.add).then_inc(sem(f"x1_{bb}"), 1)
                    if n == 5 and exists(t1):
                        if b1:
                            dve.wait_ge(sem("qm_mm1"), t1 + 2)
                            qm = bank[3][:, 0:CPT * 2 * DH].rearrange("p (n k d) -> p n k d", n=CPT, k=2)
                            q_part, m_part = qm[:, :, 0, :], qm[:, :, 1, :]
                        else:
                            dve.wait_ge(sem("vk_tile0"), 16 * (t1 + 1))
                            q_part, m_part = tt[:, 0, bass.ds(t1 * CPT, CPT), :], vk_tile[0][:, :, 1, :]
                        dve.wait_ge(sem(f"state_mm{b1}"), t1 * CPT + 1)
                        dve.tensor_tensor(step[b1][:, :, 0, :], rq[:, b1, bass.ds(t1 * CPT, CPT), :], q_part, ALU.subtract)
                        dve.tensor_tensor(step[b1][:, :, 1, :], gamma_rep[:, :].unsqueeze(1).to_broadcast([P, CPT, DH]), m_part,
                                          ALU.subtract).then_inc(sem(f"step{b1}"), 1)

            run_slots(dve, slot)
            for b in range(B):
                dve.wait_ge(sem(f"x1_{b}"), NT + 1)

            def layernorm_statistics(k, first_tile):
                if not isinstance(k, int) or k > 1:
                    dve.wait_ge(sem("ln_rows"), k - 1)
                dve.memset(wait_holder[:, :], 0.0)
                for q in range(GT):
                    ins = dve.bn_stats(stat[:, q, :], xres[:, bass.ds(first_tile + q, 1), :].rearrange("p a d -> p (a d)"))
                ins.then_inc(sem("ln_stat"), 1)
                variance(GT, k)

            def layernorm_rows(k, first_tile, rows):
                dve.wait_ge(sem("ln_rstd"), k + 1)
                for q in range(GT):
                    ins = dve.tensor_scalar(rows[:, q, :], xres[:, bass.ds(first_tile + q, 1), :].rearrange("p a d -> p (a d)"),
                                            mean[:, q:q + 1], rstd[:, q:q + 1], ALU.subtract, ALU.mult)
                ins.then_inc(sem("ln_rows"), 1)

            def best_two(g):
                dve.wait_ge(sem("gate_mm"), g + 1)
                dve.tensor_copy(gates[:, :, :].rearrange("p q e -> p (q e)"), bank[1][:, 0:GT * E]).then_inc(sem("gates"), 1)
                dve.wait_ge(sem("gates"), g + 1)
                dve.memset(wait_holder[:, :], 0.0)
                for q in range(GT):
                    ins = dve.max(top[:, q, :], gates[:, q, :])
                ins.then_inc(sem("top"), 1)
                dve.wait_ge(sem("top"), g + 1)
                dve.tensor_tensor(gap[:, :], top[:, :, 1], top[:, :, 0], ALU.subtract).then_inc(sem("gap"), 1)
                for q in range(GT):
                    ins = dve.max_index(topi[:, q, :], top[:, q, :], gates[:, q, :])
                ins.then_inc(sem("topi"), 1)
                dve.wait_ge(sem("topi"), g + 1)
                dve.tensor_copy(topf[:, :, :], topi[:, :, :]).then_inc(sem("topf"), 1)

            def expert_weights(g, i):
                dve.wait_ge(sem("topf"), g + 1)
                shape = [P, GT, E]
                for k in range(TOPK):
                    ins = dve.tensor_tensor(hot[:, k, :, :], iota8[:, :].unsqueeze(1).to_broadcast(shape),
                                            topf[:, :, k:k + 1].to_broadcast(shape), ALU.is_equal)
                ins.then_inc(sem("hot"), 1)
                dve.wait_ge(sem("odds"), g + 1)
                dve.tensor_scalar(wsel[:, 1, :], odds[:, :], 1.0, None, ALU.add).then_inc(sem("weight_steps"), 1)
                dve.wait_ge(sem("weight_steps"), 3 * g + 1)
                dve.reciprocal(wsel[:, 0, :], wsel[:, 1, :]).then_inc(sem("weight_steps"), 1)
                dve.wait_ge(sem("weight_steps"), 3 * g + 2)
                dve.tensor_tensor(wsel[:, 1, :], wsel[:, 0, :], odds[:, :], ALU.mult).then_inc(sem("weight_steps"), 1)
                dve.wait_ge(sem("weight_steps"), 3 * g + 3)
                dve.wait_ge(sem("hot"), g + 1)
                for k in range(TOPK):
                    ins = dve.tensor_tensor(hot[:, k, :, :], hot[:, k, :, :], wsel[:, k, :].unsqueeze(2).to_broadcast(shape), ALU.mult)
                ins.then_inc(sem("hot_w"), 1)
                dve.wait_ge(sem("hot_w"), g + 1)
                dve.tensor_tensor(wrow[i][:, :, :], hot[:, 0, :, :], hot[:, 1, :, :], ALU.add).then_inc(sem("wrow"), 1)

            def columns_low(k, i):
                dve.wait_ge(sem("ht"), k)
                dve.tensor_tensor(ht_lo[i][:, :], ht[i][:, :], ht_hi[i][:, :].bitcast(F32), ALU.subtract).then_inc(sem("ht_lo"), 1)

            def first():
                layernorm_statistics(1, 0)
                layernorm_rows(1, 0, hrow)
                columns_low(1, 0)
                best_two(0)
                expert_weights(0, 0)

            def add_expert(g, i, e):
                dve.wait_ge(sem("down"), g * E + e + 2)
                if e == 0:
                    dve.wait_ge(sem("bias_added"), g + 2)
                else:
                    dve.wait_ge(sem("added"), g * E + e + 1)
                for q in range(GT):
                    here = xres[:, bass.ds(tile_of(g) + q, 1), :].rearrange("p a d -> p (a d)")
                    ins = dve.scalar_tensor_tensor(out=here, in0=bank[6 + e % 2][:, q * D:(q + 1) * D], scalar=wrow[i][:, q, e:e + 1],
                                                   in1=here, op0=ALU.mult, op1=ALU.add)
                ins.then_inc(sem("added"), 1)

            def finish(g, i, rotor):
                add_expert(g, i, E - 1)
                if rotor:
                    dve.wait_ge(sem("bt_y_mm"), g + 1)
                    here = xres[:, bass.ds(tile_of(g - 1), GT), :].rearrange("p q d -> p (q d)")
                    dve.tensor_tensor(here, here, bank[0][:, :], ALU.add).then_inc(sem("x3"), 1)

            def group(g, i, rotor, last):
                tile = tile_of(g)
                next_tile = tile_of(g + 1)
                rotor_tile = tile_of(g - 1)

                def hidden(n):
                    e, c, k = n // FC, n % FC, n % 2
                    dve.wait_ge(sem("v"), g * UP + n + 2)
                    dve.tensor_scalar(vact[k][:, :], vact[k][:, :], 1 + LIMIT, 1 - LIMIT, ALU.min, ALU.max).then_inc(sem("clip"), 1)
                    if c == 0:
                        dve.wait_ge(sem("down"), positive(g * E + e))
                    dve.wait_ge(sem("clip"), g * UP + n + 1)
                    dve.wait_ge(sem("s"), g * UP + n + 2)
                    dve.scalar_tensor_tensor(out=hmid[e % 2][c][:, :], in0=gs[k][:, :], scalar=GATE_LIMIT, in1=vact[k][:, :],
                                             op0=ALU.min, op1=ALU.mult).then_inc(sem("h"), 1)

                def rotate():
                    dve.wait_ge(sem("trig"), 2 if isinstance(g, int) and g == 1 else 6)
                    dve.wait_ge(sem("bt_v_mm"), g)
                    dve.wait_ge(sem("carried"), g)
                    for k, table in enumerate((cos_t, sin_t)):
                        dve.tensor_tensor(vc[:, k, :], bank[1][:, :], table[:, bass.ds((g - 1) % (GROUPS // B) * GW, GW)], ALU.mult).then_inc(sem("rotated"), 1)

                def running_sums():
                    dve.wait_ge(sem("rotated"), 2 * g + 1)
                    dve.wait_ge(sem("carried"), g)
                    dve.wait_ge(sem("retr"), g)
                    for k in range(2):
                        dve.tensor_tensor_scan(trace[:, k, :], ones_row[:, :], vc[:, k, :], carry[:, k:k + 1],
                                               ALU.mult, ALU.add).then_inc(sem(f"trace{k}"), 1)
                    for k in range(2):
                        dve.wait_ge(sem(f"trace{k}"), g)
                    dve.tensor_tensor(carry[:, :], trace[:, :, GW - 1], keep[:, bass.ds(g - 1, 1)].to_broadcast([D, 2]),
                                      ALU.mult).then_inc(sem("carried"), 1)

                for n in range(UP):
                    hidden(n)
                    if n == 0 and not (isinstance(g, int) and g == 0):
                        finish(g - 1, 1 - i, 2 <= g <= GROUPS + 1 if isinstance(g, int) else rotor)
                    if n == 2:
                        dve.wait_ge(sem("bias_mm"), g + 1)
                        here = xres[:, bass.ds(tile, GT), :].rearrange("p q d -> p (q d)")
                        dve.tensor_tensor(here, here, bank[0][:, :], ALU.add).then_inc(sem("bias_added"), 1)
                    if n == 15 and not last:
                        expert_weights(g + 1, 1 - i)
                    if n > FC and n % FC == 1:
                        add_expert(g, i, n // FC - 1)
                    if rotor:
                        if n == 1:
                            dve.wait_ge(sem("added"), g * E + 1)
                            layernorm_statistics(rotor_k(g), rotor_tile)
                        if n == 2:
                            layernorm_rows(rotor_k(g), rotor_tile, hrow_r)
                        if n == 7:
                            rotate()
                        if n == 8:
                            running_sums()
                    if not last:
                        if n == 4:
                            if rotor:
                                dve.wait_ge(sem("x3"), g)
                            elif not isinstance(g, int) or g > GROUPS:
                                dve.wait_ge(sem("x3"), GROUPS + 1)
                            layernorm_statistics(next_k(g, rotor), next_tile)
                        if n == 6:
                            layernorm_rows(next_k(g, rotor), next_tile, hrow)
                        if n == 12:
                            columns_low(next_k(g, rotor), 1 - i)
                        if n == 13:
                            best_two(g + 1)

            dve.wait_ge(sem("small_loaded"), 4 * 16)
            link(dve.tensor_scalar(b1v_col[:, :, :], b1_col[:, :, :, 1], 1.0, None, ALU.add))
            dve.memset(half_pi[:, :], math.pi / 2).then_inc(sem("half_pi"), 1)
            dve.memset(ones_row[:, :], 1.0).then_inc(sem("bt_constants"), 1)
            dve.memset(carry[:, :], 0.0).then_inc(sem("bt_constants"), 1)
            dve.memset(keep[:, :], 1.0).then_inc(sem("bt_constants"), 1)
            dve.wait_ge(sem("bt_constants"), 3)
            for b in range(B):
                last_group = (b + 1) * GROUPS // B - 1
                dve.memset(keep[:, last_group:last_group + 1], 0.0).then_inc(sem("bt_constants"), 1)
            dve.wait_ge(sem("bt_constants"), 5)
            dve.wait_ge(sem("half"), 1)
            all_groups(dve, first, group)
            finish(ALL - 1, 1, False)


_INS = ["L0_attn_a_out", "L0_attn_a_W_write", "L0_attn_a_W_read", "L0_attn_a_W_beta", "L0_attn_a_decay",
        "L0_attn_b_Wk", "L0_attn_b_Wv", "L0_attn_b_Wo", "L0_attn_b_freqs", "L0_ffn_gate_w",
        "L0_ffn_dense_1_w", "L0_ffn_dense_1_b", "L0_ffn_dense_2_w", "L0_ffn_dense_2_b"]


def kernel(**inputs):
    import numpy as _np
    import concourse.bacc as _bacc
    from concourse import mybir as _mybir
    from concourse.bass_utils import run_bass_kernel_spmd as _run

    nc = _bacc.Bacc("TRN2", target_bir_lowering=False, num_devices=1)
    arrays, args = {}, []
    for name in _INS:
        a = _np.ascontiguousarray(inputs[name])
        arrays[f"in_{name}_dram"] = a
        args.append(nc.dram_tensor(f"in_{name}_dram", a.shape, _mybir.dt.from_np(a.dtype), kind="ExternalInput").ap())
    args.append(nc.dram_tensor("out_0_dram", (B, T, D), F32, kind="ExternalOutput").ap())
    build(nc, *args)
    r = _run(nc, [arrays], core_ids=[0])
    return r.results[0]["out_0_dram"]
```
